# Optimizing a Trainium2 kernel written in Bass

```python
import numpy as np
import jax
import jax.numpy as jnp

def _softmax(x, axis=-1):
    return jax.nn.softmax(x, axis=axis)

def _gelu(x):
    return jax.nn.gelu(x, approximate=True)

def _silu(x):
    return jax.nn.silu(x)

def _sigmoid(x):
    return jax.nn.sigmoid(x)

def _layernorm(x, axis=-1, eps=1e-05):
    m = jnp.mean(x, axis=axis, keepdims=True)
    v = jnp.var(x, axis=axis, keepdims=True)
    return (x - m) / jnp.sqrt(v + eps)

def _scatter_add(tgt, idx, src, axis=0):
    return tgt.at[idx].add(src)

def _segment_sum(src, seg, n):
    return jax.ops.segment_sum(src, seg, n)
kernel_name = 'mk_early_fusion_d1_tok_img512_r4_4ed8e5'

def setup_inputs(seed: int=0):
    np.random.seed(seed)
    _w = jnp.asarray

    def _rec_inputs():
        import jax
        import jax.numpy as jnp
        _rk = jax.random.key(seed)
        x = 7.57192e-06 + 1.00007 * jax.random.normal(jax.random.fold_in(_rk, 1), (32, 112, 112, 3), jnp.float32)
        txt = -0.000319884 + 0.450765 * jax.random.normal(jax.random.fold_in(_rk, 2), (32, 32, 128), jnp.float32)
        return (x, txt)
    x, txt = _rec_inputs()

    def _L0_tok_setup():
        import jax, jax.numpy as jnp
        import numpy as np
        B, H, W, C = (64, 224, 224, 3)
        P, D = (16, 128)
        LN_EPS = 0.001

        def _shift4(x):
            pad = lambda a, spec: jnp.pad(a, spec)
            right = pad(x[:, :, :-1, :], ((0, 0), (0, 0), (1, 0), (0, 0)))
            left = pad(x[:, :, 1:, :], ((0, 0), (0, 0), (0, 1), (0, 0)))
            down = pad(x[:, :-1, :, :], ((0, 0), (1, 0), (0, 0), (0, 0)))
            up = pad(x[:, 1:, :, :], ((0, 0), (0, 1), (0, 0), (0, 0)))
            return [right, left, down, up]
        key = jax.random.key(seed)
        k0, k1, k2 = jax.random.split(key, 3)
        x = jax.random.normal(k0, (B, H, W, C), jnp.float32)
        conv_w = jax.random.normal(k1, (P, P, 5 * C, D), jnp.float32) * 0.02
        conv_b = jnp.zeros((D,), jnp.float32)
        gamma = jnp.ones((D,), jnp.float32)
        beta = jnp.zeros((D,), jnp.float32)
        dense_w = jax.random.normal(k2, (D, D), jnp.float32) * 0.02
        dense_b = jnp.zeros((D,), jnp.float32)
        return {'x': x, 'conv_w': conv_w, 'conv_b': conv_b, 'gamma': gamma, 'beta': beta, 'dense_w': dense_w, 'dense_b': dense_b}
    _L0_tok_all = _L0_tok_setup()
    _L0_tok_in = {k: v for k, v in _L0_tok_all.items() if k in ('conv_w', 'conv_b', 'gamma', 'beta', 'dense_w', 'dense_b')}
    del _L0_tok_all

    def _L0_attn_setup():
        import jax, jax.numpy as jnp
        import numpy as np
        B, N, E, H, NDIM, WS = (1, 1024, 128, 8, 16, 128)
        key = jax.random.key(seed)
        ks = jax.random.split(key, 8)
        x = jax.random.normal(ks[0], (B, N, E), jnp.float32)
        W_qkv = jax.random.normal(ks[1], (E, 3 * E), jnp.float32) * E ** (-0.5)
        b_qkv = jnp.zeros((3 * E,), jnp.float32)
        W_out = jax.random.normal(ks[2], (E, E), jnp.float32) * E ** (-0.5)
        b_out = jnp.zeros((E,), jnp.float32)
        omega = jax.random.normal(ks[3], (E,), jnp.float32)
        p_coeff = 0.1 * jax.random.normal(ks[4], (E, NDIM), jnp.float32)
        q_coeff = jax.random.uniform(ks[5], (E, NDIM), jnp.float32, minval=-0.95, maxval=0.95)
        gamma = 0.1 * jax.random.normal(ks[6], (E, NDIM), jnp.float32)
        adaptive_weights = jnp.ones((2,), jnp.float32)
        return dict(x=x, W_qkv=W_qkv, b_qkv=b_qkv, W_out=W_out, b_out=b_out, omega=omega, p_coeff=p_coeff, q_coeff=q_coeff, gamma=gamma, adaptive_weights=adaptive_weights)
    _L0_attn_all = _L0_attn_setup()
    _L0_attn_in = {k: v for k, v in _L0_attn_all.items() if k in ('W_qkv', 'b_qkv', 'W_out', 'b_out', 'omega', 'p_coeff', 'q_coeff', 'gamma', 'adaptive_weights')}
    del _L0_attn_all

    def _L0_ffn_setup():
        import jax, jax.numpy as jnp
        import numpy as np
        D_MODEL, N_GROUPS, N_EXPERTS = (128, 8, 8)
        TOP_K_L1, TOP_K_L2 = (2, 2)
        BATCH, SEQ = (2, 128)
        key = jax.random.key(seed)
        ks = jax.random.split(key, 6)
        d, G, E = (D_MODEL, N_GROUPS, N_EXPERTS)
        scale = 0.02
        x = jax.random.normal(ks[0], (BATCH, SEQ, d), dtype=jnp.float32)
        g1 = jax.random.normal(ks[1], (d, G), dtype=jnp.float32) * scale
        g2 = jax.random.normal(ks[2], (G, d, E), dtype=jnp.float32) * scale
        W1 = jax.random.normal(ks[3], (G, E, d, 2 * d), dtype=jnp.float32) * scale
        b1 = jnp.zeros((G, E, 2 * d), dtype=jnp.float32)
        W2 = jax.random.normal(ks[4], (G, E, 2 * d, d), dtype=jnp.float32) * scale
        b2 = jnp.zeros((G, E, d), dtype=jnp.float32)
        return {'x': x, 'g1': g1, 'g2': g2, 'W1': W1, 'b1': b1, 'W2': W2, 'b2': b2}
    _L0_ffn_all = _L0_ffn_setup()
    _L0_ffn_in = {k: v for k, v in _L0_ffn_all.items() if k in ('g1', 'g2', 'W1', 'b1', 'W2', 'b2')}
    del _L0_ffn_all
    return {'x': x, 'txt': txt, 'L0_tok_conv_w': _L0_tok_in['conv_w'], 'L0_tok_conv_b': _L0_tok_in['conv_b'], 'L0_tok_gamma': _L0_tok_in['gamma'], 'L0_tok_beta': _L0_tok_in['beta'], 'L0_tok_dense_w': _L0_tok_in['dense_w'], 'L0_tok_dense_b': _L0_tok_in['dense_b'], 'L0_attn_W_qkv': _L0_attn_in['W_qkv'], 'L0_attn_b_qkv': _L0_attn_in['b_qkv'], 'L0_attn_W_out': _L0_attn_in['W_out'], 'L0_attn_b_out': _L0_attn_in['b_out'], 'L0_attn_omega': _L0_attn_in['omega'], 'L0_attn_p_coeff': _L0_attn_in['p_coeff'], 'L0_attn_q_coeff': _L0_attn_in['q_coeff'], 'L0_attn_gamma': _L0_attn_in['gamma'], 'L0_attn_adaptive_weights': _L0_attn_in['adaptive_weights'], 'L0_ffn_g1': _L0_ffn_in['g1'], 'L0_ffn_g2': _L0_ffn_in['g2'], 'L0_ffn_W1': _L0_ffn_in['W1'], 'L0_ffn_b1': _L0_ffn_in['b1'], 'L0_ffn_W2': _L0_ffn_in['W2'], 'L0_ffn_b2': _L0_ffn_in['b2']}

def reference(x, txt, L0_tok_conv_w, L0_tok_conv_b, L0_tok_gamma, L0_tok_beta, L0_tok_dense_w, L0_tok_dense_b, L0_attn_W_qkv, L0_attn_b_qkv, L0_attn_W_out, L0_attn_b_out, L0_attn_omega, L0_attn_p_coeff, L0_attn_q_coeff, L0_attn_gamma, L0_attn_adaptive_weights, L0_ffn_g1, L0_ffn_g2, L0_ffn_W1, L0_ffn_b1, L0_ffn_W2, L0_ffn_b2):
    import jax
    import jax.numpy as jnp

    def _L0_tok_ref(x, conv_w, conv_b, gamma, beta, dense_w, dense_b):
        import jax, jax.numpy as jnp
        import numpy as np
        B, H, W, C = (64, 224, 224, 3)
        P, D = (16, 128)
        LN_EPS = 0.001

        def _shift4(x):
            pad = lambda a, spec: jnp.pad(a, spec)
            right = pad(x[:, :, :-1, :], ((0, 0), (0, 0), (1, 0), (0, 0)))
            left = pad(x[:, :, 1:, :], ((0, 0), (0, 0), (0, 1), (0, 0)))
            down = pad(x[:, :-1, :, :], ((0, 0), (1, 0), (0, 0), (0, 0)))
            up = pad(x[:, 1:, :, :], ((0, 0), (0, 1), (0, 0), (0, 0)))
            return [right, left, down, up]
        xs = jnp.concatenate([x, *_shift4(x)], axis=-1)
        y = jax.lax.conv_general_dilated(xs, conv_w, window_strides=(P, P), padding='VALID', dimension_numbers=('NHWC', 'HWIO', 'NHWC')) + conv_b
        y = y.reshape(y.shape[0], -1, D)
        mu = jnp.mean(y, axis=-1, keepdims=True)
        var = jnp.mean(jnp.square(y - mu), axis=-1, keepdims=True)
        y = (y - mu) * jax.lax.rsqrt(var + LN_EPS) * gamma + beta
        return y @ dense_w + dense_b

    def _L0_attn_ref(x, W_qkv, b_qkv, W_out, b_out, omega, p_coeff, q_coeff, gamma, adaptive_weights):
        import jax, jax.numpy as jnp
        import numpy as np
        B, N, E, H, NDIM, WS = (1, 1024, 128, 8, 16, 128)
        b, n, e = x.shape
        dk = e // H
        qkv = x @ W_qkv + b_qkv
        q, k, v = jnp.split(qkv, 3, axis=-1)
        to_heads = lambda t: t.reshape(b, n, H, dk).transpose(0, 2, 1, 3)
        q, k, v = (to_heads(q), to_heads(k), to_heads(v))
        dots = jnp.einsum('bhid,bhjd->bhij', q, k) * dk ** (-0.5)
        idx = jnp.arange(n)
        blk, pos = (idx // WS, idx % WS)
        mask = (blk[:, None] == blk[None, :]) & (pos[None, :] <= pos[:, None])
        dots = dots * mask.astype(dots.dtype)
        attn = jax.nn.softmax(dots, axis=-1)
        out_attn = jnp.einsum('bhij,bhjd->bhid', attn, v)
        out_attn = out_attn.transpose(0, 2, 1, 3).reshape(b, n, e) @ W_out + b_out
        ndim = p_coeff.shape[1]

        def step(h, xt):
            h = p_coeff[None] * xt[:, :, None] + q_coeff[None] * h
            return (h, jnp.sum(gamma[None] * h, axis=-1))
        h0 = jnp.zeros((b, e, ndim), x.dtype)
        _, ys = jax.lax.scan(step, h0, jnp.swapaxes(x, 0, 1))
        x_cema = jnp.swapaxes(ys, 0, 1)
        w = jax.nn.softmax(adaptive_weights)
        return w[0] * out_attn + w[1] * x_cema

    def _L0_ffn_ref(x, g1, g2, W1, b1, W2, b2):
        import jax, jax.numpy as jnp
        import numpy as np
        D_MODEL, N_GROUPS, N_EXPERTS = (128, 8, 8)
        TOP_K_L1, TOP_K_L2 = (2, 2)
        BATCH, SEQ = (2, 128)
        B, S, d = x.shape
        G, E = (g1.shape[1], g2.shape[2])
        xt = x.reshape(-1, d)
        logits1 = xt @ g1
        v1, i1 = jax.lax.top_k(logits1, TOP_K_L1)
        w1 = jax.nn.softmax(v1.astype(jnp.float32), axis=-1).astype(x.dtype)
        c1 = jnp.sum(jax.nn.one_hot(i1, G, dtype=x.dtype) * w1[..., None], axis=1)
        logits2 = jnp.einsum('td,gde->tge', xt, g2)
        v2, i2 = jax.lax.top_k(logits2, TOP_K_L2)
        w2 = jax.nn.softmax(v2.astype(jnp.float32), axis=-1).astype(x.dtype)
        c2 = jnp.sum(jax.nn.one_hot(i2, E, dtype=x.dtype) * w2[..., None], axis=2)
        h = jax.nn.relu(jnp.einsum('td,gedh->tgeh', xt, W1) + b1)
        y = jnp.einsum('tgeh,gehd->tged', h, W2) + b2
        group_out = jnp.einsum('tged,tge->tgd', y, c2)
        out = jnp.einsum('tgd,tg->td', group_out, c1)
        return out.reshape(B, S, d)
    h = _L0_tok_ref(x, L0_tok_conv_w, L0_tok_conv_b, L0_tok_gamma, L0_tok_beta, L0_tok_dense_w, L0_tok_dense_b)
    h = jnp.concatenate([h, txt], axis=1)
    h = h + _L0_attn_ref(_layernorm(h, axis=-1), L0_attn_W_qkv, L0_attn_b_qkv, L0_attn_W_out, L0_attn_b_out, L0_attn_omega, L0_attn_p_coeff, L0_attn_q_coeff, L0_attn_gamma, L0_attn_adaptive_weights)
    h = h + _L0_ffn_ref(_layernorm(h, axis=-1), L0_ffn_g1, L0_ffn_g2, L0_ffn_W1, L0_ffn_b1, L0_ffn_W2, L0_ffn_b2)
    return h

_drawn_inputs = setup_inputs


def setup_inputs(seed=0):
    import zlib

    import numpy as np

    out = dict(_drawn_inputs(seed))
    spreads = {'L0_tok_conv_b': (0.0, 0.1),
     'L0_tok_gamma': (1.0, 0.2),
     'L0_tok_beta': (0.0, 0.1),
     'L0_tok_dense_b': (0.0, 0.1),
     'L0_attn_b_qkv': (0.0, 0.1),
     'L0_attn_b_out': (0.0, 0.1),
     'L0_attn_adaptive_weights': (1.0, 0.6),
     'L0_ffn_b1': (0.0, 0.283),
     'L0_ffn_b2': (0.0, 0.1)}
    factors = {}
    for name, (base, spread) in spreads.items():
        noise = np.random.default_rng([zlib.crc32(name.encode()), seed]).standard_normal(out[name].shape)
        drawn = base * np.exp(spread * noise) if base else spread * noise
        out[name] = jnp.asarray(drawn.astype(out[name].dtype))
    for name, factor in factors.items():
        out[name] = (out[name] * factor).astype(out[name].dtype)
    return out
```

```python
from contextlib import ExitStack

import concourse.bass as bass
from concourse import mybir

ALU = mybir.AluOpType
ACT = mybir.ActivationFunctionType
AX = mybir.AxisListType
F32 = mybir.dt.float32
I32 = mybir.dt.int32

PART = 128
B, IMG, C = 32, 112, 3
P = 16
G = IMG // P
PATCHES = G * G
TXT = 32
N = PATCHES + TXT
D = 128
ROWLEN = (IMG + 2) * C
TOK_EPS, LN_EPS = 1e-3, 1e-5

W_LOADS = 6 + 16 + 5

TILE_ROWS = [4, 3]
TILE_PARTS = [B * r for r in TILE_ROWS]
KT = [128] * 6 + [96, 96]
KCOLS = sum(KT)
KOFF = [sum(KT[:m]) for m in range(8)]
SIDES = 6 * 128
ENDS = SIDES + 96


def strided(ap, dims):
    return bass.AP(ap.tensor, ap.offset, [ap.ap[0]] + [list(d) for d in dims])


def patch_tokens(nc, x, conv_w, conv_b, gamma, beta, dense_w, dense_b, h_dram):
    with ExitStack() as ctx:
        def sb(name, shape, dt=F32):
            return ctx.enter_context(nc.sbuf_tensor(name, shape, dt))

        def psum(name, shape, dt=F32):
            return ctx.enter_context(nc.psum_tensor(name, shape, dt))

        def sem(name):
            return ctx.enter_context(nc.semaphore(name))

        image = [sb(f"image{k}", [PART, P + 2, ROWLEN]) for k in range(2)]
        patch = [sb(f"patch{k}", [PART, KCOLS]) for k in range(2)]
        patch_T = [sb(f"patch_T{k}", [PART, 8, 128]) for k in range(2)]
        w_src = sb("w_src", [PART, 5, 6, D])
        w_edge = sb("w_edge", [97, 2, D])
        y = sb("y", [PART, 2, G, D])
        stats = sb("stats", [PART, 2, 6])
        moments = sb("moments", [PART, 2, 2])
        rstd = sb("rstd", [PART, 2, G])
        half = sb("half", [PART, 2, G])
        normed = [sb(f"normed{k}", [PART, D]) for k in range(2)]
        normed_T = [sb(f"normed_T{k}", [PART, D]) for k in range(2)]
        token = [sb(f"token{k}", [PART, D]) for k in range(2)]
        dense_sb = sb("dense_sb", [D, D])
        dense_b_row = sb("dense_b_row", [PART, D])
        gamma_col = sb("gamma_col", [D, 1])
        beta_col = sb("beta_col", [D, 1])
        ident = sb("ident_a", [PART, PART])

        ps_T = [psum(f"ps_T{k}", [PART, 8, 128]) for k in range(2)]
        ps_y = [psum(f"ps_y{k}", [PART, 512]) for k in range(2)]
        ps_n = [psum(f"ps_n{k}", [PART, 512]) for k in range(2)]

        borders_zero = sem("borders_zero")
        image_in = [sem(f"image_in{k}") for k in range(2)]
        w_zero = sem("w_zero")
        w_in = sem("w_in")
        w_sum = sem("w_sum")
        small_in = sem("small_in")
        ident_ok = sem("ident_ok")
        patch_ok = sem("patch_ok")
        patch_read = sem("patch_read")
        transposed = sem("transposed")
        left_half = sem("left_half")
        right_half = sem("right_half")
        conv_ok = sem("conv_ok")
        y_ok = sem("y_ok")
        stats_ok = sem("stats_ok")
        moments_ok = sem("moments_ok")
        rstd_ok = sem("rstd_ok")
        rstd_pow = sem("rstd_pow")
        ones_ok = sem("ones_ok")
        sides_ok = sem("sides_ok")
        normed_ok = sem("normed_ok")
        normed_turned = sem("normed_turned")
        normed_T_ok = sem("normed_T_ok")
        dense_ok = sem("dense_ok")
        token_ok = sem("token_ok")
        stored = [sem(f"stored{k}") for k in range(2)]

        block = ctx.enter_context(nc.Block())

        @block.sync
        def _(sp):
            sp.wait_ge(borders_zero, 6)
            for k in range(2):
                for r in range(TILE_ROWS[k]):
                    pr = 4 * k + r
                    lo, hi = max(P * pr - 1, 0), min(P * pr + P + 1, IMG)
                    first = lo - (P * pr - 1)
                    sp.dma_start(image[k][B * r:B * r + B, first:first + hi - lo, C:C + IMG * C],
                                 x[:, lo:hi, :, :].rearrange("b i j c -> b i (j c)")).then_inc(image_in[k], 16)
            def store(pc, k, t):
                sp.wait_ge(token_ok, t + 1)
                rows = h_dram.rearrange("b (r c) d -> c r b d", c=G)
                sp.dma_start(rows[bass.ds(pc, 1), 4 * k:4 * k + TILE_ROWS[k]].rearrange("o r b d -> (o r) b d"),
                             token[k][0:TILE_PARTS[k], :]).then_inc(stored[k], 16)
            with sp.Fori(0, G) as pc:
                for k in range(2):
                    store(pc, k, 2 * pc + k)
            for k in range(2):
                sp.wait_ge(stored[k], 16 * G)

        @block.scalar
        def _(act):
            w5 = conv_w.rearrange("i j (s c) d -> s j i (c d)", s=5)
            act.wait_ge(w_zero, 1)
            for hf in range(2):
                j0, mine = 8 * hf, slice(3 * hf, 3 * hf + 3)
                act.dma_start(w_src[:, 0, mine, :], w5[0, j0:j0 + 8]).then_inc(w_in, 16)
                n, none = 8 - hf, 1 - hf
                act.dma_start(w_src[0:16 * n, 1, mine, :], w5[1, j0 + 1:j0 + 1 + n]).then_inc(w_in, 16)
                act.dma_start(w_src[16 * none:128, 2, mine, :], w5[2, j0 - 1 + none:j0 + 7]).then_inc(w_in, 16)
            for jl in range(8):
                for s, (p0, i0) in ((3, (0, 1)), (4, (1, 0))):
                    act.dma_start(
                        w_src[16 * jl + p0:16 * jl + p0 + 15, s, :, :].rearrange("i (h c) d -> i h (c d)", h=2),
                        conv_w[i0:i0 + 15, jl:16:8, 3 * s:3 * s + 3, :].rearrange("i h c d -> i h (c d)"),
                    ).then_inc(w_in, 16)
            act.dma_start(w_edge[0:48, 0, :], conv_w[:, 0, 3:6, :].rearrange("i c d -> c i d")).then_inc(w_in, 16)
            act.dma_start(w_edge[48:96, 0, :], conv_w[:, 15, 6:9, :].rearrange("i c d -> c i d")).then_inc(w_in, 16)
            act.dma_start(w_edge[0:48, 1, :], conv_w[0, :, 9:12, :].rearrange("j c d -> c j d")).then_inc(w_in, 16)
            act.dma_start(w_edge[48:96, 1, :], conv_w[15, :, 12:15, :].rearrange("j c d -> c j d")).then_inc(w_in, 16)
            act.dma_start(w_edge[96:97, 0, :], conv_b.rearrange("(o d) -> o d", o=1)).then_inc(w_in, 16)
            act.dma_start(dense_b_row[:, :], dense_b.partition_broadcast(PART)).then_inc(small_in, 16)
            act.dma_start(dense_sb[:, :], dense_w).then_inc(small_in, 16)
            act.dma_start(gamma_col[:, :], gamma.rearrange("(d o) -> d o", o=1)).then_inc(small_in, 16)
            act.dma_start(beta_col[:, :], beta.rearrange("(d o) -> d o", o=1)).then_inc(small_in, 16)

            def first_half(k, t, first):
                act.wait_ge(transposed, t + 1)
                if not first:
                    act.wait_ge(conv_ok, t - 1)
                nk = TILE_PARTS[k]
                nc.scalar.copy(patch_T[k][:, 0:4, 0:nk], ps_T[k][:, 0:4, 0:nk]).then_inc(left_half, 1)
            for k in range(2):
                first_half(k, k, True)
            with act.Fori(1, G) as pc:
                for k in range(2):
                    first_half(k, 2 * pc + k, False)

            def scaled(k, t, first):
                act.wait_ge(normed_turned, t + 1)
                if not first:
                    act.wait_ge(dense_ok, t - 1)
                nk = TILE_PARTS[k]
                nc.scalar.activation(normed_T[k][:, 0:nk], ps_n[k][:, 0:nk], ACT.Identity,
                                     bias=beta_col[:, 0:1], scale=gamma_col[:, 0:1]).then_inc(normed_T_ok, 1)
            act.wait_ge(small_in, 64)
            for k in range(2):
                scaled(k, k, True)
            with act.Fori(1, G) as pc:
                for k in range(2):
                    scaled(k, 2 * pc + k, False)

        @block.gpsimd
        def _(pool):
            nc.gpsimd.memset(ident[:, :], 0.0).then_inc(ident_ok, 1)
            nc.gpsimd.memset(half[:, :, :], -0.5).then_inc(ident_ok, 1)
            pool.wait_ge(ident_ok, 2)
            nc.gpsimd.affine_select(out=ident[:, :], in_=ident[:, :], compare_op=ALU.not_equal, fill=1.0,
                                    base=0, pattern=[[-1, PART]], channel_multiplier=1).then_inc(ident_ok, 1)

            def gather(pc, k, t, first):
                if not first:
                    pool.wait_ge(patch_read, t - 1)
                nk = TILE_PARTS[k]
                rows = image[k][0:nk, :, :].rearrange("p i f -> p (i f)")
                for hf in range(2):
                    inner = rows[:, bass.ds(pc * (P * C) + ROWLEN + C + 8 * C * hf, 1)]
                    nc.gpsimd.tensor_copy(
                        patch[k][0:nk, 384 * hf:384 * hf + 384].rearrange("p (c j i) -> p c j i", c=C, i=P),
                        strided(inner, [[1, C], [C, 8], [ROWLEN, P]])).then_inc(patch_ok, 1)
                beside = rows[:, bass.ds(pc * (P * C) + ROWLEN, 1)]
                nc.gpsimd.tensor_copy(
                    patch[k][0:nk, SIDES:ENDS].rearrange("p (s c i) -> p s c i", s=2, c=C),
                    strided(beside, [[(P + 1) * C, 2], [1, C], [ROWLEN, P]])).then_inc(patch_ok, 1)
                ends = rows[:, bass.ds(pc * (P * C) + C, 1)]
                nc.gpsimd.tensor_copy(
                    patch[k][0:nk, ENDS:KCOLS].rearrange("p (r c j) -> p r c j", r=2, c=C),
                    strided(ends, [[(P + 1) * ROWLEN, 2], [1, C], [C, P]])).then_inc(patch_ok, 1)
            for k in range(2):
                pool.wait_ge(image_in[k], 16 * TILE_ROWS[k])
                gather(0, k, k, True)
            with pool.Fori(1, G) as pc:
                for k in range(2):
                    gather(pc, k, 2 * pc + k, False)
            pool.wait_ge(rstd_ok, 1 + 2 * G)
            nc.gpsimd.tensor_tensor(rstd[:, :, :], rstd[:, :, :], half[:, :, :], ALU.pow).then_inc(rstd_pow, 1)

        @block.tensor
        def _(pe):
            def turn(k, t):
                pe.wait_ge(patch_ok, 4 * t + 4)
                nk = TILE_PARTS[k]
                for m in range(8):
                    last = pe.transpose(ps_T[k][0:KT[m], m, 0:nk], patch[k][0:nk, KOFF[m]:KOFF[m] + KT[m]],
                                        ident[0:nk, 0:nk])
                    if m == 3:
                        last.then_inc(transposed, 1)
                last.then_inc(patch_read, 1)

            def convolve(k, t, first):
                nk = TILE_PARTS[k]
                if not first:
                    pe.wait_ge(y_ok, t - 1)
                for m in range(8):
                    if m == 0:
                        pe.wait_ge(left_half, t + 1)
                    if m == 4:
                        pe.wait_ge(right_half, 2 * t + 2)
                    w = w_src[:, 0, m, :] if m < 6 else w_edge[0:(97 if m == 6 else 96), m - 6, :]
                    kk = 97 if m == 6 else KT[m]
                    last = pe.matmul(ps_y[k][0:nk, 0:D], patch_T[k][0:kk, m, 0:nk], w,
                                     start=(m == 0), stop=(m == 7))
                last.then_inc(conv_ok, 1)

            pe.wait_ge(ident_ok, 3)
            turn(0, 0)
            turn(1, 1)
            pe.wait_ge(w_in, 16 * W_LOADS)
            pe.wait_ge(w_sum, 4)
            pe.wait_ge(ones_ok, 2)
            convolve(0, 0, True)
            turn(0, 2)
            convolve(1, 1, True)
            with pe.Fori(1, G - 1) as pc:
                turn(1, 2 * pc + 1)
                convolve(0, 2 * pc, False)
                turn(0, 2 * pc + 2)
                convolve(1, 2 * pc + 1, False)
            turn(1, 2 * G - 1)
            convolve(0, 2 * G - 2, False)
            convolve(1, 2 * G - 1, False)

            def turn_normed(k, t, first):
                pe.wait_ge(normed_ok, t + 1)
                if not first:
                    pe.wait_ge(normed_T_ok, t - 1)
                nk = TILE_PARTS[k]
                pe.transpose(ps_n[k][:, 0:nk], normed[k][0:nk, :], ident[0:nk, 0:nk]).then_inc(normed_turned, 1)

            def dense(k, t):
                pe.wait_ge(normed_T_ok, t + 1)
                pe.wait_ge(token_ok, t - 1)
                nk = TILE_PARTS[k]
                pe.matmul(ps_y[k][0:nk, 0:D], normed_T[k][:, 0:nk], dense_sb[:, :],
                          start=True, stop=True).then_inc(dense_ok, 1)

            def dense_first(k, t):
                pe.wait_ge(y_ok, 2 * G)
                pe.wait_ge(small_in, 64)
                pe.wait_ge(normed_T_ok, t + 1)
                nk = TILE_PARTS[k]
                pe.matmul(ps_y[k][0:nk, 0:D], normed_T[k][:, 0:nk], dense_sb[:, :],
                          start=True, stop=True).then_inc(dense_ok, 1)
            turn_normed(0, 0, True)
            turn_normed(1, 1, True)
            dense_first(0, 0)
            turn_normed(0, 2, False)
            dense_first(1, 1)
            with pe.Fori(1, G - 1) as pc:
                turn_normed(1, 2 * pc + 1, False)
                dense(0, 2 * pc)
                turn_normed(0, 2 * pc + 2, False)
                dense(1, 2 * pc + 1)
            turn_normed(1, 2 * G - 1, False)
            dense(0, 2 * G - 2)
            dense(1, 2 * G - 1)

        @block.vector
        def _(dve):
            for k in range(2):
                nc.vector.memset(image[k][:, 1:P + 1, 0:C], 0.0).then_inc(borders_zero, 1)
                nc.vector.memset(image[k][:, 1:P + 1, ROWLEN - C:ROWLEN], 0.0).then_inc(borders_zero, 1)
            nc.vector.memset(image[0][0:B, 0, :], 0.0).then_inc(borders_zero, 1)
            nc.vector.memset(image[1][2 * B:3 * B, P + 1, :], 0.0).then_inc(borders_zero, 1)
            nc.vector.memset(w_src[:, 1:5, :, :], 0.0).then_inc(w_zero, 1)
            nc.vector.memset(rstd[:, :, :], 1.0).then_inc(rstd_ok, 1)
            for k in range(2):
                nc.vector.memset(patch_T[k][96:97, 6, :], 1.0).then_inc(ones_ok, 1)
            dve.wait_ge(w_in, 16 * W_LOADS)
            for s in range(1, 5):
                if s > 1:
                    dve.wait_ge(w_sum, s - 1)
                nc.vector.tensor_tensor(w_src[:, 0, :, :], w_src[:, 0, :, :], w_src[:, s, :, :],
                                        ALU.add).then_inc(w_sum, 1)

            def second_half(k, t, first):
                dve.wait_ge(patch_read, t + 1)
                if not first:
                    dve.wait_ge(conv_ok, t - 1)
                nk = TILE_PARTS[k]
                nc.vector.tensor_copy(patch_T[k][:, 4:6, 0:nk], ps_T[k][:, 4:6, 0:nk]).then_inc(right_half, 1)
                nc.vector.tensor_copy(patch_T[k][0:96, 6:8, 0:nk], ps_T[k][0:96, 6:8, 0:nk]).then_inc(right_half, 1)

            def moment(pc, k, t):
                nk = TILE_PARTS[k]
                dve.wait_ge(conv_ok, t + 1)
                nc.vector.bn_stats(stats[0:nk, k, :], ps_y[k][0:nk, 0:D]).then_inc(stats_ok, 1)
                dve.wait_ge(ones_ok, 2)
                dve.wait_ge(stats_ok, t + 1)
                nc.vector.bn_aggr(moments[0:nk, k, :], stats[0:nk, k, :]).then_inc(moments_ok, 1)
                dve.wait_ge(moments_ok, t + 1)
                here = y[0:nk, k, bass.ds(pc, 1), :].rearrange("p o d -> p (o d)")
                nc.vector.tensor_scalar(here, ps_y[k][0:nk, 0:D], moments[0:nk, k, 0:1], None,
                                        ALU.subtract).then_inc(y_ok, 1)
                nc.vector.tensor_scalar(rstd[0:nk, k, bass.ds(pc, 1)], moments[0:nk, k, 1:2], TOK_EPS, None,
                                        ALU.add).then_inc(rstd_ok, 1)

            dve.wait_ge(rstd_ok, 1)
            second_half(0, 0, True)
            second_half(1, 1, True)
            moment(0, 0, 0)
            second_half(0, 2, False)
            moment(0, 1, 1)
            with dve.Fori(1, G - 1) as pc:
                second_half(1, 2 * pc + 1, False)
                moment(pc, 0, 2 * pc)
                second_half(0, 2 * pc + 2, False)
                moment(pc, 1, 2 * pc + 1)
            second_half(1, 2 * G - 1, False)
            moment(G - 1, 0, 2 * G - 2)
            moment(G - 1, 1, 2 * G - 1)
            dve.wait_ge(rstd_pow, 1)
            dve.wait_ge(small_in, 64)

            def normalise(pc, k, t, first):
                if not first:
                    dve.wait_ge(normed_turned, t - 1)
                nk = TILE_PARTS[k]
                here = y[0:nk, k, bass.ds(pc, 1), :].rearrange("p o d -> p (o d)")
                scale = rstd[0:nk, k, bass.ds(pc, 1)]
                nc.vector.tensor_scalar(normed[k][0:nk, :], here, scale, None, ALU.mult).then_inc(normed_ok, 1)

            def add_bias(pc, k, t, first):
                dve.wait_ge(dense_ok, t + 1)
                if not first:
                    dve.wait_ge(stored[k], 16 * pc)
                nk = TILE_PARTS[k]
                nc.vector.tensor_tensor(token[k][0:nk, :], ps_y[k][0:nk, 0:D], dense_b_row[0:nk, :],
                                        ALU.add).then_inc(token_ok, 1)
            normalise(0, 0, 0, True)
            normalise(0, 1, 1, True)
            normalise(1, 0, 2, False)
            add_bias(0, 0, 0, True)
            normalise(1, 1, 3, False)
            add_bias(0, 1, 1, True)
            with dve.Fori(1, G - 1) as pc:
                for k in range(2):
                    normalise(pc + 1, k, 2 * pc + 2 + k, False)
                    add_bias(pc, k, 2 * pc + k, False)
            for k in range(2):
                add_bias(G - 1, k, 2 * G - 2 + k, False)


HEADS, DK = 8, 16
PAIRS = HEADS // 2
CHUNK = 16
CHUNKS = D // CHUNK
NDIM = 16
KPAD = 2 * N - 1


def attention(nc, h_dram, txt, w_qkv, b_qkv, w_out, b_out, p_coeff, q_coeff, gamma, adaptive, response, r,
              fetch_experts):
    with ExitStack() as ctx:
        def sb(name, shape, dt=F32):
            return ctx.enter_context(nc.sbuf_tensor(name, shape, dt))

        def sem(name):
            return ctx.enter_context(nc.semaphore(name))

        xn = sb("xn", [N, B, D])
        ident = sb("ident_c", [PART, PART])
        wide = sb("wide", [D, 3 * D])
        w_qqk = sb("w_qqk", [D, 3, D])
        wout_sb = sb("wout_sb", [D, D])
        b_row = sb("b_row", [1, 3 * D])
        b_qqk_row = sb("b_qqk_row", [1, 3, D])
        b_qqk = sb("b_qqk", [D, 3])
        bv_col = sb("bv_col", [D, 1])
        one = sb("one", [1, 1])
        bout_row = sb("bout_row", [N, D])
        bias = sb("bias", [N, D])
        mask = sb("mask", [N, N])
        mix = sb("mix", [PART, 2])
        mix_s = sb("mix_s", [PART, 3])
        coeff = sb("coeff", [D, 3, NDIM])
        powers = sb("powers", [D, N, NDIM])
        resp = sb("resp", [D, KPAD])
        hankel = [powers[0:N, :, :].rearrange("p n d -> p (n d)").rearrange("p (e n) -> p e n", e=CHUNK),
                  sb("hankel", [N, CHUNK, N])]
        toeplitz = [sb(f"toeplitz{k}", [N, CHUNK, N]) for k in range(2)]
        st = sb("st", [N, B, 6])
        mean = sb("mean", [N, B])
        gap = sb("gap", [N, B])
        rstd = sb("rstd_c", [N, B])
        half = sb("half_c", [N, B])
        xr = [sb(f"xr{k}", [N, D]) for k in range(2)]
        xT = [sb(f"xT{k}", [D, N]) for k in range(2)]
        qk = [sb(f"qk{k}", [D, 3, N]) for k in range(2)]
        vx = [sb(f"vx{k}", [N, HEADS, DK + 1]) for k in range(2)]
        prob = [sb(f"prob{k}", [N, PAIRS, 2, N]) for k in range(2)]
        top = [sb(f"top{k}", [N, PAIRS, 2]) for k in range(2)]
        probT = [toeplitz[1][:, HEADS * k:HEADS * k + HEADS, :] for k in range(2)]
        inv = [sb(f"inv{k}", [N, HEADS]) for k in range(2)]
        on = [sb(f"on{k}", [N, D]) for k in range(2)]
        oT = [sb(f"oT{k}", [D, N]) for k in range(2)]

        ps_s = ctx.enter_context(nc.psum_tensor("ps_s", [PART, PAIRS, 512], F32))
        ps_p = [ctx.enter_context(nc.psum_tensor(f"ps_p{k}", [PART, 512], F32)) for k in range(2)]
        ps_qk = ctx.enter_context(nc.psum_tensor("ps_qk", [PART, 512], F32))
        ps_x = ctx.enter_context(nc.psum_tensor("ps_x", [PART, 512], F32))
        S = ps_s[0:N, :, 0:2 * N].rearrange("p m (a j) -> p m a j", a=2)
        O = ps_p[0][0:N, 324:324 + HEADS * (DK + 1)].rearrange("p (h d) -> p h d", h=HEADS)
        W = ps_p[1][0:N, 324:324 + D]

        names = """setup_pool half_ok h_in small_in coeff_in adapt_in w_zero w_qqk_ok brow_zero brow_ok one_ok b_turned
            b_ok mix_max mix_sub mix_exp mix_sum mix_inv mix_ok bv_done bias_ok bias_w r_base st_ok m_gap m_ok var_ok
            rstd_ok xn_ok pow_ok resp_zero resp_ok resp_out q_sq cema_done cema_added
            xr_ok x_turned xT_ok qk_done v_done qk_ok v_ok s_done s_masked s_max s_sub p_ok p_turned pT_ok
            o_done o_inv o_ok o_turned oT_ok w_done r_ok vx_one""".split()
        q = {n: sem("c_" + n) for n in names}
        toeplitz_ok = [sem(f"c_toeplitz_ok{k}") for k in range(2)]
        hankel_in = [sem(f"c_hankel_in{k}") for k in range(2)]
        block = ctx.enter_context(nc.Block())

        SETUP_DMAS = 5

        @block.sync
        def _(sp):
            sp.dma_start(xn[0:PATCHES, :, :], h_dram.rearrange("b n d -> n b d")).then_inc(q["h_in"], 16)
            sp.dma_start(xn[PATCHES:N, :, :], txt.rearrange("b n d -> n b d")).then_inc(q["h_in"], 16)
            sp.wait_ge(q["resp_out"], 16)

            def load(c, k, first):
                if not first:
                    sp.wait_ge(toeplitz_ok[k], (c - k) // 2 if isinstance(c, int) else 0)
                start = response[bass.ds(c * CHUNK, 1), 0:1]
                sp.dma_start(hankel[k][:, :, :], bass.AP(start.tensor, start.offset, [[1, N], [KPAD, CHUNK], [1, N]])
                             ).then_inc(hankel_in[k], 16)
            for c in range(CHUNKS):
                load(c, c % 2, c < 2)
            fetch_experts(sp)

        @block.scalar
        def _(act):
            act.dma_start(coeff[:, 0, :], p_coeff).then_inc(q["coeff_in"], 16)
            act.dma_start(coeff[:, 1, :], q_coeff).then_inc(q["coeff_in"], 16)
            act.dma_start(coeff[:, 2, :], gamma).then_inc(q["coeff_in"], 16)
            act.dma_start(mix[:, :], adaptive.partition_broadcast(PART)).then_inc(q["adapt_in"], 16)
            act.dma_start(wide[:, :], w_qkv).then_inc(q["small_in"], 16)
            act.dma_start(wout_sb[:, :], w_out).then_inc(q["small_in"], 16)
            act.dma_start(b_row[:, :], b_qkv.rearrange("(o n) -> o n", o=1)).then_inc(q["small_in"], 16)
            act.dma_start(bv_col[:, :], b_qkv[2 * D:3 * D].rearrange("(n o) -> n o", o=1)).then_inc(q["small_in"], 16)
            act.dma_start(bout_row[:, :], b_out.partition_broadcast(N)).then_inc(q["small_in"], 16)
            act.wait_ge(q["mix_sub"], 1)
            nc.scalar.activation(mix[:, :], mix[:, :], ACT.Exp).then_inc(q["mix_exp"], 1)
            act.wait_ge(q["resp_ok"], 1)
            act.dma_start(response, resp[:, :]).then_inc(q["resp_out"], 16)

            def reverse(c, k, first):
                act.wait_ge(hankel_in[k], 8 * (c - k) + 16)
                if not first:
                    act.wait_ge(q["cema_done"], c - 1)
                nc.scalar.copy(toeplitz[k][:, :, :], strided(hankel[k][:, 0, N - 1:N], [[N, CHUNK], [-1, N]])
                               ).then_inc(toeplitz_ok[k], 1)
            for k in range(2):
                reverse(k, k, True)
            with act.Fori(1, CHUNKS // 2) as j:
                for k in range(2):
                    reverse(2 * j + k, k, False)

            def x_out(f, u, first):
                act.wait_ge(q["x_turned"], f + 1)
                if not first:
                    act.wait_ge(q["v_done"], f - 1)
                nc.scalar.copy(xT[u][:, :], ps_x[:, 0:N]).then_inc(q["xT_ok"], 1)

            def v_out(f, u, first):
                act.wait_ge(q["v_done"], f + 1)
                if not first:
                    act.wait_ge(q["o_done"], f - 1)
                nc.scalar.copy(vx[u][:, :, 0:DK],
                               ps_x[0:N, 128:256].rearrange("p (h d) -> p h d", h=HEADS)).then_inc(q["v_ok"], 1)

            def exponent(i, u):
                act.wait_ge(q["s_sub"], i + 1)
                nc.scalar.activation(prob[u][:, :, :, :], prob[u][:, :, :, :], ACT.Exp).then_inc(q["p_ok"], 1)

            def probs_out(i, u, first):
                for hf in range(2):
                    act.wait_ge(q["p_turned"], 2 * i + 1 + hf)
                    if not first:
                        act.wait_ge(q["o_done"], i - 1)
                    nc.scalar.copy(probT[u][:, 4 * hf:4 * hf + 4, :],
                                   ps_p[hf][0:N, 0:4 * N].rearrange("p (h j) -> p h j", h=4)).then_inc(q["pT_ok"], 1)

            def o_out(i, u, first):
                act.wait_ge(q["o_turned"], i + 1)
                if not first:
                    act.wait_ge(q["w_done"], i - 1)
                nc.scalar.copy(oT[u][:, :], ps_x[:, 256:256 + N]).then_inc(q["oT_ok"], 1)

            def step(i, u, first=False, front=True, following=True):
                if front:
                    x_out(i + 2, u, False)
                probs_out(i, u, first)
                if front:
                    v_out(i + 2, u, False)
                if following:
                    exponent(i + 1, 1 - u)
                o_out(i, u, first)
            for u in range(2):
                x_out(u, u, True)
                v_out(u, u, True)
            exponent(0, 0)
            for u in range(2):
                step(u, u, first=True)
            with act.Fori(1, B // 2 - 1) as j:
                for u in range(2):
                    step(2 * j + u, u)
            step(B - 2, 0, front=False)
            step(B - 1, 1, front=False, following=False)

        @block.gpsimd
        def _(pool):
            nc.gpsimd.memset(ident[:, :], 0.0).then_inc(q["setup_pool"], 1)
            nc.gpsimd.memset(mask[:, :], DK ** -0.5).then_inc(q["setup_pool"], 1)
            nc.gpsimd.memset(half[:, :], -0.5).then_inc(q["half_ok"], 1)
            pool.wait_ge(q["setup_pool"], 2)
            nc.gpsimd.affine_select(out=ident[:, :], in_=ident[:, :], compare_op=ALU.not_equal, fill=1.0,
                                    base=0, pattern=[[-1, PART]], channel_multiplier=1).then_inc(q["setup_pool"], 1)
            nc.gpsimd.affine_select(out=mask[:, :], in_=mask[:, :], compare_op=ALU.is_ge, fill=0.0,
                                    base=0, pattern=[[-1, N]], channel_multiplier=1).then_inc(q["setup_pool"], 1)
            pool.wait_ge(q["h_in"], 32)
            pool.wait_ge(q["bias_w"], 1)
            nc.gpsimd.tensor_tensor(r[:, :, :], xn[:, :, :], bias[:, :].unsqueeze(1).to_broadcast([N, B, D]),
                                    ALU.add).then_inc(q["r_base"], 1)
            pool.wait_ge(q["var_ok"], 1)
            pool.wait_ge(q["half_ok"], 1)
            nc.gpsimd.tensor_tensor(rstd[:, :], rstd[:, :], half[:, :], ALU.pow).then_inc(q["rstd_ok"], 1)

            def fetch(f, u, first):
                if not first:
                    pool.wait_ge(q["x_turned"], f - 1)
                nc.gpsimd.tensor_copy(xr[u][:, :], xn[:, bass.ds(f, 1), :].rearrange("p o d -> p (o d)")
                                      ).then_inc(q["xr_ok"], 1)

            def subtract(f, u):
                pool.wait_ge(q["s_max"], f + 1)
                nc.gpsimd.tensor_tensor(prob[u][:, :, :, :], prob[u][:, :, :, :],
                                        top[u][:, :, :].unsqueeze(3).to_broadcast([N, PAIRS, 2, N]),
                                        ALU.subtract).then_inc(q["s_sub"], 1)
            pool.wait_ge(q["xn_ok"], B)
            fetch(0, 0, True)
            fetch(1, 1, True)
            subtract(0, 0)
            fetch(2, 0, False)
            subtract(1, 1)
            fetch(3, 1, False)
            with pool.Fori(1, B // 2 - 1) as j:
                for u in range(2):
                    subtract(2 * j + u, u)
                    fetch(2 * j + 2 + u, u, False)
            subtract(B - 2, 0)
            subtract(B - 1, 1)

        @block.tensor
        def _(pe):
            pe.wait_ge(q["brow_ok"], 3)
            pe.wait_ge(q["one_ok"], 1)
            for a in range(3):
                pe.matmul(ps_qk[:, a:a + 1], b_qqk_row[:, a, :], one[:, :], start=(a == 0), stop=(a == 2),
                          skip_group_check=True).then_inc(q["b_turned"], 1)
            pe.wait_ge(q["small_in"], 16 * SETUP_DMAS)
            pe.matmul(ps_x[0:N, 0:D], bv_col[:, :].to_broadcast([D, N]), wout_sb[:, :],
                      start=True, stop=True).then_inc(q["bv_done"], 1)
            pe.wait_ge(q["xn_ok"], B)

            def cema(c, k, first):
                if not first:
                    pe.wait_ge(q["cema_added"], c - 1)
                for e in range(CHUNK):
                    if e == 0:
                        pe.wait_ge(toeplitz_ok[k], 1)
                    mm = pe.matmul(ps_s[0:N, k, 32 * e:32 * e + 32], toeplitz[k][:, e, :],
                                   xn[:, :, bass.ds(c * CHUNK + e, 1)].rearrange("p b o -> p (b o)"),
                                   start=(e == 0), stop=(e == CHUNK - 1), skip_group_check=True)
                mm.then_inc(q["cema_done"], 1)
            for k in range(2):
                cema(k, k, True)
            with pe.Fori(1, CHUNKS // 2) as j:
                for k in range(2):
                    pe.wait_ge(toeplitz_ok[k], j + 1)
                    pe.wait_ge(q["cema_added"], 2 * j + k - 1)
                    for e in range(CHUNK):
                        mm = pe.matmul(ps_s[0:N, k, 32 * e:32 * e + 32], toeplitz[k][:, e, :],
                                       xn[:, :, bass.ds(j * (2 * CHUNK) + (k * CHUNK + e), 1)].rearrange("p b o -> p (b o)"),
                                       start=(e == 0), stop=(e == CHUNK - 1), skip_group_check=True)
                    mm.then_inc(q["cema_done"], 1)
            pe.wait_ge(q["cema_added"], CHUNKS)
            pe.wait_ge(q["b_ok"], 1)
            pe.wait_ge(q["w_qqk_ok"], 3)
            pe.wait_ge(q["bias_ok"], 1)
            pe.wait_ge(q["setup_pool"], 4)

            def turn_x(f, u, t7):
                pe.wait_ge(q["xr_ok"], f + 1)
                for name, value in t7:
                    pe.wait_ge(q[name], value)
                pe.transpose(ps_x[:, 0:N], xr[u][:, :], ident[0:N, 0:N]).then_inc(q["x_turned"], 1)

            def project(f, u, first):
                pe.wait_ge(q["xT_ok"], f + 1)
                if not first:
                    pe.wait_ge(q["qk_ok"], f)
                for a in range(3):
                    mm = pe.matmul(ps_qk[:, N * a:N * a + N], w_qqk[:, a, :], xT[u][:, :], start=(a == 0),
                                   stop=(a == 2), skip_group_check=True)
                mm.then_inc(q["qk_done"], 1)
                pe.matmul(ps_x[0:N, 128:256], xT[u][:, :], wide[:, 2 * D:3 * D], start=True,
                          stop=True).then_inc(q["v_done"], 1)

            def scores(f, u, first):
                pe.wait_ge(q["qk_ok"], f + 1)
                if not first:
                    pe.wait_ge(q["s_masked"], f)
                for a in range(2):
                    for m in range(PAIRS):
                        at = slice(32 * m, 32 * m + 32)
                        mm = pe.matmul(S[:, m, a, :], qk[u][at, a, :], qk[u][at, 2, :], start=(a == 0), stop=(a == 1),
                                       skip_group_check=True)
                mm.then_inc(q["s_done"], 1)

            def turn_probs(i, u, first):
                pe.wait_ge(q["p_ok"], i + 1)
                for hf in range(2):
                    if not first:
                        pe.wait_ge(q["r_ok" if hf else "o_ok"], i)
                    for hh in range(4):
                        mm = pe.transpose(ps_p[hf][0:N, N * hh:N * hh + N], prob[u][:, 2 * hf + hh // 2, hh % 2, :],
                                          ident[0:N, 0:N])
                    mm.then_inc(q["p_turned"], 1)

            def weigh(i, u):
                pe.wait_ge(q["v_ok"], i + 1)
                pe.wait_ge(q["pT_ok"], 2 * i + 2)
                for hd in range(HEADS):
                    mm = pe.matmul(O[:, hd, :], probT[u][:, hd, :], vx[u][:, hd, :], start=(hd == 0),
                                   stop=(hd == HEADS - 1), skip_group_check=True)
                mm.then_inc(q["o_done"], 1)

            def turn_o(i, u, v):
                pe.wait_ge(q["o_ok"], i + 1)
                pe.wait_ge(q["v_ok"], v)
                pe.transpose(ps_x[:, 256:256 + N], on[u][:, :], ident[0:N, 0:N]).then_inc(q["o_turned"], 1)

            def project_out(i, u):
                pe.wait_ge(q["oT_ok"], i + 1)
                pe.matmul(W, oT[u][:, :], wout_sb[:, :], start=True, stop=True).then_inc(q["w_done"], 1)

            def step(i, u, first=False, front=True):
                if front:
                    turn_x(i + 2, u, [("oT_ok", i)] if not (isinstance(i, int) and i == 0) else [("v_ok", 2)])
                turn_probs(i, u, isinstance(i, int) and i == 0)
                if front:
                    project(i + 2, u, False)
                weigh(i, u)
                if front:
                    scores(i + 2, u, False)
                turn_o(i, u, i + 3 if front else B)
                project_out(i, u)
            turn_x(0, 0, [("b_ok", 1)])
            project(0, 0, True)
            scores(0, 0, True)
            turn_x(1, 1, [("v_ok", 1)])
            project(1, 1, False)
            scores(1, 1, False)
            for u in range(2):
                step(u, u, first=True)
            with pe.Fori(1, B // 2 - 1) as j:
                for u in range(2):
                    step(2 * j + u, u)
            step(B - 2, 0, front=False)
            step(B - 1, 1, front=False)

        @block.vector
        def _(dve):
            nc.vector.memset(w_qqk[:, 0:2, :], 0.0).then_inc(q["w_zero"], 1)
            nc.vector.memset(b_qqk_row[:, :, :], 0.0).then_inc(q["brow_zero"], 1)
            nc.vector.memset(one[:, :], 1.0).then_inc(q["one_ok"], 1)
            nc.vector.memset(resp[:, N:KPAD], 0.0).then_inc(q["resp_zero"], 1)
            for u in range(2):
                nc.vector.memset(vx[u][:, :, DK:DK + 1], 1.0).then_inc(q["vx_one"], 1)
            dve.wait_ge(q["adapt_in"], 16)
            nc.vector.tensor_reduce(mix_s[:, 0:1], mix[:, :], AX.X, ALU.max).then_inc(q["mix_max"], 1)
            dve.wait_ge(q["mix_max"], 1)
            nc.vector.tensor_scalar(mix[:, :], mix[:, :], mix_s[:, 0:1], None, ALU.subtract).then_inc(q["mix_sub"], 1)
            dve.wait_ge(q["coeff_in"], 48)
            nc.vector.tensor_tensor(powers[:, N - 1, :], coeff[:, 0, :], coeff[:, 2, :], ALU.mult).then_inc(q["pow_ok"], 1)
            have, steps = 1, 1
            while have < N:
                new = min(have, N - have)
                dve.wait_ge(q["pow_ok"], steps)
                if steps > 1:
                    dve.wait_ge(q["q_sq"], steps - 1)
                nc.vector.tensor_tensor(powers[:, N - have - new:N - have, :], powers[:, N - new:N, :],
                                        coeff[:, 1:2, :].to_broadcast([D, new, NDIM]), ALU.mult).then_inc(q["pow_ok"], 1)
                have, steps = have + new, steps + 1
                if have < N:
                    dve.wait_ge(q["pow_ok"], steps)
                    nc.vector.tensor_tensor(coeff[:, 1, :], coeff[:, 1, :], coeff[:, 1, :],
                                            ALU.mult).then_inc(q["q_sq"], 1)
            dve.wait_ge(q["mix_exp"], 1)
            nc.vector.tensor_reduce(mix_s[:, 1:2], mix[:, :], AX.X, ALU.add).then_inc(q["mix_sum"], 1)
            dve.wait_ge(q["mix_sum"], 1)
            nc.vector.reciprocal(mix_s[:, 2:3], mix_s[:, 1:2]).then_inc(q["mix_inv"], 1)
            dve.wait_ge(q["mix_inv"], 1)
            nc.vector.tensor_scalar(mix[:, :], mix[:, :], mix_s[:, 2:3], None, ALU.mult).then_inc(q["mix_ok"], 1)
            dve.wait_ge(q["pow_ok"], steps)
            nc.vector.tensor_reduce(resp[:, 0:N], powers[:, :, :], AX.X, ALU.add).then_inc(q["resp_zero"], 1)
            dve.wait_ge(q["resp_zero"], 2)
            dve.wait_ge(q["mix_ok"], 1)
            nc.vector.tensor_scalar(resp[:, 0:N], resp[:, 0:N], mix[:, 1:2], None,
                                    ALU.mult).then_inc(q["resp_ok"], 1)
            dve.wait_ge(q["small_in"], 16 * SETUP_DMAS)
            dve.wait_ge(q["w_zero"], 1)
            dve.wait_ge(q["brow_zero"], 1)
            for a in range(2):
                heads = slice(a, HEADS, 2)
                nc.vector.tensor_copy(
                    w_qqk[:, a, :].rearrange("p (h d) -> p h d", h=HEADS)[:, heads, :],
                    wide[:, 0:D].rearrange("p (h d) -> p h d", h=HEADS)[:, heads, :]).then_inc(q["w_qqk_ok"], 1)
                nc.vector.tensor_copy(
                    b_qqk_row[:, a, :].rearrange("p (h d) -> p h d", h=HEADS)[:, heads, :],
                    b_row[:, 0:D].rearrange("p (h d) -> p h d", h=HEADS)[:, heads, :]).then_inc(q["brow_ok"], 1)
            nc.vector.tensor_copy(w_qqk[:, 2, :], wide[:, D:2 * D]).then_inc(q["w_qqk_ok"], 1)
            nc.vector.tensor_copy(b_qqk_row[:, 2, :], b_row[:, D:2 * D]).then_inc(q["brow_ok"], 1)
            dve.wait_ge(q["b_turned"], 3)
            nc.vector.tensor_copy(b_qqk[:, :], ps_qk[:, 0:3]).then_inc(q["b_ok"], 1)
            dve.wait_ge(q["bv_done"], 1)
            nc.vector.tensor_tensor(bias[:, :], ps_x[0:N, 0:D], bout_row[:, :], ALU.add).then_inc(q["bias_ok"], 1)
            dve.wait_ge(q["bias_ok"], 1)
            nc.vector.tensor_scalar(bias[:, :], bias[:, :], mix[0:N, 0:1], None, ALU.mult).then_inc(q["bias_w"], 1)
            dve.wait_ge(q["h_in"], 32)
            with dve.Fori(0, B // 4) as j:
                for u in range(4):
                    here = bass.ds(4 * j + u, 1)
                    nc.vector.bn_stats(st[:, here, :].rearrange("p o s -> p (o s)"),
                                       xn[:, here, :].rearrange("p o d -> p (o d)")).then_inc(q["st_ok"], 1)
            moments_to_rstd(dve, nc, st, mean, gap, rstd, q)
            dve.wait_ge(q["rstd_ok"], 1)
            dve.wait_ge(q["r_base"], 1)
            with dve.Fori(0, B // 4) as j:
                for u in range(4):
                    here = bass.ds(4 * j + u, 1)
                    x = xn[:, here, :].rearrange("p o d -> p (o d)")
                    nc.vector.tensor_scalar(x, x, mean[:, here], rstd[:, here],
                                            ALU.subtract, ALU.mult).then_inc(q["xn_ok"], 1)

            def add_cema(c, k):
                dve.wait_ge(q["cema_done"], c + 1)
                at = r[:, :, bass.ds(c * CHUNK, CHUNK)]
                nc.vector.tensor_tensor(at, ps_s[0:N, k, :].rearrange("p (e b) -> p b e", b=B), at,
                                        ALU.add).then_inc(q["cema_added"], 1)
            with dve.Fori(0, CHUNKS // 2) as j:
                for k in range(2):
                    add_cema(2 * j + k, k)

            def add_biases(f, u, first):
                dve.wait_ge(q["qk_done"], f + 1)
                if not first:
                    dve.wait_ge(q["s_done"], f - 1)
                nc.vector.tensor_tensor(qk[u][:, :, :], ps_qk[:, 0:3 * N].rearrange("p (a n) -> p a n", a=3),
                                        b_qqk[:, :].unsqueeze(2).to_broadcast([D, 3, N]), ALU.add).then_inc(q["qk_ok"], 1)

            def mask_scores(f, u, first):
                dve.wait_ge(q["s_done"], f + 1)
                if not first:
                    dve.wait_ge(q["p_turned"], 2 * f - 2)
                nc.vector.tensor_tensor(prob[u][:, :, :, :], S,
                                        strided(mask[:, :], [[0, PAIRS], [0, 2], [1, N]]), ALU.mult
                                        ).then_inc(q["s_masked"], 1)
                dve.wait_ge(q["s_masked"], f + 1)
                if not first:
                    dve.wait_ge(q["s_sub"], f - 1)
                nc.vector.tensor_reduce(top[u][:, :, :], prob[u][:, :, :, :], AX.X, ALU.max).then_inc(q["s_max"], 1)

            def normalise(i, u, first):
                dve.wait_ge(q["o_done"], i + 1)
                nc.vector.reciprocal(inv[u][:, :], O[:, :, DK]).then_inc(q["o_inv"], 1)
                dve.wait_ge(q["o_inv"], i + 1)
                if not first:
                    dve.wait_ge(q["o_turned"], i - 1)
                nc.vector.tensor_tensor(on[u][:, :].rearrange("p (h d) -> p h d", h=HEADS), O[:, :, 0:DK],
                                        inv[u][:, :].unsqueeze(2).to_broadcast([N, HEADS, DK]), ALU.mult
                                        ).then_inc(q["o_ok"], 1)

            def accumulate(i):
                at = r[:, bass.ds(i, 1), :].rearrange("p o d -> p (o d)")
                dve.wait_ge(q["w_done"], i + 1)
                nc.vector.scalar_tensor_tensor(out=at, in0=W, scalar=mix[0:N, 0:1], in1=at, op0=ALU.mult,
                                               op1=ALU.add).then_inc(q["r_ok"], 1)

            def step(i, u, first=False, front=True):
                if front:
                    add_biases(i + 2, u, False)
                normalise(i, u, first)
                if front:
                    mask_scores(i + 2, u, False)
                accumulate(i)
            dve.wait_ge(q["cema_added"], CHUNKS)
            dve.wait_ge(q["setup_pool"], 4)
            for u in range(2):
                add_biases(u, u, True)
                mask_scores(u, u, True)
            for u in range(2):
                step(u, u, first=True)
            with dve.Fori(1, B // 2 - 1) as j:
                for u in range(2):
                    step(2 * j + u, u)
            step(B - 2, 0, front=False)
            step(B - 1, 1, front=False)


def moments_to_rstd(dve, nc, st, mean, gap, rstd, q):
    dve.wait_ge(q["st_ok"], B)
    nc.vector.tensor_tensor(mean[:, :], st[:, :, 1], st[:, :, 4], ALU.add).then_inc(q["m_gap"], 1)
    nc.vector.tensor_tensor(gap[:, :], st[:, :, 1], st[:, :, 4], ALU.subtract).then_inc(q["m_gap"], 1)
    nc.vector.tensor_tensor(rstd[:, :], st[:, :, 2], st[:, :, 5], ALU.add).then_inc(q["m_gap"], 1)
    dve.wait_ge(q["m_gap"], 3)
    nc.vector.tensor_scalar(mean[:, :], mean[:, :], 0.5, None, ALU.mult).then_inc(q["m_ok"], 1)
    nc.vector.scalar_tensor_tensor(out=gap[:, :], in0=gap[:, :], scalar=0.25, in1=gap[:, :], op0=ALU.mult,
                                   op1=ALU.mult).then_inc(q["m_ok"], 1)
    nc.vector.tensor_scalar(rstd[:, :], rstd[:, :], 1.0 / D, LN_EPS, ALU.mult, ALU.add).then_inc(q["m_ok"], 1)
    dve.wait_ge(q["m_ok"], 3)
    nc.vector.tensor_tensor(rstd[:, :], rstd[:, :], gap[:, :], ALU.add).then_inc(q["var_ok"], 1)


GROUPS, EXPERTS = 8, 8
GE = GROUPS * EXPERTS
HID = 2 * D
TOKENS = B * N
PICKS = 4
QUAD = 4
QUADS = B // QUAD
REGION = TOKENS
SLOT = D + 2
TILE = 128
TILES = (PICKS * TOKENS + GE * (TILE - 1)) // TILE
SKIP = float(1 << 20)
BF16 = mybir.dt.bfloat16
BIG = 3.0e38

(TOP1, BELOW1, RANK1, FIRST1, HOT1, LEFT, TOP2, BELOW2, RANK2, FIRST2, HOT2, MARGIN, ODDS, PART1, PART2,
 PAIR0, PAIR1, PAIR2, PAIR3, EITHER, CHOSEN, SHARE0, SHARE1, SHARES, WEIGHT, WEIGHED, GATES, SLOTS, PLACED,
 SLOT_OF, SLOT_INT, ADDED, RUNNING, RESULT) = range(1, 35)
ROUTE_STEPS = RESULT


def route(nc, r, g1, g2, b2, slots_dram, weight, tab_base, tab_expert, tab_skip):
    with ExitStack() as ctx:
        def sb(name, shape, dt=F32):
            return ctx.enter_context(nc.sbuf_tensor(name, shape, dt))

        def sem(name):
            return ctx.enter_context(nc.semaphore(name))

        def bank(name, dt=F32):
            return ctx.enter_context(nc.psum_tensor(name, [PART, 2048 // (4 if dt == F32 else 2)], dt))

        ident = sb("ident_d", [PART, PART])
        gate_w = sb("gate_w", [D, GROUPS + GE])
        b2_sb = sb("b2_sb", [GE, D])
        st = sb("st_d", [N, B, 6])
        mean = sb("mean_d", [N, B])
        gap = sb("gap_d", [N, B])
        rstd = sb("rstd_d", [N, B])
        half = sb("half_d", [N, B])
        rows = [sb(f"rows{k}", [N, QUAD, PICKS, SLOT]) for k in range(2)]
        xT = [sb(f"xT_d{k}", [D, QUAD * N]) for k in range(2)]
        place = sb("place", [N, B, PICKS])
        order = sb("order", [N, EXPERTS])
        region = sb("region", [N, GE])
        before = sb("before", [N, N], BF16)
        ones_b = sb("ones_b", [N, N], BF16)
        ones_f = sb("ones_f", [N, 1])
        top = sb("top_d", [N, 2, QUAD, 9])
        below = sb("below", [N, QUAD, 9, EXPERTS])
        ranked = sb("ranked", [N, QUAD, 9, EXPERTS])
        left = sb("left", [N, QUAD, 9, EXPERTS])
        winner = sb("winner", [N, 2, QUAD, 9])
        hot = sb("hot", [N, 2, QUAD, 9, EXPERTS])
        margin = sb("margin", [N, QUAD, 9])
        odds = sb("odds", [N, QUAD, 9])
        part = sb("part", [N, 2, QUAD, 9])
        pair = sb("pair", [N, PICKS, QUAD, GE])
        either = sb("either", [N, QUAD, 9, EXPERTS])
        chosen = sb("chosen", [N, QUAD, GE], BF16)
        share = sb("share", [N, 2, 2, QUAD, GROUPS])
        weighed = sb("weighed", [N, PICKS, QUAD, GE])
        gates = [sb(f"gates{k}", [N, QUAD, GE]) for k in range(2)]
        gates_T = [sb(f"gates_T{k}", [GE, QUAD * N]) for k in range(2)]
        slot_row = sb("slot_row", [N, QUAD, GE])
        slot_f = sb("slot_f", [N, PICKS, QUAD])
        shares = sb("shares", [N, PICKS, QUAD])
        slot = [sb(f"slot{k}", [N, PICKS, QUAD], I32) for k in range(2)]
        added_f = sb("added_f", [N, GE])
        running = sb("running", [N, GE], BF16)
        blank = sb("blank", [PART, SLOT])
        count = sb("count", [GE, 1])
        count_i = sb("count_i", [GE, 1], I32)
        tiles = sb("tiles", [GE, 1])
        upto = sb("upto", [GE, GE])
        bounds = sb("bounds", [GE, 2])
        tile_no = sb("tile_no", [GE, TILES])
        began = sb("began", [GE, TILES])
        mine = sb("mine", [GE, TILES])
        facts = sb("facts", [GE, 5])
        tile_of = sb("tile_of", [PART, TILES])
        at = sb("at", [PART, TILES])
        rel = sb("rel", [PART, TILES])
        unused = sb("unused", [PART, TILES])
        lane = sb("lane", [PART, 1])

        ps_x, ps_l, ps_r, ps_g, ps_b = bank("ps_dx"), bank("ps_dl"), bank("ps_dr"), bank("ps_dg"), bank("ps_db")
        ps_f = [bank(f"ps_df{k}") for k in range(3)]

        names = """x_part pool_base pool_ok half_ok blank_ok blank_base blank_out gates_in b2_in st_ok m_gap m_ok var_ok rstd_ok
            pad_ok running_zero x_ok place_ok x_turned xT_ok logits odds_exp ranks gates_turned gates_T_ok result
            route_step counted count_ok tiles_ok ends mine_ok spread table_step scattered0 scattered1""".split()
        q = {n: sem("d_" + n) for n in names}
        scattered = [q["scattered0"], q["scattered1"]]
        block = ctx.enter_context(nc.Block())
        POOL_SETUP = 12

        @block.sync
        def _(sp):
            sp.dma_start(gate_w[:, 0:GROUPS], g1).then_inc(q["gates_in"], 16)
            sp.dma_start(gate_w[:, GROUPS:].rearrange("d (g e) -> d g e", g=GROUPS),
                         g2.rearrange("g d e -> d g e")).then_inc(q["gates_in"], 16)
            sp.dma_start(b2_sb[:, :], b2.rearrange("g e d -> (g e) d")).then_inc(q["b2_in"], 16)
            sp.wait_ge(q["blank_ok"], 1)
            sp.dma_start(slots_dram.rearrange("(e p) f -> p e f", p=REGION)[0:PART],
                         blank[:, :].unsqueeze(1).to_broadcast([PART, GE + 1, SLOT])).then_inc(q["blank_out"], 16)
            sp.wait_ge(q["blank_out"], 16)

        @block.gpsimd
        def _(pool):
            def setup(n, inst):
                inst.then_inc(q["pool_ok"], 1)
            nc.gpsimd.memset(blank[:, :], 0.0).then_inc(q["blank_base"], 1)
            nc.gpsimd.memset(ident[:, :], 0.0).then_inc(q["pool_base"], 1)
            nc.gpsimd.memset(before[:, :], 1.0).then_inc(q["pool_base"], 1)
            nc.gpsimd.memset(upto[:, :], 1.0).then_inc(q["pool_base"], 1)
            nc.gpsimd.memset(half[:, :], -0.5).then_inc(q["half_ok"], 1)
            pool.wait_ge(q["blank_base"], 1)
            nc.gpsimd.memset(blank[:, D:D + 1], SKIP).then_inc(q["blank_ok"], 1)
            pool.wait_ge(q["pool_base"], 3)
            setup(0, nc.gpsimd.affine_select(out=ident[:, :], in_=ident[:, :], compare_op=ALU.not_equal, fill=1.0,
                                             base=0, pattern=[[-1, PART]], channel_multiplier=1))
            setup(1, nc.gpsimd.affine_select(out=before[:, :], in_=before[:, :], compare_op=ALU.is_gt, fill=0.0,
                                             base=0, pattern=[[1, N]], channel_multiplier=-1))
            setup(2, nc.gpsimd.affine_select(out=upto[:, :], in_=upto[:, :], compare_op=ALU.is_ge, fill=0.0,
                                             base=0, pattern=[[1, GE]], channel_multiplier=-1))
            setup(3, nc.gpsimd.memset(ones_b[:, :], 1.0))
            setup(4, nc.gpsimd.memset(ones_f[:, :], 1.0))
            setup(5, nc.gpsimd.iota(place[:, :, :], pattern=[[N, B], [TOKENS, PICKS]], base=0, channel_multiplier=1,
                                    allow_small_or_imprecise_dtypes=True))
            setup(6, nc.gpsimd.iota(order[:, :], pattern=[[-1, EXPERTS]], base=EXPERTS, channel_multiplier=0,
                                    allow_small_or_imprecise_dtypes=True))
            setup(7, nc.gpsimd.iota(region[:, :], pattern=[[REGION, GE]], base=0, channel_multiplier=0,
                                    allow_small_or_imprecise_dtypes=True))
            setup(8, nc.gpsimd.iota(tile_no[:, :], pattern=[[1, TILES]], base=0, channel_multiplier=0,
                                    allow_small_or_imprecise_dtypes=True))
            setup(9, nc.gpsimd.iota(tile_of[:, :], pattern=[[TILE, TILES]], base=0, channel_multiplier=0,
                                    allow_small_or_imprecise_dtypes=True))
            setup(10, nc.gpsimd.iota(lane[:, :], pattern=[[0, 1]], base=0, channel_multiplier=1,
                                     allow_small_or_imprecise_dtypes=True))
            setup(11, nc.gpsimd.memset(facts[:, 0:1], 1.0))
            pool.wait_ge(q["var_ok"], 1)
            pool.wait_ge(q["half_ok"], 1)
            nc.gpsimd.tensor_tensor(rstd[:, :], rstd[:, :], half[:, :], ALU.pow).then_inc(q["rstd_ok"], 1)

            def scatter(t, u):
                pool.wait_ge(q["place_ok"], t + 1)
                pool.wait_ge(q["route_step"], slots_known)
                pool.reg_add(slots_known, slots_known, ROUTE_STEPS)
                for b in range(QUAD):
                    for k in range(PICKS):
                        nc.gpsimd.indirect_dma_start(
                            out=slots_dram, out_offset=bass.IndirectOffsetOnAxis(ap=slot[u][:, k, b:b + 1], axis=0),
                            in_=rows[u][:, b, k, :], in_offset=None).then_inc(scattered[u], 16)
            slots_known = pool.alloc_register("slots_known")
            pool.reg_mov(slots_known, SLOT_INT)
            pool.wait_ge(q["blank_out"], 16)
            with pool.Fori(0, QUADS // 2) as j:
                for u in range(2):
                    scatter(2 * j + u, u)
            for u in range(2):
                pool.wait_ge(scattered[u], 16 * QUAD * PICKS * QUADS // 2)

        @block.scalar
        def _(act):
            def step(t, u, first):
                act.wait_ge(q["x_turned"], t + 1)
                if not first:
                    act.wait_ge(q["logits"], t - 1)
                nc.scalar.copy(xT[u][:, :], ps_x[:, 0:QUAD * N]).then_inc(q["xT_ok"], 1)
                act.wait_ge(q["route_step"], ROUTE_STEPS * t + MARGIN)
                nc.scalar.activation(odds[:, :, :], margin[:, :, :], ACT.Exp).then_inc(q["odds_exp"], 1)
                act.wait_ge(q["gates_turned"], t + 1)
                if not first:
                    act.wait_ge(q["result"], t - 1)
                nc.scalar.copy(gates_T[u][:, :], ps_g[0:GE, 0:QUAD * N]).then_inc(q["gates_T_ok"], 1)
            for u in range(2):
                step(u, u, True)
            with act.Fori(1, QUADS // 2) as j:
                for u in range(2):
                    step(2 * j + u, u, False)

        @block.tensor
        def _(pe):
            pe.wait_ge(q["pool_ok"], POOL_SETUP)
            pe.wait_ge(q["gates_in"], 32)
            pe.wait_ge(q["b2_in"], 16)
            gates_known = pe.alloc_register("gates_known")
            pe.reg_mov(gates_known, GATES)

            def step(t, u, first):
                pe.wait_ge(q["x_ok"], t + 1)
                if not first:
                    pe.wait_ge(q["xT_ok"], t)
                for b in range(QUAD):
                    mm = pe.transpose(ps_x[:, N * b:N * b + N], rows[u][:, b, 0, 0:D], ident[0:N, 0:N])
                mm.then_inc(q["x_turned"], 1)
                pe.wait_ge(q["xT_ok"], t + 1)
                if not first:
                    pe.wait_ge(q["route_step"], ROUTE_STEPS * (t - 1) + RESULT)
                for b in range(QUAD):
                    mm = pe.matmul(ps_l[0:N, 72 * b:72 * b + 72], xT[u][:, N * b:N * b + N], gate_w[:, :],
                                   start=(b == 0), stop=(b == QUAD - 1), skip_group_check=True)
                mm.then_inc(q["logits"], 1)
                pe.wait_ge(q["route_step"], ROUTE_STEPS * t + CHOSEN)
                for b in range(QUAD):
                    out = ps_r[0:N, GE * b:GE * b + GE]
                    pe.matmul(out, before[:, :], chosen[:, b, :], start=(b == 0), stop=False, skip_group_check=True)
                    for c in range(b):
                        pe.matmul(out, ones_b[:, :], chosen[:, c, :], start=False, stop=False, skip_group_check=True)
                    mm = pe.matmul(out, ones_b[:, :], running[:, :], start=False, stop=(b == QUAD - 1),
                                   skip_group_check=True)
                mm.then_inc(q["ranks"], 1)
                pe.wait_ge(q["route_step"], gates_known)
                pe.reg_add(gates_known, gates_known, ROUTE_STEPS)
                for b in range(QUAD):
                    mm = pe.transpose(ps_g[0:GE, N * b:N * b + N], gates[u][:, b, :], ident[0:N, 0:N])
                mm.then_inc(q["gates_turned"], 1)
                pe.wait_ge(q["gates_T_ok"], t + 1)
                for b in range(QUAD):
                    mm = pe.matmul(ps_b[0:N, D * b:D * b + D], gates_T[u][:, N * b:N * b + N], b2_sb[:, :],
                                   start=(b == 0), stop=(b == QUAD - 1), skip_group_check=True)
                mm.then_inc(q["result"], 1)
            step(0, 0, True)
            step(1, 1, False)
            with pe.Fori(1, QUADS // 2) as j:
                for u in range(2):
                    step(2 * j + u, u, False)
            pe.wait_ge(q["route_step"], ROUTE_STEPS * QUADS)
            pe.wait_ge(q["count_ok"], 1)
            pe.matmul(ps_l[0:GE, 0:1], added_f[:, :], ones_f[:, :], start=True, stop=True).then_inc(q["counted"], 1)
            pe.wait_ge(q["tiles_ok"], 1)
            pe.matmul(ps_r[0:GE, 0:1], upto[:, :], tiles[:, :], start=True, stop=True).then_inc(q["ends"], 1)
            pe.wait_ge(q["mine_ok"], 1)
            for n in range(5):
                pe.matmul(ps_f[n // 2][:, TILES * (n % 2):TILES * (n % 2) + TILES],
                          facts[:, n:n + 1].to_broadcast([GE, PART]), mine[:, :], start=(n % 2 == 0),
                          stop=(n % 2 == 1 or n == 4), skip_group_check=True).then_inc(q["spread"], 1)

        @block.vector
        def _(dve):
            nc.vector.memset(running[:, :], 0.0).then_inc(q["running_zero"], 1)
            for u in range(2):
                nc.vector.memset(rows[u][:, :, :, D + 1:SLOT], 0.0).then_inc(q["pad_ok"], 1)
            with dve.Fori(0, B // 4) as j:
                for u in range(4):
                    here = bass.ds(4 * j + u, 1)
                    nc.vector.bn_stats(st[:, here, :].rearrange("p o s -> p (o s)"),
                                       r[:, here, :].rearrange("p o d -> p (o d)")).then_inc(q["st_ok"], 1)
            moments_to_rstd(dve, nc, st, mean, gap, rstd, q)
            dve.wait_ge(q["pool_ok"], POOL_SETUP)
            dve.wait_ge(q["pad_ok"], 2)
            dve.wait_ge(q["running_zero"], 1)
            dve.wait_ge(q["rstd_ok"], 1)
            L = ps_l[0:N, 0:QUAD * 72].rearrange("p (b g e) -> p b g e", b=QUAD, g=9)

            def flat(ap):
                return ap.rearrange("p b g e -> p (b g) e")

            def over(ap):
                return ap.rearrange("p b g -> p (b g)").unsqueeze(2).to_broadcast([N, QUAD * 9, EXPERTS])

            def step(t, u, first=False, fresh=False):
                def after(n):
                    dve.wait_ge(q["route_step"], ROUTE_STEPS * t + n)

                def done(inst, n):
                    inst.then_inc(q["route_step"], 1)
                for b in range(QUAD):
                    if not fresh and b == 0:
                        dve.wait_ge(scattered[u], 128 * (t - u))
                    i = bass.ds(QUAD * t + b, 1)
                    nc.vector.tensor_scalar(
                        rows[u][:, b, :, 0:D], r[:, i, :].to_broadcast([N, PICKS, D]),
                        mean[:, i], rstd[:, i], ALU.subtract, ALU.mult).then_inc(*((q["x_ok"], 1) if b == QUAD - 1 else (q["x_part"], 1)))
                nc.vector.tensor_scalar(rows[u][:, :, :, D], place[:, bass.ds(QUAD * t, QUAD), :], 0.0, None,
                                        ALU.add).then_inc(q["place_ok"], 1)
                dve.wait_ge(q["logits"], t + 1)
                if not first:
                    after(0)
                done(nc.vector.tensor_reduce(top[:, 0, :, :].rearrange("p b g -> p (b g)"), flat(L), AX.X, ALU.max), TOP1)
                after(TOP1)
                done(nc.vector.tensor_tensor(flat(below), flat(L), over(top[:, 0]), ALU.subtract), BELOW1)
                after(BELOW1)
                order_b = order[:, :].unsqueeze(1).to_broadcast([N, QUAD * 9, EXPERTS])
                done(nc.vector.scalar_tensor_tensor(out=flat(ranked), in0=flat(below), scalar=0.0, in1=order_b,
                                                    op0=ALU.is_ge, op1=ALU.mult), RANK1)
                after(RANK1)
                done(nc.vector.tensor_reduce(winner_[0], flat(ranked), AX.X, ALU.max), FIRST1)
                after(FIRST1)
                done(nc.vector.tensor_tensor(flat(hot[:, 0]), flat(ranked), over(winner[:, 0]), ALU.is_equal), HOT1)
                after(HOT1)
                done(nc.vector.scalar_tensor_tensor(out=flat(left), in0=flat(hot[:, 0]), scalar=-BIG, in1=flat(L),
                                                    op0=ALU.mult, op1=ALU.add), LEFT)
                after(LEFT)
                done(nc.vector.tensor_reduce(top[:, 1, :, :].rearrange("p b g -> p (b g)"), flat(left), AX.X, ALU.max), TOP2)
                after(TOP2)
                done(nc.vector.tensor_tensor(flat(below), flat(left), over(top[:, 1]), ALU.subtract), BELOW2)
                after(BELOW2)
                done(nc.vector.scalar_tensor_tensor(out=flat(ranked), in0=flat(below), scalar=0.0, in1=order_b,
                                                    op0=ALU.is_ge, op1=ALU.mult), RANK2)
                after(RANK2)
                done(nc.vector.tensor_reduce(winner_[1], flat(ranked), AX.X, ALU.max), FIRST2)
                after(FIRST2)
                done(nc.vector.tensor_tensor(flat(hot[:, 1]), flat(ranked), over(winner[:, 1]), ALU.is_equal), HOT2)
                done(nc.vector.tensor_tensor(margin[:, :, :], top[:, 1], top[:, 0], ALU.subtract), MARGIN)
                dve.wait_ge(q["odds_exp"], t + 1)
                done(nc.vector.tensor_scalar(margin[:, :, :], odds[:, :, :], 1.0, None, ALU.add), ODDS)
                after(ODDS)
                done(nc.vector.reciprocal(part[:, 0], margin[:, :, :]), PART1)
                after(PART1)
                done(nc.vector.tensor_tensor(part[:, 1], odds[:, :, :], part[:, 0], ALU.mult), PART2)
                for a in range(2):
                    for c in range(2):
                        done(nc.vector.tensor_tensor(
                            pair[:, 2 * a + c].rearrange("p b (g e) -> p b g e", g=GROUPS),
                            hot[:, a, :, 0, :].unsqueeze(3).to_broadcast([N, QUAD, GROUPS, EXPERTS]),
                            hot[:, c, :, 1:9, :], ALU.mult), PAIR0 + 2 * a + c)
                done(nc.vector.tensor_tensor(flat(either), flat(hot[:, 0]), flat(hot[:, 1]), ALU.add), EITHER)
                after(EITHER)
                if not first:
                    dve.wait_ge(q["ranks"], t)
                done(nc.vector.tensor_tensor(
                    chosen[:, :, :].rearrange("p b (g e) -> p b g e", g=GROUPS),
                    either[:, :, 0, :].unsqueeze(3).to_broadcast([N, QUAD, GROUPS, EXPERTS]),
                    either[:, :, 1:9, :], ALU.mult), CHOSEN)
                after(PART2)
                for a in range(2):
                    done(nc.vector.tensor_tensor(
                        share[:, a], hot[:, a, :, 0, :].unsqueeze(1).to_broadcast([N, 2, QUAD, GROUPS]),
                        part[:, :, :, 1:9], ALU.mult), SHARE0 + a)
                after(SHARE1)
                done(nc.vector.tensor_reduce(shares[:, :, :].rearrange("p k b -> p (k b)"),
                                             share[:, :, :, :, :].rearrange("p a c b g -> p (a c b) g"),
                                             AX.X, ALU.add), SHARES)
                after(SHARES)
                done(nc.vector.tensor_tensor(
                    weight[:, bass.ds(QUAD * t, QUAD), :].rearrange("p b (a c) -> p a c b", a=2),
                    shares[:, :, :].rearrange("p (a c) b -> p a c b", a=2),
                    part[:, :, :, 0].unsqueeze(2).to_broadcast([N, 2, 2, QUAD]), ALU.mult), WEIGHT)
                after(WEIGHT)
                done(nc.vector.tensor_tensor(
                    weighed[:, :, :, :].rearrange("p k b e -> p k b e"),
                    pair[:, :, :, :],
                    weight[:, bass.ds(QUAD * t, QUAD), :].rearrange("p b k -> p k b").unsqueeze(3).to_broadcast(
                        [N, PICKS, QUAD, GE]), ALU.mult), WEIGHED)
                after(WEIGHED)
                if not fresh:
                    dve.wait_ge(q["gates_turned"], t - 1)
                done(nc.vector.tensor_reduce(gates[u][:, :, :].rearrange("p b e -> p (b e)"),
                                             weighed[:, :, :, :].rearrange("p k b e -> p (b e) k"),
                                             AX.X, ALU.add), GATES)
                dve.wait_ge(q["ranks"], t + 1)
                done(nc.vector.tensor_tensor(
                    slot_row[:, :, :], ps_r[0:N, 0:QUAD * GE].rearrange("p (b e) -> p b e", b=QUAD),
                    region[:, :].unsqueeze(1).to_broadcast([N, QUAD, GE]), ALU.add), SLOTS)
                after(SLOTS)
                done(nc.vector.tensor_tensor(
                    weighed[:, :, :, :].rearrange("p k b e -> p k (b e)"),
                    pair[:, :, :, :].rearrange("p k b e -> p k (b e)"),
                    slot_row[:, :, :].rearrange("p b e -> p (b e)").unsqueeze(1).to_broadcast([N, PICKS, QUAD * GE]),
                    ALU.mult), PLACED)
                after(PLACED)
                done(nc.vector.tensor_reduce(slot_f[:, :, :].rearrange("p k b -> p (k b)"),
                                             weighed[:, :, :, :].rearrange("p k b e -> p (k b) e"),
                                             AX.X, ALU.add), SLOT_OF)
                after(SLOT_OF)
                done(nc.vector.tensor_copy(slot[u][:, :, :], slot_f[:, :, :]), SLOT_INT)
                done(nc.vector.tensor_reduce(added_f[:, :], chosen[:, :, :].rearrange("p b e -> p e b"),
                                             AX.X, ALU.add), ADDED)
                after(ADDED)
                done(nc.vector.tensor_tensor(running[:, :], running[:, :], added_f[:, :], ALU.add), RUNNING)
                dve.wait_ge(q["result"], t + 1)
                here = r[:, bass.ds(QUAD * t, QUAD), :]
                done(nc.vector.tensor_tensor(here, here, ps_b[0:N, :].rearrange("p (b d) -> p b d", b=QUAD),
                                             ALU.add), RESULT)
            winner_ = [winner[:, k].rearrange("p b g -> p (b g)") for k in range(2)]
            step(0, 0, first=True, fresh=True)
            step(1, 1, fresh=True)
            with dve.Fori(1, QUADS // 2) as j:
                for u in range(2):
                    step(2 * j + u, u)
            dve.wait_ge(q["route_step"], ROUTE_STEPS * QUADS)
            nc.vector.tensor_copy(added_f[:, :], running[:, :]).then_inc(q["count_ok"], 1)
            n = 0

            def then(inst):
                nonlocal n
                n += 1
                inst.then_inc(q["table_step"], 1)

            def last():
                dve.wait_ge(q["table_step"], n)
            dve.wait_ge(q["counted"], 1)
            then(nc.vector.tensor_copy(count[:, :], ps_l[0:GE, 0:1]))
            last()
            then(nc.vector.tensor_scalar(count_i[:, :], count[:, :], float(TILE - 1), None, ALU.add))
            last()
            then(nc.vector.tensor_scalar(count_i[:, :], count_i[:, :], 7, None, ALU.arith_shift_right))
            last()
            nc.vector.tensor_copy(tiles[:, :], count_i[:, :]).then_inc(q["tiles_ok"], 1)
            dve.wait_ge(q["ends"], 1)
            then(nc.vector.tensor_copy(bounds[:, 1:2], ps_r[0:GE, 0:1]))
            last()
            then(nc.vector.tensor_tensor(bounds[:, 0:1], bounds[:, 1:2], tiles[:, :], ALU.subtract))
            last()
            then(nc.vector.tensor_scalar(began[:, :], tile_no[:, :], bounds[:, 0:1], None, ALU.is_ge))
            then(nc.vector.tensor_scalar(mine[:, :], tile_no[:, :], bounds[:, 1:2], None, ALU.is_ge))
            last()
            then(nc.vector.tensor_copy(facts[:, 2:3], bounds[:, 0:1]))
            then(nc.vector.tensor_scalar(facts[:, 3:4], count[:, :], float(-TILE), 0.0, ALU.add, ALU.max))
            then(nc.vector.tensor_scalar(facts[:, 1:2], lane[0:GE, :], float(REGION), None, ALU.mult))
            then(nc.vector.tensor_scalar(facts[:, 4:5], lane[0:GE, :], float(HID), None, ALU.mult))
            last()
            nc.vector.tensor_tensor(mine[:, :], began[:, :], mine[:, :], ALU.subtract).then_inc(q["mine_ok"], 1)
            dve.wait_ge(q["spread"], 5)
            used, base = ps_f[0][:, 0:TILES], ps_f[0][:, TILES:2 * TILES]
            start, room = ps_f[1][:, 0:TILES], ps_f[1][:, TILES:2 * TILES]
            then(nc.vector.scalar_tensor_tensor(out=at[:, :], in0=start, scalar=float(-TILE), in1=tile_of[:, :],
                                                op0=ALU.mult, op1=ALU.add))
            then(nc.vector.tensor_scalar(unused[:, :], used, -float(GE * REGION), float(GE * REGION), ALU.mult, ALU.add))
            last()
            then(nc.vector.tensor_tensor(rel[:, :], at[:, :], room, ALU.min))
            last()
            then(nc.vector.tensor_tensor(unused[:, :], unused[:, :], rel[:, :], ALU.add))
            then(nc.vector.tensor_tensor(at[:, :], at[:, :], rel[:, :], ALU.subtract))
            last()
            then(nc.vector.tensor_tensor(tab_base[:, :], unused[0:1, :], base[0:1, :], ALU.add))
            then(nc.vector.tensor_copy(tab_expert[:, :], ps_f[2][0:1, 0:TILES]))
            then(nc.vector.tensor_scalar(tab_skip[:, :], at[:, :], lane[:, 0:1], SKIP, ALU.is_gt, ALU.mult))
            last()


def experts(nc, w1_sb, w2_sb, b1, experts_in, expert_loads, slots_dram, results_dram, tab_base, tab_expert, tab_skip):
    with ExitStack() as ctx:
        def sb(name, shape, dt=F32):
            return ctx.enter_context(nc.sbuf_tensor(name, shape, dt))

        def sem(name):
            return ctx.enter_context(nc.semaphore(name))

        RING = 4
        x = [sb(f"x_e{k}", [TILE, SLOT]) for k in range(RING)]
        y = [sb(f"y_e{k}", [TILE, D]) for k in range(RING)]
        place = [sb(f"place_e{k}", [TILE, 1], I32) for k in range(RING)]
        xT = [sb(f"xT_e{k}", [D, TILE]) for k in range(2)]
        hid = [sb(f"hid_e{k}", [TILE, HID]) for k in range(2)]
        hidT = [sb(f"hidT_e{k}", [D, 2, TILE]) for k in range(2)]
        b1_sb = sb("b1_sb", [GE, HID])
        b1_T = sb("b1_T", [D, 2, GE])
        b1_now = [sb(f"b1_now{k}", [D, 2]) for k in range(2)]
        ident = sb("ident_e", [PART, PART])
        ps_x = [ctx.enter_context(nc.psum_tensor(f"ps_ex{k}", [PART, 512], F32)) for k in range(2)]
        ps_h = [ctx.enter_context(nc.psum_tensor(f"ps_eh{k}", [PART, 512], F32)) for k in range(2)]
        ps_t = [ctx.enter_context(nc.psum_tensor(f"ps_et{k}", [PART, 512], F32)) for k in range(2)]
        ps_y = [ctx.enter_context(nc.psum_tensor(f"ps_ey{k}", [PART, 512], F32)) for k in range(2)]

        names = """b1_in base_ok ident_ok b1_turned b1_ok x_turned xT_ok hid_done hid_ok hid_turned hidT_ok
            y_done y_ok place_ok bias_ok""".split()
        q = {n: sem("e_" + n) for n in names}
        x_in = [sem(f"e_x_in{k}") for k in range(RING)]
        stored = [sem(f"e_stored{k}") for k in range(RING)]
        block = ctx.enter_context(nc.Block())

        @block.sync
        def _(sp):
            sp.dma_start(b1_sb[:, :], b1.rearrange("g e h -> (g e) h")).then_inc(q["b1_in"], 16)

            def load(t, u, fresh):
                base = sp.value_load(tab_base[0:1, bass.ds(t, 1)], min_val=0, max_val=GE * REGION)
                if not fresh:
                    sp.wait_ge(q["x_turned"], t - RING + 1)
                    sp.wait_ge(q["place_ok"], t - RING + 1)
                sp.dma_start(x[u][:, :], slots_dram[bass.ds(base, TILE), :]).then_inc(x_in[u], 16)
            for u in range(RING):
                load(u, u, True)
            with sp.Fori(1, TILES // RING) as j:
                for u in range(RING):
                    load(RING * j + u, u, False)

        def pipeline(eng, body, lead, lag):
            for t in range(-lead, RING):
                body(t, t % RING)
            with eng.Fori(1, TILES // RING - 1) as j:
                for u in range(RING):
                    body(RING * j + u, u)
            for t in range(TILES - RING, TILES + lag):
                body(t, t % RING)

        def has(t):
            return not isinstance(t, int) or 0 <= t < TILES

        def later(t, n):
            return not isinstance(t, int) or t >= n

        @block.gpsimd
        def _(pool):
            nc.gpsimd.memset(ident[:, :], 0.0).then_inc(q["base_ok"], 1)
            pool.wait_ge(q["base_ok"], 1)
            nc.gpsimd.affine_select(out=ident[:, :], in_=ident[:, :], compare_op=ALU.not_equal, fill=1.0,
                                    base=0, pattern=[[-1, PART]], channel_multiplier=1).then_inc(q["ident_ok"], 1)

            def store(t, u):
                pool.wait_ge(q["place_ok"], t + 1)
                pool.wait_ge(q["y_ok"], stores)
                pool.reg_add(stores, stores, 1)
                nc.gpsimd.indirect_dma_start(
                    out=results_dram, out_offset=bass.IndirectOffsetOnAxis(ap=place[u][:, 0:1], axis=0),
                    in_=y[u][:, :], in_offset=None, bounds_check=PICKS * TOKENS - 1,
                    oob_is_err=False).then_inc(stored[u], 16)
            stores = pool.alloc_register("stores")
            pool.reg_mov(stores, 1)
            with pool.Fori(0, TILES // RING) as j:
                for u in range(RING):
                    store(RING * j + u, u)
            for u in range(RING):
                pool.wait_ge(stored[u], 16 * TILES // RING)

        @block.tensor
        def _(pe):
            pe.wait_ge(q["ident_ok"], 1)
            pe.wait_ge(q["b1_in"], 16)
            for half in range(2):
                pe.transpose(ps_t[0][:, GE * half:GE * half + GE], b1_sb[:, D * half:D * half + D],
                             ident[0:GE, 0:GE]).then_inc(q["b1_turned"], 1)
            for k in range(len(experts_in)):
                pe.wait_ge(experts_in[k], 16 * expert_loads)
            pe.wait_ge(q["b1_ok"], 1)

            def body(t, u):
                v = u % 2
                if has(t + 2):
                    a = t + 2
                    pe.wait_ge(x_in[(u + 2) % RING],
                               16 * (a // RING + 1) if isinstance(a, int) else 4 * (t - u) + (16 if u < 2 else 32))
                    if later(a, 2):
                        pe.wait_ge(q["xT_ok"], a - 1)
                    pe.transpose(ps_x[v][:, 0:TILE], x[(u + 2) % RING][:, 0:D], ident[:, :]).then_inc(q["x_turned"], 1)
                if has(t + 1):
                    a, w = t + 1, 1 - v
                    first = pe.value_load(tab_expert[0:1, bass.ds(a, 1)], min_val=0, max_val=(GE - 1) * HID)
                    pe.wait_ge(q["xT_ok"], a + 1)
                    if later(a, 2):
                        pe.wait_ge(q["hid_ok"], a - 1)
                    pe.matmul(ps_h[w][:, 0:HID], xT[w][:, :], w1_sb[:, bass.ds(first, HID)], start=True,
                              stop=True).then_inc(q["hid_done"], 1)
                if has(t):
                    pe.wait_ge(q["hid_ok"], t + 1)
                    if later(t, 2):
                        pe.wait_ge(q["hidT_ok"], 2 * t - 2)
                    for half in range(2):
                        pe.transpose(ps_t[v][:, TILE * half:TILE * half + TILE], hid[v][:, D * half:D * half + D],
                                     ident[:, :]).then_inc(q["hid_turned"], 1)
                if has(t - 1):
                    a, w = t - 1, 1 - v
                    first = pe.value_load(tab_expert[0:1, bass.ds(a, 1)], min_val=0, max_val=(GE - 1) * HID)
                    pe.wait_ge(q["hidT_ok"], 2 * a + 2)
                    if later(a, 2):
                        pe.wait_ge(q["y_ok"], a - 1)
                    for half in range(2):
                        mm = pe.matmul(ps_y[w][:, 0:D], hidT[w][:, half, :], w2_sb[:, bass.ds(first + D * half, D)],
                                       start=(half == 0), stop=(half == 1))
                    mm.then_inc(q["y_done"], 1)
            pipeline(pe, body, 2, 1)

        @block.scalar
        def _(act):
            act.wait_ge(q["b1_turned"], 2)
            nc.scalar.copy(b1_T[:, :, :], ps_t[0][:, 0:2 * GE].rearrange("p (k e) -> p k e", k=2)).then_inc(q["b1_ok"], 1)

            def body(t, u):
                v = u % 2
                if has(t + 2):
                    a = t + 2
                    act.wait_ge(q["x_turned"], a + 1)
                    if later(a, 2):
                        act.wait_ge(q["hid_done"], a - 1)
                    nc.scalar.copy(xT[v][:, :], ps_x[v][:, 0:TILE]).then_inc(q["xT_ok"], 1)
                if has(t):
                    act.wait_ge(q["bias_ok"], t + 1)
                    if later(t, 2):
                        act.wait_ge(q["y_done"], t - 1)
                    act.wait_ge(q["hid_turned"], 2 * t + 2)
                    for half in range(2):
                        nc.scalar.activation(hidT[v][:, half, :], ps_t[v][:, TILE * half:TILE * half + TILE],
                                             ACT.Relu, bias=b1_now[v][:, half:half + 1]).then_inc(q["hidT_ok"], 1)
            pipeline(act, body, 2, 0)

        @block.vector
        def _(dve):
            def body(t, u):
                v = u % 2
                if has(t + 1):
                    a, w = t + 1, 1 - v
                    dve.wait_ge(q["hid_done"], a + 1)
                    if later(a, 2):
                        dve.wait_ge(q["hid_turned"], 2 * a - 2)
                    nc.vector.tensor_copy(hid[w][:, :], ps_h[w][:, 0:HID]).then_inc(q["hid_ok"], 1)
                    first = dve.value_load(tab_expert[0:1, bass.ds(a, 1)], min_val=0, max_val=(GE - 1) * HID)
                    if later(a, 2):
                        dve.wait_ge(q["hidT_ok"], 2 * a - 2)
                    nc.vector.tensor_scalar(b1_now[w][:, :].unsqueeze(2), b1_T[:, :, bass.ds(first // HID, 1)], 0.0, None,
                                            ALU.add).then_inc(q["bias_ok"], 1)
                if has(t):
                    if later(t, RING):
                        dve.wait_ge(stored[u], 4 * (t - u) if not isinstance(t, int) else 16 * (t // RING))
                    nc.vector.tensor_tensor(place[u][:, :], x[u][:, D:D + 1], tab_skip[:, bass.ds(t, 1)],
                                            ALU.add).then_inc(q["place_ok"], 1)
                if has(t - 1):
                    a, w, z = t - 1, 1 - v, (u - 1) % RING
                    dve.wait_ge(q["y_done"], a + 1)
                    if later(a, RING):
                        dve.wait_ge(stored[z], 16 * (a // RING) if isinstance(a, int) else
                                    4 * (t - u) - (16 if u == 0 else 0))
                    nc.vector.tensor_copy(y[z][:, :], ps_y[w][:, 0:D]).then_inc(q["y_ok"], 1)

            dve.wait_ge(q["b1_ok"], 1)
            pipeline(dve, body, 1, 1)


def combine(nc, r, weight, results_dram, out):
    with ExitStack() as ctx:
        def sem(name):
            return ctx.enter_context(nc.semaphore(name))
        parts = [ctx.enter_context(nc.sbuf_tensor(f"parts{k}", [N, PICKS, QUAD, D], F32)) for k in range(2)]
        parts_in = [sem(f"f_parts_in{k}") for k in range(2)]
        summed = sem("f_summed")
        out_ok = sem("f_out_ok")
        block = ctx.enter_context(nc.Block())

        @block.sync
        def _(sp):
            pick = results_dram.rearrange("(k b n) d -> k n b d", k=PICKS, b=B)

            def load(t, u, fresh):
                if not fresh:
                    sp.wait_ge(summed, 16 * t - 16)
                for k in range(PICKS):
                    sp.dma_start(parts[u][:, k, :, :], pick[k, :, bass.ds(QUAD * t, QUAD), :]).then_inc(parts_in[u], 16)
            for u in range(2):
                load(u, u, True)
            with sp.Fori(1, QUADS // 2) as j:
                for u in range(2):
                    load(2 * j + u, u, False)

        @block.scalar
        def _(act):
            with act.Fori(0, QUADS) as t:
                act.wait_ge(summed, 16 * t + 16)
                act.dma_start(out[bass.ds(QUAD * t, QUAD)].rearrange("b n d -> n b d"),
                              r[:, bass.ds(QUAD * t, QUAD), :]).then_inc(out_ok, 16)
            act.wait_ge(out_ok, 16 * QUADS)

        @block.vector
        def _(dve):
            def add(t, u):
                dve.wait_ge(parts_in[u], 32 * (t - u) + 64)
                for k in range(PICKS):
                    for b in range(QUAD):
                        i = bass.ds(QUAD * t + b, 1)
                        at = r[:, i, :].rearrange("p o d -> p (o d)")
                        if k > 0:
                            dve.wait_ge(summed, 16 * t + 4 * (k - 1) + b + 1)
                        nc.vector.scalar_tensor_tensor(
                            out=at, in0=parts[u][:, k, b, :], scalar=weight[:, i, k:k + 1].rearrange("p o k -> p (o k)"),
                            in1=at, op0=ALU.mult, op1=ALU.add).then_inc(summed, 1)
            with dve.Fori(0, QUADS // 2) as j:
                for u in range(2):
                    add(2 * j + u, u)


def early_fusion(nc, args, out):
    (x, txt, conv_w, conv_b, gamma, beta, dense_w, dense_b, w_qkv, b_qkv, w_out, b_out, p_coeff, q_coeff, cema_gamma,
     adaptive, g1, g2, w1, b1, w2, b2) = args
    h_dram = nc.dram_tensor("image_tokens", [B, PATCHES, D], F32, kind="Internal").ap()
    response = nc.dram_tensor("impulse_response", [D, KPAD], F32, kind="Internal").ap()
    slots_dram = nc.dram_tensor("expert_slots", [(GE + 1) * REGION, SLOT], F32, kind="Internal").ap()
    results_dram = nc.dram_tensor("expert_results", [PICKS * TOKENS, D], F32, kind="Internal").ap()
    patch_tokens(nc, x, conv_w, conv_b, gamma, beta, dense_w, dense_b, h_dram)
    with ExitStack() as ctx:
        def sb(name, shape, dt=F32):
            return ctx.enter_context(nc.sbuf_tensor(name, shape, dt))
        r = sb("r", [N, B, D])
        w1_sb = sb("w1_sb", [D, GE * HID])
        w2_sb = sb("w2_sb", [D, GE * HID])
        experts_in = [ctx.enter_context(nc.semaphore(f"experts_in{k}")) for k in range(2)]

        def fetch_experts(sp):
            for g in range(GROUPS):
                cols = slice(g * EXPERTS * HID, (g + 1) * EXPERTS * HID)
                sp.dma_start(w1_sb[:, cols].rearrange("d (e h) -> d e h", e=EXPERTS),
                             w1[g].rearrange("e d h -> d e h")).then_inc(experts_in[0], 16)
                sp.dma_start(w2_sb[:, cols].rearrange("p (k d) -> p k d", d=D),
                             w2[g].rearrange("e (k p) d -> p (e k) d", p=D)).then_inc(experts_in[1], 16)
        attention(nc, h_dram, txt, w_qkv, b_qkv, w_out, b_out, p_coeff, q_coeff, cema_gamma, adaptive, response, r,
                  fetch_experts)
        weight = sb("weight", [N, B, PICKS])
        tab_base = sb("tab_base", [1, TILES], I32)
        tab_expert = sb("tab_expert", [1, TILES], I32)
        tab_skip = sb("tab_skip", [PART, TILES])
        route(nc, r, g1, g2, b2, slots_dram, weight, tab_base, tab_expert, tab_skip)
        experts(nc, w1_sb, w2_sb, b1, experts_in, GROUPS, slots_dram, results_dram, tab_base, tab_expert, tab_skip)
        combine(nc, r, weight, results_dram, out)


_INS = ['x', 'txt', 'L0_tok_conv_w', 'L0_tok_conv_b', 'L0_tok_gamma', 'L0_tok_beta', 'L0_tok_dense_w',
        'L0_tok_dense_b', 'L0_attn_W_qkv', 'L0_attn_b_qkv', 'L0_attn_W_out', 'L0_attn_b_out', 'L0_attn_p_coeff',
        'L0_attn_q_coeff', 'L0_attn_gamma', 'L0_attn_adaptive_weights', 'L0_ffn_g1', 'L0_ffn_g2', 'L0_ffn_W1',
        'L0_ffn_b1', 'L0_ffn_W2', 'L0_ffn_b2']


def kernel(**inputs):
    import numpy as _np
    import concourse.bacc as _bacc
    from concourse import mybir as _mybir
    from concourse.bass_utils import run_bass_kernel_spmd as _run

    nc = _bacc.Bacc("TRN2", target_bir_lowering=False, num_devices=1)
    arrays, args = {}, []
    for name in _INS:
        a = _np.ascontiguousarray(inputs[name])
        arrays[f"in_{name}_dram"] = a
        args.append(nc.dram_tensor(f"in_{name}_dram", a.shape, _mybir.dt.from_np(a.dtype), kind="ExternalInput").ap())
    out = nc.dram_tensor("out_dram", (B, N, D), _mybir.dt.float32, kind="ExternalOutput").ap()
    early_fusion(nc, args, out)
    r = _run(nc, [arrays], core_ids=[0])
    return r.results[0]["out_dram"]
```

```python
from contextlib import ExitStack

import concourse.bass as bass
from concourse import mybir

ALU = mybir.AluOpType
ACT = mybir.ActivationFunctionType
AX = mybir.AxisListType
F32 = mybir.dt.float32
I32 = mybir.dt.int32

PART = 128
B, IMG, C = 32, 112, 3
P = 16
G = IMG // P
PATCHES = G * G
TXT = 32
N = PATCHES + TXT
D = 128
ROWLEN = (IMG + 2) * C
TOK_EPS, LN_EPS = 1e-3, 1e-5

W_LOADS = 6 + 16 + 5

TILE_ROWS = [4, 3]
TILE_PARTS = [B * r for r in TILE_ROWS]
KT = [128] * 6 + [96, 96]
KCOLS = sum(KT)
KOFF = [sum(KT[:m]) for m in range(8)]
SIDES = 6 * 128
ENDS = SIDES + 96


def strided(ap, dims):
    return bass.AP(ap.tensor, ap.offset, [ap.ap[0]] + [list(d) for d in dims])


def patch_tokens(nc, x, conv_w, conv_b, gamma, beta, dense_w, dense_b, h_dram):
    with ExitStack() as ctx:
        def sb(name, shape, dt=F32):
            return ctx.enter_context(nc.sbuf_tensor(name, shape, dt))

        def psum(name, shape, dt=F32):
            return ctx.enter_context(nc.psum_tensor(name, shape, dt))

        def sem(name):
            return ctx.enter_context(nc.semaphore(name))

        image = [sb(f"image{k}", [PART, P + 2, ROWLEN]) for k in range(2)]
        patch = [sb(f"patch{k}", [PART, KCOLS]) for k in range(2)]
        patch_T = [sb(f"patch_T{k}", [PART, 8, 128]) for k in range(2)]
        w_src = sb("w_src", [PART, 5, 6, D])
        w_edge = sb("w_edge", [97, 2, D])
        y = sb("y", [PART, 2, G, D])
        stats = sb("stats", [PART, 2, 6])
        moments = sb("moments", [PART, 2, 2])
        rstd = sb("rstd", [PART, 2, G])
        half = sb("half", [PART, 2, G])
        normed = [sb(f"normed{k}", [PART, D]) for k in range(2)]
        normed_T = [sb(f"normed_T{k}", [PART, D]) for k in range(2)]
        token = [sb(f"token{k}", [PART, D]) for k in range(2)]
        dense_sb = sb("dense_sb", [D, D])
        dense_b_row = sb("dense_b_row", [PART, D])
        gamma_col = sb("gamma_col", [D, 1])
        beta_col = sb("beta_col", [D, 1])
        ident = sb("ident_a", [PART, PART])

        ps_T = [psum(f"ps_T{k}", [PART, 8, 128]) for k in range(2)]
        ps_y = [psum(f"ps_y{k}", [PART, 512]) for k in range(2)]
        ps_n = [psum(f"ps_n{k}", [PART, 512]) for k in range(2)]

        borders_zero = sem("borders_zero")
        image_in = [sem(f"image_in{k}") for k in range(2)]
        w_zero = sem("w_zero")
        w_in = sem("w_in")
        w_sum = sem("w_sum")
        small_in = sem("small_in")
        ident_ok = sem("ident_ok")
        patch_ok = sem("patch_ok")
        patch_read = sem("patch_read")
        transposed = sem("transposed")
        left_half = sem("left_half")
        right_half = sem("right_half")
        conv_ok = sem("conv_ok")
        y_ok = sem("y_ok")
        stats_ok = sem("stats_ok")
        moments_ok = sem("moments_ok")
        rstd_ok = sem("rstd_ok")
        rstd_pow = sem("rstd_pow")
        ones_ok = sem("ones_ok")
        sides_ok = sem("sides_ok")
        normed_ok = sem("normed_ok")
        normed_turned = sem("normed_turned")
        normed_T_ok = sem("normed_T_ok")
        dense_ok = sem("dense_ok")
        token_ok = sem("token_ok")
        stored = [sem(f"stored{k}") for k in range(2)]

        block = ctx.enter_context(nc.Block())

        @block.sync
        def _(sp):
            sp.wait_ge(borders_zero, 6)
            for k in range(2):
                for r in range(TILE_ROWS[k]):
                    pr = 4 * k + r
                    lo, hi = max(P * pr - 1, 0), min(P * pr + P + 1, IMG)
                    first = lo - (P * pr - 1)
                    sp.dma_start(image[k][B * r:B * r + B, first:first + hi - lo, C:C + IMG * C],
                                 x[:, lo:hi, :, :].rearrange("b i j c -> b i (j c)")).then_inc(image_in[k], 16)
            def store(pc, k, t):
                sp.wait_ge(token_ok, t + 1)
                rows = h_dram.rearrange("b (r c) d -> c r b d", c=G)
                sp.dma_start(rows[bass.ds(pc, 1), 4 * k:4 * k + TILE_ROWS[k]].rearrange("o r b d -> (o r) b d"),
                             token[k][0:TILE_PARTS[k], :]).then_inc(stored[k], 16)
            with sp.Fori(0, G) as pc:
                for k in range(2):
                    store(pc, k, 2 * pc + k)
            for k in range(2):
                sp.wait_ge(stored[k], 16 * G)

        @block.scalar
        def _(act):
            w5 = conv_w.rearrange("i j (s c) d -> s j i (c d)", s=5)
            act.wait_ge(w_zero, 1)
            for hf in range(2):
                j0, mine = 8 * hf, slice(3 * hf, 3 * hf + 3)
                act.dma_start(w_src[:, 0, mine, :], w5[0, j0:j0 + 8]).then_inc(w_in, 16)
                n, none = 8 - hf, 1 - hf
                act.dma_start(w_src[0:16 * n, 1, mine, :], w5[1, j0 + 1:j0 + 1 + n]).then_inc(w_in, 16)
                act.dma_start(w_src[16 * none:128, 2, mine, :], w5[2, j0 - 1 + none:j0 + 7]).then_inc(w_in, 16)
            for jl in range(8):
                for s, (p0, i0) in ((3, (0, 1)), (4, (1, 0))):
                    act.dma_start(
                        w_src[16 * jl + p0:16 * jl + p0 + 15, s, :, :].rearrange("i (h c) d -> i h (c d)", h=2),
                        conv_w[i0:i0 + 15, jl:16:8, 3 * s:3 * s + 3, :].rearrange("i h c d -> i h (c d)"),
                    ).then_inc(w_in, 16)
            act.dma_start(w_edge[0:48, 0, :], conv_w[:, 0, 3:6, :].rearrange("i c d -> c i d")).then_inc(w_in, 16)
            act.dma_start(w_edge[48:96, 0, :], conv_w[:, 15, 6:9, :].rearrange("i c d -> c i d")).then_inc(w_in, 16)
            act.dma_start(w_edge[0:48, 1, :], conv_w[0, :, 9:12, :].rearrange("j c d -> c j d")).then_inc(w_in, 16)
            act.dma_start(w_edge[48:96, 1, :], conv_w[15, :, 12:15, :].rearrange("j c d -> c j d")).then_inc(w_in, 16)
            act.dma_start(w_edge[96:97, 0, :], conv_b.rearrange("(o d) -> o d", o=1)).then_inc(w_in, 16)
            act.dma_start(dense_b_row[:, :], dense_b.partition_broadcast(PART)).then_inc(small_in, 16)
            act.dma_start(dense_sb[:, :], dense_w).then_inc(small_in, 16)
            act.dma_start(gamma_col[:, :], gamma.rearrange("(d o) -> d o", o=1)).then_inc(small_in, 16)
            act.dma_start(beta_col[:, :], beta.rearrange("(d o) -> d o", o=1)).then_inc(small_in, 16)

            def first_half(k, t, first):
                act.wait_ge(transposed, t + 1)
                if not first:
                    act.wait_ge(conv_ok, t - 1)
                nk = TILE_PARTS[k]
                nc.scalar.copy(patch_T[k][:, 0:4, 0:nk], ps_T[k][:, 0:4, 0:nk]).then_inc(left_half, 1)
            for k in range(2):
                first_half(k, k, True)
            with act.Fori(1, G) as pc:
                for k in range(2):
                    first_half(k, 2 * pc + k, False)

            def scaled(k, t, first):
                act.wait_ge(normed_turned, t + 1)
                if not first:
                    act.wait_ge(dense_ok, t - 1)
                nk = TILE_PARTS[k]
                nc.scalar.activation(normed_T[k][:, 0:nk], ps_n[k][:, 0:nk], ACT.Identity,
                                     bias=beta_col[:, 0:1], scale=gamma_col[:, 0:1]).then_inc(normed_T_ok, 1)
            act.wait_ge(small_in, 64)
            for k in range(2):
                scaled(k, k, True)
            with act.Fori(1, G) as pc:
                for k in range(2):
                    scaled(k, 2 * pc + k, False)

        @block.gpsimd
        def _(pool):
            nc.gpsimd.memset(ident[:, :], 0.0).then_inc(ident_ok, 1)
            nc.gpsimd.memset(half[:, :, :], -0.5).then_inc(ident_ok, 1)
            pool.wait_ge(ident_ok, 2)
            nc.gpsimd.affine_select(out=ident[:, :], in_=ident[:, :], compare_op=ALU.not_equal, fill=1.0,
                                    base=0, pattern=[[-1, PART]], channel_multiplier=1).then_inc(ident_ok, 1)

            def gather(pc, k, t, first):
                if not first:
                    pool.wait_ge(patch_read, t - 1)
                nk = TILE_PARTS[k]
                rows = image[k][0:nk, :, :].rearrange("p i f -> p (i f)")
                for hf in range(2):
                    inner = rows[:, bass.ds(pc * (P * C) + ROWLEN + C + 8 * C * hf, 1)]
                    nc.gpsimd.tensor_copy(
                        patch[k][0:nk, 384 * hf:384 * hf + 384].rearrange("p (c j i) -> p c j i", c=C, i=P),
                        strided(inner, [[1, C], [C, 8], [ROWLEN, P]])).then_inc(patch_ok, 1)
                beside = rows[:, bass.ds(pc * (P * C) + ROWLEN, 1)]
                nc.gpsimd.tensor_copy(
                    patch[k][0:nk, SIDES:ENDS].rearrange("p (s c i) -> p s c i", s=2, c=C),
                    strided(beside, [[(P + 1) * C, 2], [1, C], [ROWLEN, P]])).then_inc(patch_ok, 1)
                ends = rows[:, bass.ds(pc * (P * C) + C, 1)]
                nc.gpsimd.tensor_copy(
                    patch[k][0:nk, ENDS:KCOLS].rearrange("p (r c j) -> p r c j", r=2, c=C),
                    strided(ends, [[(P + 1) * ROWLEN, 2], [1, C], [C, P]])).then_inc(patch_ok, 1)
            for k in range(2):
                pool.wait_ge(image_in[k], 16 * TILE_ROWS[k])
                gather(0, k, k, True)
            with pool.Fori(1, G) as pc:
                for k in range(2):
                    gather(pc, k, 2 * pc + k, False)
            pool.wait_ge(rstd_ok, 1 + 2 * G)
            nc.gpsimd.tensor_tensor(rstd[:, :, :], rstd[:, :, :], half[:, :, :], ALU.pow).then_inc(rstd_pow, 1)

        @block.tensor
        def _(pe):
            def turn(k, t):
                pe.wait_ge(patch_ok, 4 * t + 4)
                nk = TILE_PARTS[k]
                for m in range(8):
                    last = pe.transpose(ps_T[k][0:KT[m], m, 0:nk], patch[k][0:nk, KOFF[m]:KOFF[m] + KT[m]],
                                        ident[0:nk, 0:nk])
                    if m == 3:
                        last.then_inc(transposed, 1)
                last.then_inc(patch_read, 1)

            def convolve(k, t, first):
                nk = TILE_PARTS[k]
                if not first:
                    pe.wait_ge(y_ok, t - 1)
                for m in range(8):
                    if m == 0:
                        pe.wait_ge(left_half, t + 1)
                    if m == 4:
                        pe.wait_ge(right_half, 2 * t + 2)
                    w = w_src[:, 0, m, :] if m < 6 else w_edge[0:(97 if m == 6 else 96), m - 6, :]
                    kk = 97 if m == 6 else KT[m]
                    last = pe.matmul(ps_y[k][0:nk, 0:D], patch_T[k][0:kk, m, 0:nk], w,
                                     start=(m == 0), stop=(m == 7))
                last.then_inc(conv_ok, 1)

            pe.wait_ge(ident_ok, 3)
            turn(0, 0)
            turn(1, 1)
            pe.wait_ge(w_in, 16 * W_LOADS)
            pe.wait_ge(w_sum, 4)
            pe.wait_ge(ones_ok, 2)
            convolve(0, 0, True)
            turn(0, 2)
            convolve(1, 1, True)
            with pe.Fori(1, G - 1) as pc:
                turn(1, 2 * pc + 1)
                convolve(0, 2 * pc, False)
                turn(0, 2 * pc + 2)
                convolve(1, 2 * pc + 1, False)
            turn(1, 2 * G - 1)
            convolve(0, 2 * G - 2, False)
            convolve(1, 2 * G - 1, False)

            def turn_normed(k, t, first):
                pe.wait_ge(normed_ok, t + 1)
                if not first:
                    pe.wait_ge(normed_T_ok, t - 1)
                nk = TILE_PARTS[k]
                pe.transpose(ps_n[k][:, 0:nk], normed[k][0:nk, :], ident[0:nk, 0:nk]).then_inc(normed_turned, 1)

            def dense(k, t):
                pe.wait_ge(normed_T_ok, t + 1)
                pe.wait_ge(token_ok, t - 1)
                nk = TILE_PARTS[k]
                pe.matmul(ps_y[k][0:nk, 0:D], normed_T[k][:, 0:nk], dense_sb[:, :],
                          start=True, stop=True).then_inc(dense_ok, 1)

            def dense_first(k, t):
                pe.wait_ge(y_ok, 2 * G)
                pe.wait_ge(small_in, 64)
                pe.wait_ge(normed_T_ok, t + 1)
                nk = TILE_PARTS[k]
                pe.matmul(ps_y[k][0:nk, 0:D], normed_T[k][:, 0:nk], dense_sb[:, :],
                          start=True, stop=True).then_inc(dense_ok, 1)
            turn_normed(0, 0, True)
            turn_normed(1, 1, True)
            dense_first(0, 0)
            turn_normed(0, 2, False)
            dense_first(1, 1)
            with pe.Fori(1, G - 1) as pc:
                turn_normed(1, 2 * pc + 1, False)
                dense(0, 2 * pc)
                turn_normed(0, 2 * pc + 2, False)
                dense(1, 2 * pc + 1)
            turn_normed(1, 2 * G - 1, False)
            dense(0, 2 * G - 2)
            dense(1, 2 * G - 1)

        @block.vector
        def _(dve):
            for k in range(2):
                nc.vector.memset(image[k][:, 1:P + 1, 0:C], 0.0).then_inc(borders_zero, 1)
                nc.vector.memset(image[k][:, 1:P + 1, ROWLEN - C:ROWLEN], 0.0).then_inc(borders_zero, 1)
            nc.vector.memset(image[0][0:B, 0, :], 0.0).then_inc(borders_zero, 1)
            nc.vector.memset(image[1][2 * B:3 * B, P + 1, :], 0.0).then_inc(borders_zero, 1)
            nc.vector.memset(w_src[:, 1:5, :, :], 0.0).then_inc(w_zero, 1)
            nc.vector.memset(rstd[:, :, :], 1.0).then_inc(rstd_ok, 1)
            for k in range(2):
                nc.vector.memset(patch_T[k][96:97, 6, :], 1.0).then_inc(ones_ok, 1)
            dve.wait_ge(w_in, 16 * W_LOADS)
            for s in range(1, 5):
                if s > 1:
                    dve.wait_ge(w_sum, s - 1)
                nc.vector.tensor_tensor(w_src[:, 0, :, :], w_src[:, 0, :, :], w_src[:, s, :, :],
                                        ALU.add).then_inc(w_sum, 1)

            def second_half(k, t, first):
                dve.wait_ge(patch_read, t + 1)
                if not first:
                    dve.wait_ge(conv_ok, t - 1)
                nk = TILE_PARTS[k]
                nc.vector.tensor_copy(patch_T[k][:, 4:6, 0:nk], ps_T[k][:, 4:6, 0:nk]).then_inc(right_half, 1)
                nc.vector.tensor_copy(patch_T[k][0:96, 6:8, 0:nk], ps_T[k][0:96, 6:8, 0:nk]).then_inc(right_half, 1)

            def moment(pc, k, t):
                nk = TILE_PARTS[k]
                dve.wait_ge(conv_ok, t + 1)
                nc.vector.bn_stats(stats[0:nk, k, :], ps_y[k][0:nk, 0:D]).then_inc(stats_ok, 1)
                dve.wait_ge(ones_ok, 2)
                dve.wait_ge(stats_ok, t + 1)
                nc.vector.bn_aggr(moments[0:nk, k, :], stats[0:nk, k, :]).then_inc(moments_ok, 1)
                dve.wait_ge(moments_ok, t + 1)
                here = y[0:nk, k, bass.ds(pc, 1), :].rearrange("p o d -> p (o d)")
                nc.vector.tensor_scalar(here, ps_y[k][0:nk, 0:D], moments[0:nk, k, 0:1], None,
                                        ALU.subtract).then_inc(y_ok, 1)
                nc.vector.tensor_scalar(rstd[0:nk, k, bass.ds(pc, 1)], moments[0:nk, k, 1:2], TOK_EPS, None,
                                        ALU.add).then_inc(rstd_ok, 1)

            dve.wait_ge(rstd_ok, 1)
            second_half(0, 0, True)
            second_half(1, 1, True)
            moment(0, 0, 0)
            second_half(0, 2, False)
            moment(0, 1, 1)
            with dve.Fori(1, G - 1) as pc:
                second_half(1, 2 * pc + 1, False)
                moment(pc, 0, 2 * pc)
                second_half(0, 2 * pc + 2, False)
                moment(pc, 1, 2 * pc + 1)
            second_half(1, 2 * G - 1, False)
            moment(G - 1, 0, 2 * G - 2)
            moment(G - 1, 1, 2 * G - 1)
            dve.wait_ge(rstd_pow, 1)
            dve.wait_ge(small_in, 64)

            def normalise(pc, k, t, first):
                if not first:
                    dve.wait_ge(normed_turned, t - 1)
                nk = TILE_PARTS[k]
                here = y[0:nk, k, bass.ds(pc, 1), :].rearrange("p o d -> p (o d)")
                scale = rstd[0:nk, k, bass.ds(pc, 1)]
                nc.vector.tensor_scalar(normed[k][0:nk, :], here, scale, None, ALU.mult).then_inc(normed_ok, 1)

            def add_bias(pc, k, t, first):
                dve.wait_ge(dense_ok, t + 1)
                if not first:
                    dve.wait_ge(stored[k], 16 * pc)
                nk = TILE_PARTS[k]
                nc.vector.tensor_tensor(token[k][0:nk, :], ps_y[k][0:nk, 0:D], dense_b_row[0:nk, :],
                                        ALU.add).then_inc(token_ok, 1)
            normalise(0, 0, 0, True)
            normalise(0, 1, 1, True)
            normalise(1, 0, 2, False)
            add_bias(0, 0, 0, True)
            normalise(1, 1, 3, False)
            add_bias(0, 1, 1, True)
            with dve.Fori(1, G - 1) as pc:
                for k in range(2):
                    normalise(pc + 1, k, 2 * pc + 2 + k, False)
                    add_bias(pc, k, 2 * pc + k, False)
            for k in range(2):
                add_bias(G - 1, k, 2 * G - 2 + k, False)


HEADS, DK = 8, 16
HALF = HEADS // 2
CHUNK = 16
CHUNKS = D // CHUNK
NDIM = 16
KPAD = 2 * N - 1

MIX_MAX, MIX_SUB, MIX_EXP, MIX_SUM, MIX_INV, MIX_OK = range(1, 7)


def attention(nc, h_dram, txt, w_qkv, b_qkv, w_out, b_out, p_coeff, q_coeff, gamma, adaptive, response, r,
              fetch_experts):
    with ExitStack() as ctx:
        def sb(name, shape, dt=F32):
            return ctx.enter_context(nc.sbuf_tensor(name, shape, dt))

        def sem(name):
            return ctx.enter_context(nc.semaphore(name))

        xn = sb("xn", [N, B, D])
        ident = sb("ident_c", [PART, PART])
        wide = sb("wide", [D, 3 * D])
        wout_sb = sb("wout_sb", [D, D])
        b_cols = sb("b_cols", [D, 3])
        bout_row = sb("bout_row", [N, D])
        bias = sb("bias", [N, D])
        mask = sb("mask", [N, N])
        head_of = sb("head_of", [D, HEADS])
        mix = sb("mix", [PART, 2])
        mix_s = sb("mix_s", [PART, 3])
        coeff = sb("coeff", [D, 3, NDIM])
        powers = sb("powers", [D, N, NDIM])
        resp = sb("resp", [D, KPAD])
        hankel = [powers[0:N, :, :].rearrange("p n d -> p (n d)").rearrange("p (e n) -> p e n", e=CHUNK),
                  sb("hankel", [N, CHUNK, N])]
        toeplitz = [sb(f"toeplitz{k}", [N, CHUNK, N]) for k in range(2)]
        st = sb("st", [N, B, 6])
        mean = sb("mean", [N, B])
        gap = sb("gap", [N, B])
        rstd = sb("rstd_c", [N, B])
        half = sb("half_c", [N, B])
        xr = [sb(f"xr{k}", [N, D]) for k in range(2)]
        xT = [sb(f"xT{k}", [D, N]) for k in range(2)]
        qT = sb("qT", [D, N])
        kx = sb("kx", [D, HEADS, N])
        vx = [sb(f"vx{k}", [N, HEADS, DK + 1]) for k in range(2)]
        prob = [sb(f"prob{k}", [N, HEADS, N]) for k in range(2)]
        top = [sb(f"top{k}", [N, HEADS]) for k in range(2)]
        probT = [toeplitz[1][:, HEADS * k:HEADS * k + HEADS, :] for k in range(2)]
        inv = [sb(f"inv{k}", [N, HEADS]) for k in range(2)]
        on = [sb(f"on{k}", [N, D]) for k in range(2)]
        oT = [sb(f"oT{k}", [D, N]) for k in range(2)]

        def banks(name, n=1):
            return ctx.enter_context(nc.psum_tensor(name, [PART, n, 512], F32))
        ps_s = banks("ps_s", 2)
        ps_p = banks("ps_p", 2)
        ps_k, ps_x, ps_v, ps_o = banks("ps_k"), banks("ps_x"), banks("ps_v"), banks("ps_o")
        S = ps_s[0:N, :, 0:HALF * N].rearrange("p a (h j) -> p a h j", h=HALF)
        O = ps_o[0:N, 0, 0:HEADS * (DK + 1)].rearrange("p (h d) -> p h d", h=HEADS)
        OT = ps_o[:, 0, 160:160 + N]
        W = ps_o[0:N, 0, 256:256 + D]

        names = """setup_pool half_ok h_in small_in coeff_in adapt_in mix_step bv_done bias_ok bias_w r_base st_ok
            m_gap m_ok var_ok rstd_ok xn_ok pow_ok resp_zero resp_ok resp_out q_sq cema_done cema_added
            xr_ok x_turned xT_ok k_done q_done v_done q_ok k_ok v_ok s_half s_done s_masked s_max s_sub p_ok p_turned pT_ok
            o_done o_inv o_ok o_turned oT_ok w_done r_ok vx_one""".split()
        q = {n: sem("c_" + n) for n in names}
        toeplitz_ok = [sem(f"c_toeplitz_ok{k}") for k in range(2)]
        hankel_in = [sem(f"c_hankel_in{k}") for k in range(2)]
        block = ctx.enter_context(nc.Block())

        SETUP_DMAS = 6
        SETUP_POOL = 7

        @block.sync
        def _(sp):
            sp.dma_start(xn[0:PATCHES, :, :], h_dram.rearrange("b n d -> n b d")).then_inc(q["h_in"], 16)
            sp.dma_start(xn[PATCHES:N, :, :], txt.rearrange("b n d -> n b d")).then_inc(q["h_in"], 16)
            sp.wait_ge(q["resp_out"], 16)

            def load(c, k, first):
                if not first:
                    sp.wait_ge(toeplitz_ok[k], (c - k) // 2 if isinstance(c, int) else 0)
                start = response[bass.ds(c * CHUNK, 1), 0:1]
                sp.dma_start(hankel[k][:, :, :], bass.AP(start.tensor, start.offset, [[1, N], [KPAD, CHUNK], [1, N]])
                             ).then_inc(hankel_in[k], 16)
            for c in range(CHUNKS):
                load(c, c % 2, c < 2)
            fetch_experts(sp)

        @block.scalar
        def _(act):
            act.dma_start(coeff[:, 0, :], p_coeff).then_inc(q["coeff_in"], 16)
            act.dma_start(coeff[:, 1, :], q_coeff).then_inc(q["coeff_in"], 16)
            act.dma_start(coeff[:, 2, :], gamma).then_inc(q["coeff_in"], 16)
            act.dma_start(mix[:, :], adaptive.partition_broadcast(PART)).then_inc(q["adapt_in"], 16)
            act.dma_start(wide[:, :], w_qkv).then_inc(q["small_in"], 16)
            act.dma_start(wout_sb[:, :], w_out).then_inc(q["small_in"], 16)
            for a in range(3):
                act.dma_start(b_cols[:, a:a + 1], b_qkv[a * D:a * D + D].rearrange("(n o) -> n o", o=1)
                              ).then_inc(q["small_in"], 16)
            act.dma_start(bout_row[:, :], b_out.partition_broadcast(N)).then_inc(q["small_in"], 16)
            act.wait_ge(q["mix_step"], MIX_SUB)
            nc.scalar.activation(mix[:, :], mix[:, :], ACT.Exp).then_inc(q["mix_step"], 1)
            act.wait_ge(q["resp_ok"], 1)
            act.dma_start(response, resp[:, :]).then_inc(q["resp_out"], 16)

            def reverse(c, k, first):
                act.wait_ge(hankel_in[k], 8 * (c - k) + 16)
                if not first:
                    act.wait_ge(q["cema_done"], c - 1)
                nc.scalar.copy(toeplitz[k][:, :, :], strided(hankel[k][:, 0, N - 1:N], [[N, CHUNK], [-1, N]])
                               ).then_inc(toeplitz_ok[k], 1)
            for k in range(2):
                reverse(k, k, True)
            with act.Fori(1, CHUNKS // 2) as j:
                for k in range(2):
                    reverse(2 * j + k, k, False)

            def x_out(f, u, first):
                act.wait_ge(q["x_turned"], f + 1)
                if not first:
                    act.wait_ge(q["v_done"], f - 1)
                nc.scalar.copy(xT[u][:, :], ps_x[:, 0, 0:N]).then_inc(q["xT_ok"], 1)

            def q_out(f, fresh):
                act.wait_ge(q["q_done"], f + 1)
                if not fresh:
                    act.wait_ge(q["s_done"], f)
                nc.scalar.activation(qT[:, :], ps_x[:, 0, N:2 * N], ACT.Identity, bias=b_cols[:, 0:1]
                                     ).then_inc(q["q_ok"], 1)

            def v_out(f, u, first):
                act.wait_ge(q["v_done"], f + 1)
                if not first:
                    act.wait_ge(q["o_done"], f - 1)
                nc.scalar.copy(vx[u][:, :, 0:DK],
                               ps_v[0:N, 0, 0:D].rearrange("p (h d) -> p h d", h=HEADS)).then_inc(q["v_ok"], 1)

            def exponent(i, u):
                act.wait_ge(q["s_sub"], i + 1)
                nc.scalar.activation(prob[u][:, :, :], prob[u][:, :, :], ACT.Exp).then_inc(q["p_ok"], 1)

            def probs_out(i, u, first):
                for hf in range(2):
                    act.wait_ge(q["p_turned"], 2 * i + 1 + hf)
                    if not first:
                        act.wait_ge(q["o_done"], i - 1)
                    nc.scalar.copy(probT[u][:, HALF * hf:HALF * hf + HALF, :],
                                   ps_p[0:N, hf, 0:HALF * N].rearrange("p (h j) -> p h j", h=HALF)
                                   ).then_inc(q["pT_ok"], 1)

            def o_out(i, u, first):
                act.wait_ge(q["o_turned"], i + 1)
                if not first:
                    act.wait_ge(q["w_done"], i - 1)
                nc.scalar.copy(oT[u][:, :], OT).then_inc(q["oT_ok"], 1)

            def step(i, u, first=False, front=True, following=True):
                if front:
                    x_out(i + 2, u, False)
                probs_out(i, u, first)
                if front:
                    q_out(i + 2, False)
                    v_out(i + 2, u, False)
                o_out(i, u, first)
                if following:
                    exponent(i + 1, 1 - u)
            for u in range(2):
                x_out(u, u, True)
                q_out(u, u == 0)
                v_out(u, u, True)
            exponent(0, 0)
            for u in range(2):
                step(u, u, first=True)
            with act.Fori(1, B // 2 - 1) as j:
                for u in range(2):
                    step(2 * j + u, u)
            step(B - 2, 0, front=False)
            step(B - 1, 1, front=False, following=False)

        @block.gpsimd
        def _(pool):
            nc.gpsimd.memset(ident[:, :], 0.0).then_inc(q["setup_pool"], 1)
            nc.gpsimd.memset(mask[:, :], DK ** -0.5).then_inc(q["setup_pool"], 1)
            nc.gpsimd.memset(head_of[:, :], 1.0).then_inc(q["setup_pool"], 1)
            nc.gpsimd.memset(half[:, :], -0.5).then_inc(q["half_ok"], 1)
            pool.wait_ge(q["setup_pool"], 3)
            nc.gpsimd.affine_select(out=head_of[:, :], in_=head_of[:, :], compare_op=ALU.is_ge, fill=0.0,
                                    base=0, pattern=[[-DK, HEADS]], channel_multiplier=1).then_inc(q["setup_pool"], 1)
            nc.gpsimd.affine_select(out=ident[:, :], in_=ident[:, :], compare_op=ALU.not_equal, fill=1.0,
                                    base=0, pattern=[[-1, PART]], channel_multiplier=1).then_inc(q["setup_pool"], 1)
            nc.gpsimd.affine_select(out=mask[:, :], in_=mask[:, :], compare_op=ALU.is_ge, fill=0.0,
                                    base=0, pattern=[[-1, N]], channel_multiplier=1).then_inc(q["setup_pool"], 1)
            pool.wait_ge(q["setup_pool"], 6)
            nc.gpsimd.affine_select(out=head_of[:, :], in_=head_of[:, :], compare_op=ALU.is_ge, fill=0.0,
                                    base=DK - 1, pattern=[[DK, HEADS]], channel_multiplier=-1
                                    ).then_inc(q["setup_pool"], 1)
            pool.wait_ge(q["h_in"], 32)
            pool.wait_ge(q["bias_w"], 1)
            nc.gpsimd.tensor_tensor(r[:, :, :], xn[:, :, :], bias[:, :].unsqueeze(1).to_broadcast([N, B, D]),
                                    ALU.add).then_inc(q["r_base"], 1)
            pool.wait_ge(q["var_ok"], 1)
            pool.wait_ge(q["half_ok"], 1)
            nc.gpsimd.tensor_tensor(rstd[:, :], rstd[:, :], half[:, :], ALU.pow).then_inc(q["rstd_ok"], 1)

            def fetch(f, u, first):
                if not first:
                    pool.wait_ge(q["x_turned"], f - 1)
                nc.gpsimd.tensor_copy(xr[u][:, :], xn[:, bass.ds(f, 1), :].rearrange("p o d -> p (o d)")
                                      ).then_inc(q["xr_ok"], 1)

            def subtract(f, u):
                pool.wait_ge(q["s_max"], f + 1)
                nc.gpsimd.tensor_tensor(prob[u][:, :, :], prob[u][:, :, :],
                                        top[u][:, :].unsqueeze(2).to_broadcast([N, HEADS, N]),
                                        ALU.subtract).then_inc(q["s_sub"], 1)
            pool.wait_ge(q["xn_ok"], B)
            fetch(0, 0, True)
            fetch(1, 1, True)
            subtract(0, 0)
            fetch(2, 0, False)
            subtract(1, 1)
            fetch(3, 1, False)
            with pool.Fori(1, B // 2 - 1) as j:
                for u in range(2):
                    subtract(2 * j + u, u)
                    fetch(2 * j + 2 + u, u, False)
            subtract(B - 2, 0)
            subtract(B - 1, 1)

        @block.tensor
        def _(pe):
            pe.wait_ge(q["small_in"], 16 * SETUP_DMAS)
            pe.matmul(ps_x[0:N, 0, 0:D], b_cols[:, 2:3].to_broadcast([D, N]), wout_sb[:, :],
                      start=True, stop=True).then_inc(q["bv_done"], 1)
            pe.wait_ge(q["xn_ok"], B)

            def cema(c, k, first):
                if not first:
                    pe.wait_ge(q["cema_added"], c - 1)
                for e in range(CHUNK):
                    if e == 0:
                        pe.wait_ge(toeplitz_ok[k], 1)
                    mm = pe.matmul(ps_s[0:N, k, 32 * e:32 * e + 32], toeplitz[k][:, e, :],
                                   xn[:, :, bass.ds(c * CHUNK + e, 1)].rearrange("p b o -> p (b o)"),
                                   start=(e == 0), stop=(e == CHUNK - 1), skip_group_check=True)
                mm.then_inc(q["cema_done"], 1)
            for k in range(2):
                cema(k, k, True)
            with pe.Fori(1, CHUNKS // 2) as j:
                for k in range(2):
                    pe.wait_ge(toeplitz_ok[k], j + 1)
                    pe.wait_ge(q["cema_added"], 2 * j + k - 1)
                    for e in range(CHUNK):
                        mm = pe.matmul(ps_s[0:N, k, 32 * e:32 * e + 32], toeplitz[k][:, e, :],
                                       xn[:, :, bass.ds(j * (2 * CHUNK) + (k * CHUNK + e), 1)].rearrange("p b o -> p (b o)"),
                                       start=(e == 0), stop=(e == CHUNK - 1), skip_group_check=True)
                    mm.then_inc(q["cema_done"], 1)
            pe.wait_ge(q["cema_added"], CHUNKS)
            pe.wait_ge(q["bias_ok"], 1)
            pe.wait_ge(q["setup_pool"], SETUP_POOL)

            def turn_x(f, u):
                pe.wait_ge(q["xr_ok"], f + 1)
                pe.transpose(ps_x[:, 0, 0:N], xr[u][:, :], ident[0:N, 0:N]).then_inc(q["x_turned"], 1)

            def project(f, u, first):
                pe.wait_ge(q["xT_ok"], f + 1)
                pe.matmul(ps_k[:, 0, 0:N], wide[:, D:2 * D], xT[u][:, :], start=True, stop=True
                          ).then_inc(q["k_done"], 1)
                pe.matmul(ps_x[:, 0, N:2 * N], wide[:, 0:D], xT[u][:, :], start=True, stop=True
                          ).then_inc(q["q_done"], 1)
                if not first:
                    pe.wait_ge(q["v_ok"], f)
                pe.matmul(ps_v[0:N, 0, 0:D], xT[u][:, :], wide[:, 2 * D:3 * D], start=True,
                          stop=True).then_inc(q["v_done"], 1)

            def scores(f, a, first):
                if a == 0:
                    pe.wait_ge(q["q_ok"], f + 1)
                    pe.wait_ge(q["k_ok"], f + 1)
                    if not first:
                        pe.wait_ge(q["s_masked"], f)
                pe.matmul(ps_s[0:N, a, 0:HALF * N], qT[:, :], kx[:, HALF * a:HALF * a + HALF, :].rearrange(
                    "p h j -> p (h j)"), start=True, stop=True).then_inc(q["s_done" if a else "s_half"], 1)

            def turn_probs(i, u):
                pe.wait_ge(q["p_ok"], i + 1)
                for hf in range(2):
                    for hh in range(HALF):
                        mm = pe.transpose(ps_p[0:N, hf, N * hh:N * hh + N], prob[u][:, HALF * hf + hh, :],
                                          ident[0:N, 0:N])
                    mm.then_inc(q["p_turned"], 1)

            def weigh(i, u, first):
                pe.wait_ge(q["v_ok"], i + 1)
                pe.wait_ge(q["pT_ok"], 2 * i + 2)
                if not first:
                    pe.wait_ge(q["r_ok"], i)
                for hd in range(HEADS):
                    mm = pe.matmul(O[:, hd, :], probT[u][:, hd, :], vx[u][:, hd, :], start=(hd == 0),
                                   stop=(hd == HEADS - 1), skip_group_check=True)
                mm.then_inc(q["o_done"], 1)

            def turn_o(i, u):
                pe.wait_ge(q["o_ok"], i + 1)
                pe.transpose(OT, on[u][:, :], ident[0:N, 0:N]).then_inc(q["o_turned"], 1)

            def project_out(i, u):
                pe.wait_ge(q["oT_ok"], i + 1)
                pe.matmul(W, oT[u][:, :], wout_sb[:, :], start=True, stop=True).then_inc(q["w_done"], 1)

            def step(i, u, front=True):
                if front:
                    turn_x(i + 2, u)
                turn_probs(i, u)
                if front:
                    project(i + 2, u, False)
                weigh(i, u, isinstance(i, int) and i == 0)
                if front:
                    scores(i + 2, 0, False)
                turn_o(i, u)
                if front:
                    scores(i + 2, 1, False)
                project_out(i, u)
            for u in range(2):
                turn_x(u, u)
                project(u, u, u == 0)
                for a in range(2):
                    scores(u, a, u == 0)
            for u in range(2):
                step(u, u)
            with pe.Fori(1, B // 2 - 1) as j:
                for u in range(2):
                    step(2 * j + u, u)
            step(B - 2, 0, front=False)
            step(B - 1, 1, front=False)

        @block.vector
        def _(dve):
            nc.vector.memset(resp[:, N:KPAD], 0.0).then_inc(q["resp_zero"], 1)
            for u in range(2):
                nc.vector.memset(vx[u][:, :, DK:DK + 1], 1.0).then_inc(q["vx_one"], 1)
            dve.wait_ge(q["adapt_in"], 16)
            nc.vector.tensor_reduce(mix_s[:, 0:1], mix[:, :], AX.X, ALU.max).then_inc(q["mix_step"], 1)
            dve.wait_ge(q["mix_step"], MIX_MAX)
            nc.vector.tensor_scalar(mix[:, :], mix[:, :], mix_s[:, 0:1], None, ALU.subtract).then_inc(q["mix_step"], 1)
            dve.wait_ge(q["coeff_in"], 48)
            nc.vector.tensor_tensor(powers[:, N - 1, :], coeff[:, 0, :], coeff[:, 2, :], ALU.mult).then_inc(q["pow_ok"], 1)
            have, steps = 1, 1
            while have < N:
                new = min(have, N - have)
                dve.wait_ge(q["pow_ok"], steps)
                if steps > 1:
                    dve.wait_ge(q["q_sq"], steps - 1)
                nc.vector.tensor_tensor(powers[:, N - have - new:N - have, :], powers[:, N - new:N, :],
                                        coeff[:, 1:2, :].to_broadcast([D, new, NDIM]), ALU.mult).then_inc(q["pow_ok"], 1)
                have, steps = have + new, steps + 1
                if have < N:
                    dve.wait_ge(q["pow_ok"], steps)
                    nc.vector.tensor_tensor(coeff[:, 1, :], coeff[:, 1, :], coeff[:, 1, :],
                                            ALU.mult).then_inc(q["q_sq"], 1)
            dve.wait_ge(q["mix_step"], MIX_EXP)
            nc.vector.tensor_reduce(mix_s[:, 1:2], mix[:, :], AX.X, ALU.add).then_inc(q["mix_step"], 1)
            dve.wait_ge(q["mix_step"], MIX_SUM)
            nc.vector.reciprocal(mix_s[:, 2:3], mix_s[:, 1:2]).then_inc(q["mix_step"], 1)
            dve.wait_ge(q["mix_step"], MIX_INV)
            nc.vector.tensor_scalar(mix[:, :], mix[:, :], mix_s[:, 2:3], None, ALU.mult).then_inc(q["mix_step"], 1)
            dve.wait_ge(q["pow_ok"], steps)
            nc.vector.tensor_reduce(resp[:, 0:N], powers[:, :, :], AX.X, ALU.add).then_inc(q["resp_zero"], 1)
            dve.wait_ge(q["resp_zero"], 2)
            dve.wait_ge(q["mix_step"], MIX_OK)
            nc.vector.tensor_scalar(resp[:, 0:N], resp[:, 0:N], mix[:, 1:2], None,
                                    ALU.mult).then_inc(q["resp_ok"], 1)
            dve.wait_ge(q["bv_done"], 1)
            nc.vector.tensor_tensor(bias[:, :], ps_x[0:N, 0, 0:D], bout_row[:, :], ALU.add).then_inc(q["bias_ok"], 1)
            dve.wait_ge(q["bias_ok"], 1)
            nc.vector.tensor_scalar(bias[:, :], bias[:, :], mix[0:N, 0:1], None, ALU.mult).then_inc(q["bias_w"], 1)
            dve.wait_ge(q["h_in"], 32)
            with dve.Fori(0, B // 4) as j:
                for u in range(4):
                    here = bass.ds(4 * j + u, 1)
                    nc.vector.bn_stats(st[:, here, :].rearrange("p o s -> p (o s)"),
                                       xn[:, here, :].rearrange("p o d -> p (o d)")).then_inc(q["st_ok"], 1)
            moments_to_rstd(dve, nc, st, mean, gap, rstd, q)
            dve.wait_ge(q["rstd_ok"], 1)
            dve.wait_ge(q["r_base"], 1)
            with dve.Fori(0, B // 4) as j:
                for u in range(4):
                    here = bass.ds(4 * j + u, 1)
                    x = xn[:, here, :].rearrange("p o d -> p (o d)")
                    nc.vector.tensor_scalar(x, x, mean[:, here], rstd[:, here],
                                            ALU.subtract, ALU.mult).then_inc(q["xn_ok"], 1)

            def add_cema(c, k):
                dve.wait_ge(q["cema_done"], c + 1)
                at = r[:, :, bass.ds(c * CHUNK, CHUNK)]
                nc.vector.tensor_tensor(at, ps_s[0:N, k, :].rearrange("p (e b) -> p b e", b=B), at,
                                        ALU.add).then_inc(q["cema_added"], 1)
            with dve.Fori(0, CHUNKS // 2) as j:
                for k in range(2):
                    add_cema(2 * j + k, k)

            def spread_keys(f, fresh):
                dve.wait_ge(q["k_done"], f + 1)
                if not fresh:
                    dve.wait_ge(q["s_done"], f)
                nc.vector.scalar_tensor_tensor(
                    out=kx[:, :, :], in0=ps_k[:, 0:1, 0:N].to_broadcast([D, HEADS, N]), scalar=b_cols[:, 1:2],
                    in1=head_of[:, :].unsqueeze(2).to_broadcast([D, HEADS, N]), op0=ALU.add, op1=ALU.mult
                ).then_inc(q["k_ok"], 1)

            def mask_scores(f, u, first):
                dve.wait_ge(q["s_done"], f + 1)
                if not first:
                    dve.wait_ge(q["p_turned"], 2 * f - 2)
                nc.vector.tensor_tensor(prob[u][:, :, :].rearrange("p (a h) j -> p a h j", a=2), S,
                                        strided(mask[:, :], [[0, 2], [0, HALF], [1, N]]), ALU.mult
                                        ).then_inc(q["s_masked"], 1)

            def maxima(f, u, first):
                dve.wait_ge(q["s_masked"], f + 1)
                if not first:
                    dve.wait_ge(q["s_sub"], f - 1)
                nc.vector.tensor_reduce(top[u][:, :], prob[u][:, :, :], AX.X, ALU.max).then_inc(q["s_max"], 1)

            def normalise(i, u, first):
                dve.wait_ge(q["o_done"], i + 1)
                nc.vector.reciprocal(inv[u][:, :], O[:, :, DK]).then_inc(q["o_inv"], 1)
                dve.wait_ge(q["o_inv"], i + 1)
                if not first:
                    dve.wait_ge(q["o_turned"], i - 1)
                nc.vector.tensor_tensor(on[u][:, :].rearrange("p (h d) -> p h d", h=HEADS), O[:, :, 0:DK],
                                        inv[u][:, :].unsqueeze(2).to_broadcast([N, HEADS, DK]), ALU.mult
                                        ).then_inc(q["o_ok"], 1)

            def accumulate(i):
                at = r[:, bass.ds(i, 1), :].rearrange("p o d -> p (o d)")
                dve.wait_ge(q["w_done"], i + 1)
                nc.vector.scalar_tensor_tensor(out=at, in0=W, scalar=mix[0:N, 0:1], in1=at, op0=ALU.mult,
                                               op1=ALU.add).then_inc(q["r_ok"], 1)

            def step(i, u, first=False, front=True):
                if front:
                    spread_keys(i + 2, False)
                normalise(i, u, first)
                if front:
                    mask_scores(i + 2, u, False)
                accumulate(i)
                if front:
                    maxima(i + 2, u, False)
            dve.wait_ge(q["cema_added"], CHUNKS)
            dve.wait_ge(q["setup_pool"], SETUP_POOL)
            for u in range(2):
                spread_keys(u, u == 0)
                mask_scores(u, u, True)
                maxima(u, u, True)
            for u in range(2):
                step(u, u, first=True)
            with dve.Fori(1, B // 2 - 1) as j:
                for u in range(2):
                    step(2 * j + u, u)
            step(B - 2, 0, front=False)
            step(B - 1, 1, front=False)


def moments_to_rstd(dve, nc, st, mean, gap, rstd, q):
    dve.wait_ge(q["st_ok"], B)
    nc.vector.tensor_tensor(mean[:, :], st[:, :, 1], st[:, :, 4], ALU.add).then_inc(q["m_gap"], 1)
    nc.vector.tensor_tensor(gap[:, :], st[:, :, 1], st[:, :, 4], ALU.subtract).then_inc(q["m_gap"], 1)
    nc.vector.tensor_tensor(rstd[:, :], st[:, :, 2], st[:, :, 5], ALU.add).then_inc(q["m_gap"], 1)
    dve.wait_ge(q["m_gap"], 3)
    nc.vector.tensor_scalar(mean[:, :], mean[:, :], 0.5, None, ALU.mult).then_inc(q["m_ok"], 1)
    nc.vector.scalar_tensor_tensor(out=gap[:, :], in0=gap[:, :], scalar=0.25, in1=gap[:, :], op0=ALU.mult,
                                   op1=ALU.mult).then_inc(q["m_ok"], 1)
    nc.vector.tensor_scalar(rstd[:, :], rstd[:, :], 1.0 / D, LN_EPS, ALU.mult, ALU.add).then_inc(q["m_ok"], 1)
    dve.wait_ge(q["m_ok"], 3)
    nc.vector.tensor_tensor(rstd[:, :], rstd[:, :], gap[:, :], ALU.add).then_inc(q["var_ok"], 1)


GROUPS, EXPERTS = 8, 8
GE = GROUPS * EXPERTS
HID = 2 * D
TOKENS = B * N
PICKS = 4
QUAD = 4
QUADS = B // QUAD
REGION = TOKENS
SLOT = D + 2
TILE = 128
TILES = (PICKS * TOKENS + GE * (TILE - 1)) // TILE
SKIP = float(1 << 20)
BF16 = mybir.dt.bfloat16
BIG = 3.0e38

(TOP1, BELOW1, RANK1, FIRST1, HOT1, LEFT, TOP2, BELOW2, RANK2, FIRST2, HOT2, MARGIN, ODDS, PART1, PART2,
 PAIR0, PAIR1, PAIR2, PAIR3, EITHER, CHOSEN, SHARE0, SHARE1, SHARES, WEIGHT, WEIGHED, GATES, SLOTS, PLACED,
 SLOT_OF, SLOT_INT, ADDED, RUNNING, RESULT) = range(1, 35)
ROUTE_STEPS = RESULT


def route(nc, r, g1, g2, b2, slots_dram, weight, tab_base, tab_expert, tab_skip):
    with ExitStack() as ctx:
        def sb(name, shape, dt=F32):
            return ctx.enter_context(nc.sbuf_tensor(name, shape, dt))

        def sem(name):
            return ctx.enter_context(nc.semaphore(name))

        def bank(name, dt=F32):
            return ctx.enter_context(nc.psum_tensor(name, [PART, 2048 // (4 if dt == F32 else 2)], dt))

        ident = sb("ident_d", [PART, PART])
        gate_w = sb("gate_w", [D, GROUPS + GE])
        b2_sb = sb("b2_sb", [GE, D])
        st = sb("st_d", [N, B, 6])
        mean = sb("mean_d", [N, B])
        gap = sb("gap_d", [N, B])
        rstd = sb("rstd_d", [N, B])
        half = sb("half_d", [N, B])
        rows = [sb(f"rows{k}", [N, QUAD, PICKS, SLOT]) for k in range(2)]
        xT = [sb(f"xT_d{k}", [D, QUAD * N]) for k in range(2)]
        place = sb("place", [N, B, PICKS])
        order = sb("order", [N, EXPERTS])
        region = sb("region", [N, GE])
        before = sb("before", [N, N], BF16)
        ones_b = sb("ones_b", [N, N], BF16)
        ones_f = sb("ones_f", [N, 1])
        top = sb("top_d", [N, 2, QUAD, 9])
        below = sb("below", [N, QUAD, 9, EXPERTS])
        ranked = sb("ranked", [N, QUAD, 9, EXPERTS])
        left = sb("left", [N, QUAD, 9, EXPERTS])
        winner = sb("winner", [N, 2, QUAD, 9])
        hot = sb("hot", [N, 2, QUAD, 9, EXPERTS])
        margin = sb("margin", [N, QUAD, 9])
        odds = sb("odds", [N, QUAD, 9])
        part = sb("part", [N, 2, QUAD, 9])
        pair = sb("pair", [N, PICKS, QUAD, GE])
        either = sb("either", [N, QUAD, 9, EXPERTS])
        chosen = sb("chosen", [N, QUAD, GE], BF16)
        share = sb("share", [N, 2, 2, QUAD, GROUPS])
        weighed = sb("weighed", [N, PICKS, QUAD, GE])
        gates = [sb(f"gates{k}", [N, QUAD, GE]) for k in range(2)]
        gates_T = [sb(f"gates_T{k}", [GE, QUAD * N]) for k in range(2)]
        slot_row = sb("slot_row", [N, QUAD, GE])
        slot_f = sb("slot_f", [N, PICKS, QUAD])
        shares = sb("shares", [N, PICKS, QUAD])
        slot = [sb(f"slot{k}", [N, PICKS, QUAD], I32) for k in range(2)]
        added_f = sb("added_f", [N, GE])
        running = sb("running", [N, GE], BF16)
        blank = sb("blank", [PART, SLOT])
        count = sb("count", [GE, 1])
        count_i = sb("count_i", [GE, 1], I32)
        tiles = sb("tiles", [GE, 1])
        upto = sb("upto", [GE, GE])
        bounds = sb("bounds", [GE, 2])
        tile_no = sb("tile_no", [GE, TILES])
        began = sb("began", [GE, TILES])
        mine = sb("mine", [GE, TILES])
        facts = sb("facts", [GE, 5])
        tile_of = sb("tile_of", [PART, TILES])
        at = sb("at", [PART, TILES])
        rel = sb("rel", [PART, TILES])
        unused = sb("unused", [PART, TILES])
        lane = sb("lane", [PART, 1])

        ps_x, ps_l, ps_r, ps_g, ps_b = bank("ps_dx"), bank("ps_dl"), bank("ps_dr"), bank("ps_dg"), bank("ps_db")
        ps_f = [bank(f"ps_df{k}") for k in range(3)]

        names = """x_part pool_base pool_ok half_ok blank_ok blank_base blank_out gates_in b2_in st_ok m_gap m_ok var_ok rstd_ok
            pad_ok running_zero x_ok place_ok x_turned xT_ok logits odds_exp ranks gates_turned gates_T_ok result
            route_step counted count_ok tiles_ok ends mine_ok spread table_step scattered0 scattered1""".split()
        q = {n: sem("d_" + n) for n in names}
        scattered = [q["scattered0"], q["scattered1"]]
        block = ctx.enter_context(nc.Block())
        POOL_SETUP = 12

        @block.sync
        def _(sp):
            sp.dma_start(gate_w[:, 0:GROUPS], g1).then_inc(q["gates_in"], 16)
            sp.dma_start(gate_w[:, GROUPS:].rearrange("d (g e) -> d g e", g=GROUPS),
                         g2.rearrange("g d e -> d g e")).then_inc(q["gates_in"], 16)
            sp.dma_start(b2_sb[:, :], b2.rearrange("g e d -> (g e) d")).then_inc(q["b2_in"], 16)
            sp.wait_ge(q["blank_ok"], 1)
            sp.dma_start(slots_dram.rearrange("(e p) f -> p e f", p=REGION)[0:PART],
                         blank[:, :].unsqueeze(1).to_broadcast([PART, GE + 1, SLOT])).then_inc(q["blank_out"], 16)
            sp.wait_ge(q["blank_out"], 16)

        @block.gpsimd
        def _(pool):
            def setup(n, inst):
                inst.then_inc(q["pool_ok"], 1)
            nc.gpsimd.memset(blank[:, :], 0.0).then_inc(q["blank_base"], 1)
            nc.gpsimd.memset(ident[:, :], 0.0).then_inc(q["pool_base"], 1)
            nc.gpsimd.memset(before[:, :], 1.0).then_inc(q["pool_base"], 1)
            nc.gpsimd.memset(upto[:, :], 1.0).then_inc(q["pool_base"], 1)
            nc.gpsimd.memset(half[:, :], -0.5).then_inc(q["half_ok"], 1)
            pool.wait_ge(q["blank_base"], 1)
            nc.gpsimd.memset(blank[:, D:D + 1], SKIP).then_inc(q["blank_ok"], 1)
            pool.wait_ge(q["pool_base"], 3)
            setup(0, nc.gpsimd.affine_select(out=ident[:, :], in_=ident[:, :], compare_op=ALU.not_equal, fill=1.0,
                                             base=0, pattern=[[-1, PART]], channel_multiplier=1))
            setup(1, nc.gpsimd.affine_select(out=before[:, :], in_=before[:, :], compare_op=ALU.is_gt, fill=0.0,
                                             base=0, pattern=[[1, N]], channel_multiplier=-1))
            setup(2, nc.gpsimd.affine_select(out=upto[:, :], in_=upto[:, :], compare_op=ALU.is_ge, fill=0.0,
                                             base=0, pattern=[[1, GE]], channel_multiplier=-1))
            setup(3, nc.gpsimd.memset(ones_b[:, :], 1.0))
            setup(4, nc.gpsimd.memset(ones_f[:, :], 1.0))
            setup(5, nc.gpsimd.iota(place[:, :, :], pattern=[[N, B], [TOKENS, PICKS]], base=0, channel_multiplier=1,
                                    allow_small_or_imprecise_dtypes=True))
            setup(6, nc.gpsimd.iota(order[:, :], pattern=[[-1, EXPERTS]], base=EXPERTS, channel_multiplier=0,
                                    allow_small_or_imprecise_dtypes=True))
            setup(7, nc.gpsimd.iota(region[:, :], pattern=[[REGION, GE]], base=0, channel_multiplier=0,
                                    allow_small_or_imprecise_dtypes=True))
            setup(8, nc.gpsimd.iota(tile_no[:, :], pattern=[[1, TILES]], base=0, channel_multiplier=0,
                                    allow_small_or_imprecise_dtypes=True))
            setup(9, nc.gpsimd.iota(tile_of[:, :], pattern=[[TILE, TILES]], base=0, channel_multiplier=0,
                                    allow_small_or_imprecise_dtypes=True))
            setup(10, nc.gpsimd.iota(lane[:, :], pattern=[[0, 1]], base=0, channel_multiplier=1,
                                     allow_small_or_imprecise_dtypes=True))
            setup(11, nc.gpsimd.memset(facts[:, 0:1], 1.0))
            pool.wait_ge(q["var_ok"], 1)
            pool.wait_ge(q["half_ok"], 1)
            nc.gpsimd.tensor_tensor(rstd[:, :], rstd[:, :], half[:, :], ALU.pow).then_inc(q["rstd_ok"], 1)

            def scatter(t, u):
                pool.wait_ge(q["place_ok"], t + 1)
                pool.wait_ge(q["route_step"], slots_known)
                pool.reg_add(slots_known, slots_known, ROUTE_STEPS)
                for b in range(QUAD):
                    for k in range(PICKS):
                        nc.gpsimd.indirect_dma_start(
                            out=slots_dram, out_offset=bass.IndirectOffsetOnAxis(ap=slot[u][:, k, b:b + 1], axis=0),
                            in_=rows[u][:, b, k, :], in_offset=None).then_inc(scattered[u], 16)
            slots_known = pool.alloc_register("slots_known")
            pool.reg_mov(slots_known, SLOT_INT)
            pool.wait_ge(q["blank_out"], 16)
            with pool.Fori(0, QUADS // 2) as j:
                for u in range(2):
                    scatter(2 * j + u, u)
            for u in range(2):
                pool.wait_ge(scattered[u], 16 * QUAD * PICKS * QUADS // 2)

        @block.scalar
        def _(act):
            def step(t, u, first):
                act.wait_ge(q["x_turned"], t + 1)
                if not first:
                    act.wait_ge(q["logits"], t - 1)
                nc.scalar.copy(xT[u][:, :], ps_x[:, 0:QUAD * N]).then_inc(q["xT_ok"], 1)
                act.wait_ge(q["route_step"], ROUTE_STEPS * t + MARGIN)
                nc.scalar.activation(odds[:, :, :], margin[:, :, :], ACT.Exp).then_inc(q["odds_exp"], 1)
                act.wait_ge(q["gates_turned"], t + 1)
                if not first:
                    act.wait_ge(q["result"], t - 1)
                nc.scalar.copy(gates_T[u][:, :], ps_g[0:GE, 0:QUAD * N]).then_inc(q["gates_T_ok"], 1)
            for u in range(2):
                step(u, u, True)
            with act.Fori(1, QUADS // 2) as j:
                for u in range(2):
                    step(2 * j + u, u, False)

        @block.tensor
        def _(pe):
            pe.wait_ge(q["pool_ok"], POOL_SETUP)
            pe.wait_ge(q["gates_in"], 32)
            pe.wait_ge(q["b2_in"], 16)
            gates_known = pe.alloc_register("gates_known")
            pe.reg_mov(gates_known, GATES)

            def step(t, u, first):
                pe.wait_ge(q["x_ok"], t + 1)
                if not first:
                    pe.wait_ge(q["xT_ok"], t)
                for b in range(QUAD):
                    mm = pe.transpose(ps_x[:, N * b:N * b + N], rows[u][:, b, 0, 0:D], ident[0:N, 0:N])
                mm.then_inc(q["x_turned"], 1)
                pe.wait_ge(q["xT_ok"], t + 1)
                if not first:
                    pe.wait_ge(q["route_step"], ROUTE_STEPS * (t - 1) + RESULT)
                for b in range(QUAD):
                    mm = pe.matmul(ps_l[0:N, 72 * b:72 * b + 72], xT[u][:, N * b:N * b + N], gate_w[:, :],
                                   start=(b == 0), stop=(b == QUAD - 1), skip_group_check=True)
                mm.then_inc(q["logits"], 1)
                pe.wait_ge(q["route_step"], ROUTE_STEPS * t + CHOSEN)
                for b in range(QUAD):
                    out = ps_r[0:N, GE * b:GE * b + GE]
                    pe.matmul(out, before[:, :], chosen[:, b, :], start=(b == 0), stop=False, skip_group_check=True)
                    for c in range(b):
                        pe.matmul(out, ones_b[:, :], chosen[:, c, :], start=False, stop=False, skip_group_check=True)
                    mm = pe.matmul(out, ones_b[:, :], running[:, :], start=False, stop=(b == QUAD - 1),
                                   skip_group_check=True)
                mm.then_inc(q["ranks"], 1)
                pe.wait_ge(q["route_step"], gates_known)
                pe.reg_add(gates_known, gates_known, ROUTE_STEPS)
                for b in range(QUAD):
                    mm = pe.transpose(ps_g[0:GE, N * b:N * b + N], gates[u][:, b, :], ident[0:N, 0:N])
                mm.then_inc(q["gates_turned"], 1)
                pe.wait_ge(q["gates_T_ok"], t + 1)
                for b in range(QUAD):
                    mm = pe.matmul(ps_b[0:N, D * b:D * b + D], gates_T[u][:, N * b:N * b + N], b2_sb[:, :],
                                   start=(b == 0), stop=(b == QUAD - 1), skip_group_check=True)
                mm.then_inc(q["result"], 1)
            step(0, 0, True)
            step(1, 1, False)
            with pe.Fori(1, QUADS // 2) as j:
                for u in range(2):
                    step(2 * j + u, u, False)
            pe.wait_ge(q["route_step"], ROUTE_STEPS * QUADS)
            pe.wait_ge(q["count_ok"], 1)
            pe.matmul(ps_l[0:GE, 0:1], added_f[:, :], ones_f[:, :], start=True, stop=True).then_inc(q["counted"], 1)
            pe.wait_ge(q["tiles_ok"], 1)
            pe.matmul(ps_r[0:GE, 0:1], upto[:, :], tiles[:, :], start=True, stop=True).then_inc(q["ends"], 1)
            pe.wait_ge(q["mine_ok"], 1)
            for n in range(5):
                pe.matmul(ps_f[n // 2][:, TILES * (n % 2):TILES * (n % 2) + TILES],
                          facts[:, n:n + 1].to_broadcast([GE, PART]), mine[:, :], start=(n % 2 == 0),
                          stop=(n % 2 == 1 or n == 4), skip_group_check=True).then_inc(q["spread"], 1)

        @block.vector
        def _(dve):
            nc.vector.memset(running[:, :], 0.0).then_inc(q["running_zero"], 1)
            for u in range(2):
                nc.vector.memset(rows[u][:, :, :, D + 1:SLOT], 0.0).then_inc(q["pad_ok"], 1)
            with dve.Fori(0, B // 4) as j:
                for u in range(4):
                    here = bass.ds(4 * j + u, 1)
                    nc.vector.bn_stats(st[:, here, :].rearrange("p o s -> p (o s)"),
                                       r[:, here, :].rearrange("p o d -> p (o d)")).then_inc(q["st_ok"], 1)
            moments_to_rstd(dve, nc, st, mean, gap, rstd, q)
            dve.wait_ge(q["pool_ok"], POOL_SETUP)
            dve.wait_ge(q["pad_ok"], 2)
            dve.wait_ge(q["running_zero"], 1)
            dve.wait_ge(q["rstd_ok"], 1)
            L = ps_l[0:N, 0:QUAD * 72].rearrange("p (b g e) -> p b g e", b=QUAD, g=9)

            def flat(ap):
                return ap.rearrange("p b g e -> p (b g) e")

            def over(ap):
                return ap.rearrange("p b g -> p (b g)").unsqueeze(2).to_broadcast([N, QUAD * 9, EXPERTS])

            def step(t, u, first=False, fresh=False):
                def after(n):
                    dve.wait_ge(q["route_step"], ROUTE_STEPS * t + n)

                def done(inst, n):
                    inst.then_inc(q["route_step"], 1)
                for b in range(QUAD):
                    if not fresh and b == 0:
                        dve.wait_ge(scattered[u], 128 * (t - u))
                    i = bass.ds(QUAD * t + b, 1)
                    nc.vector.tensor_scalar(
                        rows[u][:, b, :, 0:D], r[:, i, :].to_broadcast([N, PICKS, D]),
                        mean[:, i], rstd[:, i], ALU.subtract, ALU.mult).then_inc(*((q["x_ok"], 1) if b == QUAD - 1 else (q["x_part"], 1)))
                nc.vector.tensor_scalar(rows[u][:, :, :, D], place[:, bass.ds(QUAD * t, QUAD), :], 0.0, None,
                                        ALU.add).then_inc(q["place_ok"], 1)
                dve.wait_ge(q["logits"], t + 1)
                if not first:
                    after(0)
                done(nc.vector.tensor_reduce(top[:, 0, :, :].rearrange("p b g -> p (b g)"), flat(L), AX.X, ALU.max), TOP1)
                after(TOP1)
                done(nc.vector.tensor_tensor(flat(below), flat(L), over(top[:, 0]), ALU.subtract), BELOW1)
                after(BELOW1)
                order_b = order[:, :].unsqueeze(1).to_broadcast([N, QUAD * 9, EXPERTS])
                done(nc.vector.scalar_tensor_tensor(out=flat(ranked), in0=flat(below), scalar=0.0, in1=order_b,
                                                    op0=ALU.is_ge, op1=ALU.mult), RANK1)
                after(RANK1)
                done(nc.vector.tensor_reduce(winner_[0], flat(ranked), AX.X, ALU.max), FIRST1)
                after(FIRST1)
                done(nc.vector.tensor_tensor(flat(hot[:, 0]), flat(ranked), over(winner[:, 0]), ALU.is_equal), HOT1)
                after(HOT1)
                done(nc.vector.scalar_tensor_tensor(out=flat(left), in0=flat(hot[:, 0]), scalar=-BIG, in1=flat(L),
                                                    op0=ALU.mult, op1=ALU.add), LEFT)
                after(LEFT)
                done(nc.vector.tensor_reduce(top[:, 1, :, :].rearrange("p b g -> p (b g)"), flat(left), AX.X, ALU.max), TOP2)
                after(TOP2)
                done(nc.vector.tensor_tensor(flat(below), flat(left), over(top[:, 1]), ALU.subtract), BELOW2)
                after(BELOW2)
                done(nc.vector.scalar_tensor_tensor(out=flat(ranked), in0=flat(below), scalar=0.0, in1=order_b,
                                                    op0=ALU.is_ge, op1=ALU.mult), RANK2)
                after(RANK2)
                done(nc.vector.tensor_reduce(winner_[1], flat(ranked), AX.X, ALU.max), FIRST2)
                after(FIRST2)
                done(nc.vector.tensor_tensor(flat(hot[:, 1]), flat(ranked), over(winner[:, 1]), ALU.is_equal), HOT2)
                done(nc.vector.tensor_tensor(margin[:, :, :], top[:, 1], top[:, 0], ALU.subtract), MARGIN)
                dve.wait_ge(q["odds_exp"], t + 1)
                done(nc.vector.tensor_scalar(margin[:, :, :], odds[:, :, :], 1.0, None, ALU.add), ODDS)
                after(ODDS)
                done(nc.vector.reciprocal(part[:, 0], margin[:, :, :]), PART1)
                after(PART1)
                done(nc.vector.tensor_tensor(part[:, 1], odds[:, :, :], part[:, 0], ALU.mult), PART2)
                for a in range(2):
                    for c in range(2):
                        done(nc.vector.tensor_tensor(
                            pair[:, 2 * a + c].rearrange("p b (g e) -> p b g e", g=GROUPS),
                            hot[:, a, :, 0, :].unsqueeze(3).to_broadcast([N, QUAD, GROUPS, EXPERTS]),
                            hot[:, c, :, 1:9, :], ALU.mult), PAIR0 + 2 * a + c)
                done(nc.vector.tensor_tensor(flat(either), flat(hot[:, 0]), flat(hot[:, 1]), ALU.add), EITHER)
                after(EITHER)
                if not first:
                    dve.wait_ge(q["ranks"], t)
                done(nc.vector.tensor_tensor(
                    chosen[:, :, :].rearrange("p b (g e) -> p b g e", g=GROUPS),
                    either[:, :, 0, :].unsqueeze(3).to_broadcast([N, QUAD, GROUPS, EXPERTS]),
                    either[:, :, 1:9, :], ALU.mult), CHOSEN)
                after(PART2)
                for a in range(2):
                    done(nc.vector.tensor_tensor(
                        share[:, a], hot[:, a, :, 0, :].unsqueeze(1).to_broadcast([N, 2, QUAD, GROUPS]),
                        part[:, :, :, 1:9], ALU.mult), SHARE0 + a)
                after(SHARE1)
                done(nc.vector.tensor_reduce(shares[:, :, :].rearrange("p k b -> p (k b)"),
                                             share[:, :, :, :, :].rearrange("p a c b g -> p (a c b) g"),
                                             AX.X, ALU.add), SHARES)
                after(SHARES)
                done(nc.vector.tensor_tensor(
                    weight[:, bass.ds(QUAD * t, QUAD), :].rearrange("p b (a c) -> p a c b", a=2),
                    shares[:, :, :].rearrange("p (a c) b -> p a c b", a=2),
                    part[:, :, :, 0].unsqueeze(2).to_broadcast([N, 2, 2, QUAD]), ALU.mult), WEIGHT)
                after(WEIGHT)
                done(nc.vector.tensor_tensor(
                    weighed[:, :, :, :].rearrange("p k b e -> p k b e"),
                    pair[:, :, :, :],
                    weight[:, bass.ds(QUAD * t, QUAD), :].rearrange("p b k -> p k b").unsqueeze(3).to_broadcast(
                        [N, PICKS, QUAD, GE]), ALU.mult), WEIGHED)
                after(WEIGHED)
                if not fresh:
                    dve.wait_ge(q["gates_turned"], t - 1)
                done(nc.vector.tensor_reduce(gates[u][:, :, :].rearrange("p b e -> p (b e)"),
                                             weighed[:, :, :, :].rearrange("p k b e -> p (b e) k"),
                                             AX.X, ALU.add), GATES)
                dve.wait_ge(q["ranks"], t + 1)
                done(nc.vector.tensor_tensor(
                    slot_row[:, :, :], ps_r[0:N, 0:QUAD * GE].rearrange("p (b e) -> p b e", b=QUAD),
                    region[:, :].unsqueeze(1).to_broadcast([N, QUAD, GE]), ALU.add), SLOTS)
                after(SLOTS)
                done(nc.vector.tensor_tensor(
                    weighed[:, :, :, :].rearrange("p k b e -> p k (b e)"),
                    pair[:, :, :, :].rearrange("p k b e -> p k (b e)"),
                    slot_row[:, :, :].rearrange("p b e -> p (b e)").unsqueeze(1).to_broadcast([N, PICKS, QUAD * GE]),
                    ALU.mult), PLACED)
                after(PLACED)
                done(nc.vector.tensor_reduce(slot_f[:, :, :].rearrange("p k b -> p (k b)"),
                                             weighed[:, :, :, :].rearrange("p k b e -> p (k b) e"),
                                             AX.X, ALU.add), SLOT_OF)
                after(SLOT_OF)
                done(nc.vector.tensor_copy(slot[u][:, :, :], slot_f[:, :, :]), SLOT_INT)
                done(nc.vector.tensor_reduce(added_f[:, :], chosen[:, :, :].rearrange("p b e -> p e b"),
                                             AX.X, ALU.add), ADDED)
                after(ADDED)
                done(nc.vector.tensor_tensor(running[:, :], running[:, :], added_f[:, :], ALU.add), RUNNING)
                dve.wait_ge(q["result"], t + 1)
                here = r[:, bass.ds(QUAD * t, QUAD), :]
                done(nc.vector.tensor_tensor(here, here, ps_b[0:N, :].rearrange("p (b d) -> p b d", b=QUAD),
                                             ALU.add), RESULT)
            winner_ = [winner[:, k].rearrange("p b g -> p (b g)") for k in range(2)]
            step(0, 0, first=True, fresh=True)
            step(1, 1, fresh=True)
            with dve.Fori(1, QUADS // 2) as j:
                for u in range(2):
                    step(2 * j + u, u)
            dve.wait_ge(q["route_step"], ROUTE_STEPS * QUADS)
            nc.vector.tensor_copy(added_f[:, :], running[:, :]).then_inc(q["count_ok"], 1)
            n = 0

            def then(inst):
                nonlocal n
                n += 1
                inst.then_inc(q["table_step"], 1)

            def last():
                dve.wait_ge(q["table_step"], n)
            dve.wait_ge(q["counted"], 1)
            then(nc.vector.tensor_copy(count[:, :], ps_l[0:GE, 0:1]))
            last()
            then(nc.vector.tensor_scalar(count_i[:, :], count[:, :], float(TILE - 1), None, ALU.add))
            last()
            then(nc.vector.tensor_scalar(count_i[:, :], count_i[:, :], 7, None, ALU.arith_shift_right))
            last()
            nc.vector.tensor_copy(tiles[:, :], count_i[:, :]).then_inc(q["tiles_ok"], 1)
            dve.wait_ge(q["ends"], 1)
            then(nc.vector.tensor_copy(bounds[:, 1:2], ps_r[0:GE, 0:1]))
            last()
            then(nc.vector.tensor_tensor(bounds[:, 0:1], bounds[:, 1:2], tiles[:, :], ALU.subtract))
            last()
            then(nc.vector.tensor_scalar(began[:, :], tile_no[:, :], bounds[:, 0:1], None, ALU.is_ge))
            then(nc.vector.tensor_scalar(mine[:, :], tile_no[:, :], bounds[:, 1:2], None, ALU.is_ge))
            last()
            then(nc.vector.tensor_copy(facts[:, 2:3], bounds[:, 0:1]))
            then(nc.vector.tensor_scalar(facts[:, 3:4], count[:, :], float(-TILE), 0.0, ALU.add, ALU.max))
            then(nc.vector.tensor_scalar(facts[:, 1:2], lane[0:GE, :], float(REGION), None, ALU.mult))
            then(nc.vector.tensor_scalar(facts[:, 4:5], lane[0:GE, :], float(HID), None, ALU.mult))
            last()
            nc.vector.tensor_tensor(mine[:, :], began[:, :], mine[:, :], ALU.subtract).then_inc(q["mine_ok"], 1)
            dve.wait_ge(q["spread"], 5)
            used, base = ps_f[0][:, 0:TILES], ps_f[0][:, TILES:2 * TILES]
            start, room = ps_f[1][:, 0:TILES], ps_f[1][:, TILES:2 * TILES]
            then(nc.vector.scalar_tensor_tensor(out=at[:, :], in0=start, scalar=float(-TILE), in1=tile_of[:, :],
                                                op0=ALU.mult, op1=ALU.add))
            then(nc.vector.tensor_scalar(unused[:, :], used, -float(GE * REGION), float(GE * REGION), ALU.mult, ALU.add))
            last()
            then(nc.vector.tensor_tensor(rel[:, :], at[:, :], room, ALU.min))
            last()
            then(nc.vector.tensor_tensor(unused[:, :], unused[:, :], rel[:, :], ALU.add))
            then(nc.vector.tensor_tensor(at[:, :], at[:, :], rel[:, :], ALU.subtract))
            last()
            then(nc.vector.tensor_tensor(tab_base[:, :], unused[0:1, :], base[0:1, :], ALU.add))
            then(nc.vector.tensor_copy(tab_expert[:, :], ps_f[2][0:1, 0:TILES]))
            then(nc.vector.tensor_scalar(tab_skip[:, :], at[:, :], lane[:, 0:1], SKIP, ALU.is_gt, ALU.mult))
            last()


def experts(nc, w1_sb, w2_sb, b1, experts_in, expert_loads, slots_dram, results_dram, tab_base, tab_expert, tab_skip):
    with ExitStack() as ctx:
        def sb(name, shape, dt=F32):
            return ctx.enter_context(nc.sbuf_tensor(name, shape, dt))

        def sem(name):
            return ctx.enter_context(nc.semaphore(name))

        RING = 8
        YRING = 4
        x = [sb(f"x_e{k}", [TILE, SLOT]) for k in range(RING)]
        y = [sb(f"y_e{k}", [TILE, D]) for k in range(YRING)]
        place = [sb(f"place_e{k}", [TILE, 1], I32) for k in range(YRING)]
        xT = [sb(f"xT_e{k}", [D, TILE]) for k in range(2)]
        hid = [sb(f"hid_e{k}", [TILE, HID]) for k in range(2)]
        hidT = [sb(f"hidT_e{k}", [D, 2, TILE]) for k in range(2)]
        b1_sb = sb("b1_sb", [GE, HID])
        b1_T = sb("b1_T", [D, 2, GE])
        b1_now = [sb(f"b1_now{k}", [D, 2]) for k in range(2)]
        ident = sb("ident_e", [PART, PART])
        ps_x = [ctx.enter_context(nc.psum_tensor(f"ps_ex{k}", [PART, 512], F32)) for k in range(2)]
        ps_h = [ctx.enter_context(nc.psum_tensor(f"ps_eh{k}", [PART, 512], F32)) for k in range(2)]
        ps_t = [ctx.enter_context(nc.psum_tensor(f"ps_et{k}", [PART, 512], F32)) for k in range(2)]
        ps_y = [ctx.enter_context(nc.psum_tensor(f"ps_ey{k}", [PART, 512], F32)) for k in range(2)]

        names = """b1_in base_ok ident_ok b1_turned b1_ok x_turned xT_ok hid_done hid_ok hid_turned hidT_ok
            y_done y_ok place_ok bias_ok""".split()
        q = {n: sem("e_" + n) for n in names}
        x_in = [sem(f"e_x_in{k}") for k in range(RING)]
        stored = [sem(f"e_stored{k}") for k in range(YRING)]
        block = ctx.enter_context(nc.Block())

        @block.sync
        def _(sp):
            sp.dma_start(b1_sb[:, :], b1.rearrange("g e h -> (g e) h")).then_inc(q["b1_in"], 16)

            def load(t, u, fresh):
                base = sp.value_load(tab_base[0:1, bass.ds(t, 1)], min_val=0, max_val=GE * REGION)
                if not fresh:
                    sp.wait_ge(q["x_turned"], t - RING + 1)
                    sp.wait_ge(q["place_ok"], t - RING + 1)
                sp.dma_start(x[u][:, :], slots_dram[bass.ds(base, TILE), :]).then_inc(x_in[u], 16)
            for u in range(RING):
                load(u, u, True)
            with sp.Fori(1, TILES // RING) as j:
                for u in range(RING):
                    load(RING * j + u, u, False)

        def columns(engine, t, first, many):
            _, values = nc.values_load_multi_w_load_instructions(
                tab_expert[0:1, bass.ds(t + first, many)], [engine], min_val=0, max_val=(GE - 1) * HID)
            return {first + k: value for k, value in enumerate(values)}

        def pipeline(eng, body, lead, lag, engine=None):
            def ring(t, steps, first, many):
                where = columns(engine, t, first, many) if engine else None
                for u in steps:
                    body(t + u, u % RING, where)
            ring(0, range(-lead, 0), 0, 1)
            ring(0, range(0, RING), 0, RING + 1)
            with eng.Fori(1, TILES // RING - 1) as j:
                ring(RING * j, range(0, RING), -1, RING + 2)
            ring(TILES - RING, range(0, RING + lag), -1, RING + 1)

        def where_at(t, u):
            if isinstance(t, int):
                return t - (TILES - RING if t >= TILES - RING else 0)
            return u

        def has(t):
            return not isinstance(t, int) or 0 <= t < TILES

        def later(t, n):
            return not isinstance(t, int) or t >= n

        @block.gpsimd
        def _(pool):
            nc.gpsimd.memset(ident[:, :], 0.0).then_inc(q["base_ok"], 1)
            pool.wait_ge(q["base_ok"], 1)
            nc.gpsimd.affine_select(out=ident[:, :], in_=ident[:, :], compare_op=ALU.not_equal, fill=1.0,
                                    base=0, pattern=[[-1, PART]], channel_multiplier=1).then_inc(q["ident_ok"], 1)

            def store(t, u):
                pool.wait_ge(q["place_ok"], t + 1)
                pool.wait_ge(q["y_ok"], stores)
                pool.reg_add(stores, stores, 1)
                nc.gpsimd.indirect_dma_start(
                    out=results_dram, out_offset=bass.IndirectOffsetOnAxis(ap=place[u][:, 0:1], axis=0),
                    in_=y[u][:, :], in_offset=None, bounds_check=PICKS * TOKENS - 1,
                    oob_is_err=False).then_inc(stored[u], 16)
            stores = pool.alloc_register("stores")
            pool.reg_mov(stores, 1)
            with pool.Fori(0, TILES // YRING) as j:
                for u in range(YRING):
                    store(YRING * j + u, u)
            for u in range(YRING):
                pool.wait_ge(stored[u], 16 * TILES // YRING)

        @block.tensor
        def _(pe):
            pe.wait_ge(q["ident_ok"], 1)
            pe.wait_ge(q["b1_in"], 16)
            for half in range(2):
                pe.transpose(ps_t[0][:, GE * half:GE * half + GE], b1_sb[:, D * half:D * half + D],
                             ident[0:GE, 0:GE]).then_inc(q["b1_turned"], 1)
            for k in range(len(experts_in)):
                pe.wait_ge(experts_in[k], 16 * expert_loads)
            pe.wait_ge(q["b1_ok"], 1)

            def body(t, u, where):
                v = u % 2
                if has(t + 2):
                    a = t + 2
                    pe.wait_ge(x_in[(u + 2) % RING],
                               16 * (a // RING + 1) if isinstance(a, int) else 16 // RING * (t - u) + (16 if u < RING - 2 else 32))
                    if later(a, 2):
                        pe.wait_ge(q["xT_ok"], a - 1)
                    pe.transpose(ps_x[v][:, 0:TILE], x[(u + 2) % RING][:, 0:D], ident[:, :]).then_inc(q["x_turned"], 1)
                if has(t + 1):
                    a, w = t + 1, 1 - v
                    first = where[where_at(t, u) + 1]
                    pe.wait_ge(q["xT_ok"], a + 1)
                    if later(a, 2):
                        pe.wait_ge(q["hid_ok"], a - 1)
                    pe.matmul(ps_h[w][:, 0:HID], xT[w][:, :], w1_sb[:, bass.ds(first, HID)], start=True,
                              stop=True).then_inc(q["hid_done"], 1)
                if has(t):
                    pe.wait_ge(q["hid_ok"], t + 1)
                    if later(t, 2):
                        pe.wait_ge(q["hidT_ok"], 2 * t - 2)
                    for half in range(2):
                        pe.transpose(ps_t[v][:, TILE * half:TILE * half + TILE], hid[v][:, D * half:D * half + D],
                                     ident[:, :]).then_inc(q["hid_turned"], 1)
                if has(t - 1):
                    a, w = t - 1, 1 - v
                    first = where[where_at(t, u) - 1]
                    pe.wait_ge(q["hidT_ok"], 2 * a + 2)
                    if later(a, 2):
                        pe.wait_ge(q["y_ok"], a - 1)
                    for half in range(2):
                        mm = pe.matmul(ps_y[w][:, 0:D], hidT[w][:, half, :], w2_sb[:, bass.ds(first + D * half, D)],
                                       start=(half == 0), stop=(half == 1))
                    mm.then_inc(q["y_done"], 1)
            pipeline(pe, body, 2, 1, mybir.EngineType.PE)

        @block.scalar
        def _(act):
            act.wait_ge(q["b1_turned"], 2)
            nc.scalar.copy(b1_T[:, :, :], ps_t[0][:, 0:2 * GE].rearrange("p (k e) -> p k e", k=2)).then_inc(q["b1_ok"], 1)

            def body(t, u, where):
                v = u % 2
                if has(t + 2):
                    a = t + 2
                    act.wait_ge(q["x_turned"], a + 1)
                    if later(a, 2):
                        act.wait_ge(q["hid_done"], a - 1)
                    nc.scalar.copy(xT[v][:, :], ps_x[v][:, 0:TILE]).then_inc(q["xT_ok"], 1)
                if has(t):
                    act.wait_ge(q["bias_ok"], t + 1)
                    if later(t, 2):
                        act.wait_ge(q["y_done"], t - 1)
                    act.wait_ge(q["hid_turned"], 2 * t + 2)
                    for half in range(2):
                        nc.scalar.activation(hidT[v][:, half, :], ps_t[v][:, TILE * half:TILE * half + TILE],
                                             ACT.Relu, bias=b1_now[v][:, half:half + 1]).then_inc(q["hidT_ok"], 1)
            pipeline(act, body, 2, 0)

        @block.vector
        def _(dve):
            def body(t, u, where):
                v = u % 2
                if has(t + 1):
                    a, w = t + 1, 1 - v
                    dve.wait_ge(q["hid_done"], a + 1)
                    if later(a, 2):
                        dve.wait_ge(q["hid_turned"], 2 * a - 2)
                    nc.vector.tensor_copy(hid[w][:, :], ps_h[w][:, 0:HID]).then_inc(q["hid_ok"], 1)
                    first = where[where_at(t, u) + 1]
                    if later(a, 2):
                        dve.wait_ge(q["hidT_ok"], 2 * a - 2)
                    nc.vector.tensor_scalar(b1_now[w][:, :].unsqueeze(2), b1_T[:, :, bass.ds(first // HID, 1)], 0.0, None,
                                            ALU.add).then_inc(q["bias_ok"], 1)
                if has(t):
                    if later(t, YRING):
                        dve.wait_ge(stored[u % YRING], 16 * (t // YRING) if isinstance(t, int) else
                                    16 // YRING * (t - u % YRING))
                    nc.vector.tensor_tensor(place[u % YRING][:, :], x[u][:, D:D + 1], tab_skip[:, bass.ds(t, 1)],
                                            ALU.add).then_inc(q["place_ok"], 1)
                if has(t - 1):
                    a, w, z = t - 1, 1 - v, (u - 1) % YRING
                    dve.wait_ge(q["y_done"], a + 1)
                    if later(a, YRING):
                        dve.wait_ge(stored[z], 16 * (a // YRING) if isinstance(a, int) else
                                    16 // YRING * (a - z))
                    nc.vector.tensor_copy(y[z][:, :], ps_y[w][:, 0:D]).then_inc(q["y_ok"], 1)

            dve.wait_ge(q["b1_ok"], 1)
            pipeline(dve, body, 1, 1, mybir.EngineType.DVE)


def combine(nc, r, weight, results_dram, out):
    with ExitStack() as ctx:
        def sem(name):
            return ctx.enter_context(nc.semaphore(name))
        parts = [ctx.enter_context(nc.sbuf_tensor(f"parts{k}", [N, PICKS, QUAD, D], F32)) for k in range(2)]
        parts_in = [sem(f"f_parts_in{k}") for k in range(2)]
        summed = sem("f_summed")
        out_ok = sem("f_out_ok")
        block = ctx.enter_context(nc.Block())

        @block.sync
        def _(sp):
            pick = results_dram.rearrange("(k b n) d -> k n b d", k=PICKS, b=B)

            def load(t, u, fresh):
                if not fresh:
                    sp.wait_ge(summed, 16 * t - 16)
                for k in range(PICKS):
                    sp.dma_start(parts[u][:, k, :, :], pick[k, :, bass.ds(QUAD * t, QUAD), :]).then_inc(parts_in[u], 16)
            for u in range(2):
                load(u, u, True)
            with sp.Fori(1, QUADS // 2) as j:
                for u in range(2):
                    load(2 * j + u, u, False)

        @block.scalar
        def _(act):
            with act.Fori(0, QUADS) as t:
                act.wait_ge(summed, 16 * t + 16)
                act.dma_start(out[bass.ds(QUAD * t, QUAD)].rearrange("b n d -> n b d"),
                              r[:, bass.ds(QUAD * t, QUAD), :]).then_inc(out_ok, 16)
            act.wait_ge(out_ok, 16 * QUADS)

        @block.vector
        def _(dve):
            def add(t, u):
                dve.wait_ge(parts_in[u], 32 * (t - u) + 64)
                for k in range(PICKS):
                    for b in range(QUAD):
                        i = bass.ds(QUAD * t + b, 1)
                        at = r[:, i, :].rearrange("p o d -> p (o d)")
                        if k > 0:
                            dve.wait_ge(summed, 16 * t + 4 * (k - 1) + b + 1)
                        nc.vector.scalar_tensor_tensor(
                            out=at, in0=parts[u][:, k, b, :], scalar=weight[:, i, k:k + 1].rearrange("p o k -> p (o k)"),
                            in1=at, op0=ALU.mult, op1=ALU.add).then_inc(summed, 1)
            with dve.Fori(0, QUADS // 2) as j:
                for u in range(2):
                    add(2 * j + u, u)


def early_fusion(nc, args, out):
    (x, txt, conv_w, conv_b, gamma, beta, dense_w, dense_b, w_qkv, b_qkv, w_out, b_out, p_coeff, q_coeff, cema_gamma,
     adaptive, g1, g2, w1, b1, w2, b2) = args
    h_dram = nc.dram_tensor("image_tokens", [B, PATCHES, D], F32, kind="Internal").ap()
    response = nc.dram_tensor("impulse_response", [D, KPAD], F32, kind="Internal").ap()
    slots_dram = nc.dram_tensor("expert_slots", [(GE + 1) * REGION, SLOT], F32, kind="Internal").ap()
    results_dram = nc.dram_tensor("expert_results", [PICKS * TOKENS, D], F32, kind="Internal").ap()
    patch_tokens(nc, x, conv_w, conv_b, gamma, beta, dense_w, dense_b, h_dram)
    with ExitStack() as ctx:
        def sb(name, shape, dt=F32):
            return ctx.enter_context(nc.sbuf_tensor(name, shape, dt))
        r = sb("r", [N, B, D])
        w1_sb = sb("w1_sb", [D, GE * HID])
        w2_sb = sb("w2_sb", [D, GE * HID])
        experts_in = [ctx.enter_context(nc.semaphore(f"experts_in{k}")) for k in range(2)]

        def fetch_experts(sp):
            for g in range(GROUPS):
                cols = slice(g * EXPERTS * HID, (g + 1) * EXPERTS * HID)
                sp.dma_start(w1_sb[:, cols].rearrange("d (e h) -> d e h", e=EXPERTS),
                             w1[g].rearrange("e d h -> d e h")).then_inc(experts_in[0], 16)
                sp.dma_start(w2_sb[:, cols].rearrange("p (k d) -> p k d", d=D),
                             w2[g].rearrange("e (k p) d -> p (e k) d", p=D)).then_inc(experts_in[1], 16)
        attention(nc, h_dram, txt, w_qkv, b_qkv, w_out, b_out, p_coeff, q_coeff, cema_gamma, adaptive, response, r,
                  fetch_experts)
        weight = sb("weight", [N, B, PICKS])
        tab_base = sb("tab_base", [1, TILES], I32)
        tab_expert = sb("tab_expert", [1, TILES], I32)
        tab_skip = sb("tab_skip", [PART, TILES])
        route(nc, r, g1, g2, b2, slots_dram, weight, tab_base, tab_expert, tab_skip)
        experts(nc, w1_sb, w2_sb, b1, experts_in, GROUPS, slots_dram, results_dram, tab_base, tab_expert, tab_skip)
        combine(nc, r, weight, results_dram, out)


_INS = ['x', 'txt', 'L0_tok_conv_w', 'L0_tok_conv_b', 'L0_tok_gamma', 'L0_tok_beta', 'L0_tok_dense_w',
        'L0_tok_dense_b', 'L0_attn_W_qkv', 'L0_attn_b_qkv', 'L0_attn_W_out', 'L0_attn_b_out', 'L0_attn_p_coeff',
        'L0_attn_q_coeff', 'L0_attn_gamma', 'L0_attn_adaptive_weights', 'L0_ffn_g1', 'L0_ffn_g2', 'L0_ffn_W1',
        'L0_ffn_b1', 'L0_ffn_W2', 'L0_ffn_b2']


def kernel(**inputs):
    import numpy as _np
    import concourse.bacc as _bacc
    from concourse import mybir as _mybir
    from concourse.bass_utils import run_bass_kernel_spmd as _run

    nc = _bacc.Bacc("TRN2", target_bir_lowering=False, num_devices=1)
    arrays, args = {}, []
    for name in _INS:
        a = _np.ascontiguousarray(inputs[name])
        arrays[f"in_{name}_dram"] = a
        args.append(nc.dram_tensor(f"in_{name}_dram", a.shape, _mybir.dt.from_np(a.dtype), kind="ExternalInput").ap())
    out = nc.dram_tensor("out_dram", (B, N, D), _mybir.dt.float32, kind="ExternalOutput").ap()
    early_fusion(nc, args, out)
    r = _run(nc, [arrays], core_ids=[0])
    return r.results[0]["out_dram"]
```

```python
from contextlib import ExitStack

import concourse.bass as bass
from concourse import mybir

ALU = mybir.AluOpType
ACT = mybir.ActivationFunctionType
AX = mybir.AxisListType
F32 = mybir.dt.float32
I32 = mybir.dt.int32

PART = 128
B, IMG, C = 32, 112, 3
P = 16
G = IMG // P
PATCHES = G * G
TXT = 32
N = PATCHES + TXT
D = 128
ROWLEN = (IMG + 2) * C
TOK_EPS, LN_EPS = 1e-3, 1e-5

W_LOADS = 6 + 8 + 5
ROW_LOADS = 8

TILE_ROWS = [4, 3]
TILE_PARTS = [B * r for r in TILE_ROWS]
KT = [128] * 6 + [96, 96]
KCOLS = sum(KT)
KOFF = [sum(KT[:m]) for m in range(8)]
PIXELS_HALF = C * (P // 2) * P
SIDES = 2 * PIXELS_HALF
ENDS = SIDES + 96


def strided(ap, dims):
    return bass.AP(ap.tensor, ap.offset, [ap.ap[0]] + [list(d) for d in dims])


def at_start(pc):
    return isinstance(pc, int) and pc == 0


MIX_MAX, MIX_SUB, MIX_EXP, MIX_SUM, MIX_INV, MIX_OK = range(1, 7)


def patch_tokens(nc, x, conv_w, conv_b, gamma, beta, dense_w, dense_b, h_dram, coefficients, adaptive, mix,
                 response, attention_loads):
    with ExitStack() as ctx:
        def sb(name, shape, dt=F32):
            return ctx.enter_context(nc.sbuf_tensor(name, shape, dt))

        def psum(name, shape, dt=F32):
            return ctx.enter_context(nc.psum_tensor(name, shape, dt))

        def sem(name):
            return ctx.enter_context(nc.semaphore(name))

        image = [sb(f"image{k}", [PART, P + 2, ROWLEN]) for k in range(2)]
        patch = [sb(f"patch{k}", [PART, KCOLS]) for k in range(2)]
        patch_T = [sb(f"patch_T{k}", [PART, 8, 128]) for k in range(2)]
        w_src = sb("w_src", [PART, 5, 6, D])
        w_edge = sb("w_edge", [97, 2, D])
        stats = sb("stats", [PART, 2, 6])
        moments = sb("moments", [PART, 2, 2])
        rstd = sb("rstd", [PART, 2])
        half = sb("half", [PART, 1])
        mix_s = sb("mix_s", [PART, 3])
        coeff = sb("coeff", [D, 3, NDIM])
        powers = sb("powers", [D, N, NDIM])
        resp = sb("resp", [D, KPAD])
        normed = [sb(f"normed{k}", [PART, D]) for k in range(2)]
        normed_T = [sb(f"normed_T{k}", [PART, D]) for k in range(2)]
        token = [sb(f"token{k}", [PART, D]) for k in range(2)]
        dense_sb = sb("dense_sb", [D, D])
        dense_b_row = sb("dense_b_row", [PART, D])
        gamma_col = sb("gamma_col", [D, 1])
        beta_col = sb("beta_col", [D, 1])
        ident = sb("ident_a", [PART, PART])

        ps_T = [psum(f"ps_T{k}", [PART, 8, 128]) for k in range(2)]
        ps_y = [psum(f"ps_y{k}", [PART, 512]) for k in range(2)]
        ps_n = [psum(f"ps_n{k}", [PART, 512]) for k in range(2)]

        borders_zero = sem("borders_zero")
        image_in = [sem(f"image_in{k}") for k in range(2)]
        w_zero = sem("w_zero")
        w_in = sem("w_in")
        rows_in = sem("rows_in")
        w_sum = sem("w_sum")
        small_in = sem("small_in")
        ident_ok = sem("ident_ok")
        patch_ok = sem("patch_ok")
        patch_read = sem("patch_read")
        transposed = sem("transposed")
        left_half = sem("left_half")
        right_half = sem("right_half")
        conv_ok = sem("conv_ok")
        rest_ok = sem("rest_ok")
        stats_ok = sem("stats_ok")
        moments_ok = sem("moments_ok")
        rstd_ok = sem("rstd_ok")
        rstd_pow = sem("rstd_pow")
        ones_ok = sem("ones_ok")
        normed_ok = sem("normed_ok")
        normed_turned = sem("normed_turned")
        normed_T_ok = sem("normed_T_ok")
        dense_ok = sem("dense_ok")
        token_ok = sem("token_ok")
        weights_in = sem("weights_in")
        coeff_in = sem("coeff_in")
        adapt_in = sem("adapt_in")
        mix_step = sem("mix_step")
        pow_ok = sem("pow_ok")
        q_squared = sem("q_squared")
        resp_rows = sem("resp_rows")
        resp_ok = sem("resp_ok")
        resp_out = sem("resp_out")
        stored = [sem(f"stored{k}") for k in range(2)]

        block = ctx.enter_context(nc.Block())

        def load_rows(queue, jl, signal):
            for s, (p0, i0) in ((3, (0, 1)), (4, (1, 0))):
                queue.dma_start(
                    w_src[16 * jl + p0:16 * jl + p0 + 15, s, :, :].rearrange("i (h c) d -> i h (c d)", h=2),
                    conv_w[i0:i0 + 15, jl:16:8, 3 * s:3 * s + 3, :].rearrange("i h c d -> i h (c d)"),
                ).then_inc(signal, 16)

        def load_image(queue, k):
            for r in range(TILE_ROWS[k]):
                pr = 4 * k + r
                lo, hi = max(P * pr - 1, 0), min(P * pr + P + 1, IMG)
                first = lo - (P * pr - 1)
                queue.dma_start(image[k][B * r:B * r + B, first:first + hi - lo, C:C + IMG * C],
                                x[:, lo:hi, :, :].rearrange("b i j c -> b i (j c)")).then_inc(image_in[k], 16)

        @block.sync
        def _(sp):
            for n, coefficient in enumerate(coefficients):
                sp.dma_start(coeff[:, n, :], coefficient).then_inc(coeff_in, 16)
            sp.dma_start(mix[:, :], adaptive.partition_broadcast(PART)).then_inc(adapt_in, 16)
            sp.wait_ge(borders_zero, 6)
            load_image(sp, 0)
            load_image(sp, 1)
            sp.wait_ge(w_in, 16 * W_LOADS)
            for place, source in attention_loads:
                sp.dma_start(place, source).then_inc(weights_in, 16)
            sp.wait_ge(resp_ok, 1)
            sp.dma_start(response, resp[:, :]).then_inc(resp_out, 16)

            def store(pc, k, t):
                sp.wait_ge(token_ok, t + 1)
                rows = h_dram.rearrange("b (r c) d -> c r b d", c=G)
                sp.dma_start(rows[bass.ds(pc, 1), 4 * k:4 * k + TILE_ROWS[k]].rearrange("o r b d -> (o r) b d"),
                             token[k][0:TILE_PARTS[k], :]).then_inc(stored[k], 16)
            with sp.Fori(0, G) as pc:
                for k in range(2):
                    store(pc, k, 2 * pc + k)
            for k in range(2):
                sp.wait_ge(stored[k], 16 * G)
            sp.wait_ge(resp_out, 16)
            sp.wait_ge(weights_in, 16 * len(attention_loads))

        @block.scalar
        def _(act):
            w5 = conv_w.rearrange("i j (s c) d -> s j i (c d)", s=5)
            act.wait_ge(w_zero, 1)
            for hf in range(2):
                j0, mine = 8 * hf, slice(3 * hf, 3 * hf + 3)
                act.dma_start(w_src[:, 0, mine, :], w5[0, j0:j0 + 8]).then_inc(w_in, 16)
                n, none = 8 - hf, 1 - hf
                act.dma_start(w_src[0:16 * n, 1, mine, :], w5[1, j0 + 1:j0 + 1 + n]).then_inc(w_in, 16)
                act.dma_start(w_src[16 * none:128, 2, mine, :], w5[2, j0 - 1 + none:j0 + 7]).then_inc(w_in, 16)
            for jl in range(4, 8):
                load_rows(act, jl, w_in)
            act.dma_start(w_edge[0:48, 0, :], conv_w[:, 0, 3:6, :].rearrange("i c d -> c i d")).then_inc(w_in, 16)
            act.dma_start(w_edge[48:96, 0, :], conv_w[:, 15, 6:9, :].rearrange("i c d -> c i d")).then_inc(w_in, 16)
            act.dma_start(w_edge[0:48, 1, :], conv_w[0, :, 9:12, :].rearrange("j c d -> c j d")).then_inc(w_in, 16)
            act.dma_start(w_edge[48:96, 1, :], conv_w[15, :, 12:15, :].rearrange("j c d -> c j d")).then_inc(w_in, 16)
            act.dma_start(w_edge[96:97, 0, :], conv_b.rearrange("(o d) -> o d", o=1)).then_inc(w_in, 16)
            act.dma_start(dense_b_row[:, :], dense_b.partition_broadcast(PART)).then_inc(small_in, 16)
            act.dma_start(dense_sb[:, :], dense_w).then_inc(small_in, 16)
            act.dma_start(gamma_col[:, :], gamma.rearrange("(d o) -> d o", o=1)).then_inc(small_in, 16)
            act.dma_start(beta_col[:, :], beta.rearrange("(d o) -> d o", o=1)).then_inc(small_in, 16)

            act.wait_ge(mix_step, MIX_SUB)
            nc.scalar.activation(mix[:, :], mix[:, :], ACT.Exp).then_inc(mix_step, 1)

            def first_half(pc, k):
                t = 2 * pc + k
                act.wait_ge(transposed, t + 1)
                if not at_start(pc):
                    act.wait_ge(conv_ok, t - 1)
                nk = TILE_PARTS[k]
                nc.scalar.copy(patch_T[k][:, 0:4, 0:nk], ps_T[k][:, 0:4, 0:nk]).then_inc(left_half, 1)

            def scaled(pc, k):
                t = 2 * pc + k
                act.wait_ge(normed_turned, t + 1)
                if not at_start(pc):
                    act.wait_ge(dense_ok, t - 1)
                nk = TILE_PARTS[k]
                nc.scalar.activation(normed_T[k][:, 0:nk], ps_n[k][:, 0:nk], ACT.Identity,
                                     bias=beta_col[:, 0:1], scale=gamma_col[:, 0:1]).then_inc(normed_T_ok, 1)
            first_half(0, 0)
            first_half(0, 1)
            first_half(1, 0)
            act.wait_ge(small_in, 64)
            first_half(1, 1)
            scaled(0, 0)
            with act.Fori(2, G) as pc:
                first_half(pc, 0)
                scaled(pc - 2, 1)
                first_half(pc, 1)
                scaled(pc - 1, 0)
            scaled(G - 2, 1)
            scaled(G - 1, 0)
            scaled(G - 1, 1)

        @block.gpsimd
        def _(pool):
            nc.gpsimd.memset(ident[:, :], 0.0).then_inc(ident_ok, 1)
            nc.gpsimd.memset(half[:, :], -0.5).then_inc(ident_ok, 1)
            pool.wait_ge(ident_ok, 2)
            nc.gpsimd.affine_select(out=ident[:, :], in_=ident[:, :], compare_op=ALU.not_equal, fill=1.0,
                                    base=0, pattern=[[-1, PART]], channel_multiplier=1).then_inc(ident_ok, 1)

            def gather(pc, k):
                if not at_start(pc):
                    pool.wait_ge(patch_read, 2 * pc + k - 1)
                nk = TILE_PARTS[k]
                rows = image[k][0:nk, :, :].rearrange("p i f -> p (i f)")
                inner = rows[:, bass.ds(pc * (P * C) + ROWLEN + C, 1)]
                nc.gpsimd.tensor_copy(
                    patch[k][0:nk, 0:PIXELS_HALF].rearrange("p (c j i) -> p c j i", c=C, i=P),
                    strided(inner, [[1, C], [C, 8], [ROWLEN, P]])).then_inc(patch_ok, 1)
                beside = rows[:, bass.ds(pc * (P * C) + ROWLEN, 1)]
                nc.gpsimd.tensor_copy(
                    patch[k][0:nk, SIDES:ENDS].rearrange("p (s c i) -> p s c i", s=2, c=C),
                    strided(beside, [[(P + 1) * C, 2], [1, C], [ROWLEN, P]])).then_inc(patch_ok, 1)

            def root(pc, k):
                nk = TILE_PARTS[k]
                pool.wait_ge(rstd_ok, 2 * pc + k + 1)
                nc.gpsimd.tensor_tensor(rstd[0:nk, k:k + 1], rstd[0:nk, k:k + 1], half[0:nk, :],
                                        ALU.pow).then_inc(rstd_pow, 1)
            pool.wait_ge(w_zero, 1)
            for jl in range(4):
                load_rows(pool, jl, rows_in)
            for k in range(2):
                pool.wait_ge(image_in[k], 16 * TILE_ROWS[k])
                gather(0, k)
            gather(1, 0)
            gather(1, 1)
            gather(2, 0)
            root(0, 0)
            with pool.Fori(2, G - 1) as pc:
                root(pc - 2, 1)
                gather(pc, 1)
                root(pc - 1, 0)
                gather(pc + 1, 0)
            root(G - 3, 1)
            gather(G - 1, 1)
            root(G - 2, 0)
            root(G - 2, 1)
            root(G - 1, 0)
            root(G - 1, 1)

        @block.tensor
        def _(pe):
            def turn(pc, k):
                t = 2 * pc + k
                pe.wait_ge(rest_ok, 2 * t + 2)
                pe.wait_ge(patch_ok, 2 * t + 2)
                nk = TILE_PARTS[k]
                for m in range(8):
                    last = pe.transpose(ps_T[k][0:KT[m], m, 0:nk], patch[k][0:nk, KOFF[m]:KOFF[m] + KT[m]],
                                        ident[0:nk, 0:nk])
                    if m == 3:
                        last.then_inc(transposed, 1)
                last.then_inc(patch_read, 1)

            def convolve(pc, k):
                t = 2 * pc + k
                nk = TILE_PARTS[k]
                if not at_start(pc):
                    pe.wait_ge(normed_ok, t - 1)
                for m in range(8):
                    if m == 0:
                        pe.wait_ge(left_half, t + 1)
                    if m == 4:
                        pe.wait_ge(right_half, 2 * t + 2)
                    w = w_src[:, 0, m, :] if m < 6 else w_edge[0:(97 if m == 6 else 96), m - 6, :]
                    kk = 97 if m == 6 else KT[m]
                    last = pe.matmul(ps_y[k][0:nk, 0:D], patch_T[k][0:kk, m, 0:nk], w,
                                     start=(m == 0), stop=(m == 7))
                last.then_inc(conv_ok, 1)

            def turn_normed(pc, k):
                t = 2 * pc + k
                pe.wait_ge(normed_ok, t + 1)
                if not at_start(pc):
                    pe.wait_ge(token_ok, t - 1)
                nk = TILE_PARTS[k]
                pe.transpose(ps_n[k][:, 0:nk], normed[k][0:nk, :], ident[0:nk, 0:nk]).then_inc(normed_turned, 1)

            def dense(pc, k):
                t = 2 * pc + k
                pe.wait_ge(normed_T_ok, t + 1)
                nk = TILE_PARTS[k]
                pe.matmul(ps_n[k][0:nk, D:2 * D], normed_T[k][:, 0:nk], dense_sb[:, :],
                          start=True, stop=True).then_inc(dense_ok, 1)

            pe.wait_ge(ident_ok, 3)
            turn(0, 0)
            turn(0, 1)
            pe.wait_ge(left_half, 1)
            pe.wait_ge(right_half, 2)
            turn(1, 0)
            pe.wait_ge(w_in, 16 * W_LOADS)
            pe.wait_ge(w_sum, 4)
            pe.wait_ge(ones_ok, 2)
            convolve(0, 0)
            convolve(0, 1)
            turn(1, 1)
            convolve(1, 0)
            turn_normed(0, 0)
            turn(2, 0)
            convolve(1, 1)
            turn_normed(0, 1)
            pe.wait_ge(small_in, 64)
            dense(0, 0)
            with pe.Fori(2, G - 1) as pc:
                turn(pc, 1)
                convolve(pc, 0)
                turn_normed(pc - 1, 0)
                dense(pc - 2, 1)
                turn(pc + 1, 0)
                convolve(pc, 1)
                turn_normed(pc - 1, 1)
                dense(pc - 1, 0)
            turn(G - 1, 1)
            convolve(G - 1, 0)
            turn_normed(G - 2, 0)
            dense(G - 3, 1)
            convolve(G - 1, 1)
            turn_normed(G - 2, 1)
            dense(G - 2, 0)
            turn_normed(G - 1, 0)
            dense(G - 2, 1)
            turn_normed(G - 1, 1)
            dense(G - 1, 0)
            dense(G - 1, 1)

        @block.vector
        def _(dve):
            for k in range(2):
                nc.vector.memset(image[k][:, 1:P + 1, 0:C], 0.0).then_inc(borders_zero, 1)
                nc.vector.memset(image[k][:, 1:P + 1, ROWLEN - C:ROWLEN], 0.0).then_inc(borders_zero, 1)
            nc.vector.memset(image[0][0:B, 0, :], 0.0).then_inc(borders_zero, 1)
            nc.vector.memset(image[1][2 * B:3 * B, P + 1, :], 0.0).then_inc(borders_zero, 1)
            nc.vector.memset(w_src[:, 1:5, :, :], 0.0).then_inc(w_zero, 1)
            for k in range(2):
                nc.vector.memset(patch_T[k][96:97, 6, :], 1.0).then_inc(ones_ok, 1)
            nc.vector.memset(resp[:, N:KPAD], 0.0).then_inc(resp_rows, 1)

            def gather_rest(pc, k):
                nk = TILE_PARTS[k]
                rows = image[k][0:nk, :, :].rearrange("p i f -> p (i f)")
                inner = rows[:, bass.ds(pc * (P * C) + ROWLEN + C + 8 * C, 1)]
                nc.vector.tensor_copy(
                    patch[k][0:nk, PIXELS_HALF:2 * PIXELS_HALF].rearrange("p (c j i) -> p c j i", c=C, i=P),
                    strided(inner, [[1, C], [C, 8], [ROWLEN, P]])).then_inc(rest_ok, 1)
                ends = rows[:, bass.ds(pc * (P * C) + C, 1)]
                nc.vector.tensor_copy(
                    patch[k][0:nk, ENDS:KCOLS].rearrange("p (r c j) -> p r c j", r=2, c=C),
                    strided(ends, [[(P + 1) * ROWLEN, 2], [1, C], [C, P]])).then_inc(rest_ok, 1)

            def second_half(pc, k):
                t = 2 * pc + k
                dve.wait_ge(patch_read, t + 1)
                if not at_start(pc):
                    dve.wait_ge(conv_ok, t - 1)
                nk = TILE_PARTS[k]
                nc.vector.tensor_copy(patch_T[k][:, 4:6, 0:nk], ps_T[k][:, 4:6, 0:nk]).then_inc(right_half, 1)
                nc.vector.tensor_copy(patch_T[k][0:96, 6:8, 0:nk], ps_T[k][0:96, 6:8, 0:nk]).then_inc(right_half, 1)

            dve.wait_ge(image_in[0], 16 * TILE_ROWS[0])
            gather_rest(0, 0)
            dve.wait_ge(adapt_in, 16)
            nc.vector.tensor_reduce(mix_s[:, 0:1], mix[:, :], AX.X, ALU.max).then_inc(mix_step, 1)
            dve.wait_ge(mix_step, MIX_MAX)
            nc.vector.tensor_scalar(mix[:, :], mix[:, :], mix_s[:, 0:1], None, ALU.subtract).then_inc(mix_step, 1)
            dve.wait_ge(coeff_in, 48)
            nc.vector.tensor_tensor(powers[:, N - 1, :], coeff[:, 0, :], coeff[:, 2, :], ALU.mult).then_inc(pow_ok, 1)
            have, steps = 1, 1
            while have < N:
                new = min(have, N - have)
                dve.wait_ge(pow_ok, steps)
                if steps > 1:
                    dve.wait_ge(q_squared, steps - 1)
                nc.vector.tensor_tensor(powers[:, N - have - new:N - have, :], powers[:, N - new:N, :],
                                        coeff[:, 1:2, :].to_broadcast([D, new, NDIM]), ALU.mult).then_inc(pow_ok, 1)
                have, steps = have + new, steps + 1
                if have < N:
                    dve.wait_ge(pow_ok, steps)
                    nc.vector.tensor_tensor(coeff[:, 1, :], coeff[:, 1, :], coeff[:, 1, :],
                                            ALU.mult).then_inc(q_squared, 1)
            dve.wait_ge(pow_ok, steps)
            nc.vector.tensor_reduce(resp[:, 0:N], powers[:, :, :], AX.X, ALU.add).then_inc(resp_rows, 1)
            dve.wait_ge(image_in[1], 16 * TILE_ROWS[1])
            gather_rest(0, 1)
            second_half(0, 0)
            gather_rest(1, 0)
            second_half(0, 1)
            gather_rest(1, 1)
            dve.wait_ge(w_in, 16 * W_LOADS)
            dve.wait_ge(rows_in, 16 * ROW_LOADS)
            for s in range(1, 5):
                if s > 1:
                    dve.wait_ge(w_sum, s - 1)
                nc.vector.tensor_tensor(w_src[:, 0, :, :], w_src[:, 0, :, :], w_src[:, s, :, :],
                                        ALU.add).then_inc(w_sum, 1)

            def moment(pc, k):
                t = 2 * pc + k
                nk = TILE_PARTS[k]
                dve.wait_ge(conv_ok, t + 1)
                nc.vector.bn_stats(stats[0:nk, k, :], ps_y[k][0:nk, 0:D]).then_inc(stats_ok, 1)
                dve.wait_ge(ones_ok, 2)
                dve.wait_ge(stats_ok, t + 1)
                nc.vector.bn_aggr(moments[0:nk, k, :], stats[0:nk, k, :]).then_inc(moments_ok, 1)
                dve.wait_ge(moments_ok, t + 1)
                nc.vector.tensor_scalar(rstd[0:nk, k:k + 1], moments[0:nk, k, 1:2], TOK_EPS, None,
                                        ALU.add).then_inc(rstd_ok, 1)

            def normalise(pc, k):
                t = 2 * pc + k
                dve.wait_ge(rstd_pow, t + 1)
                if not at_start(pc):
                    dve.wait_ge(normed_turned, t - 1)
                nk = TILE_PARTS[k]
                nc.vector.tensor_scalar(normed[k][0:nk, :], ps_y[k][0:nk, 0:D], moments[0:nk, k, 0:1],
                                        rstd[0:nk, k:k + 1], ALU.subtract, ALU.mult).then_inc(normed_ok, 1)

            def add_bias(pc, k):
                dve.wait_ge(dense_ok, 2 * pc + k + 1)
                if not at_start(pc):
                    dve.wait_ge(stored[k], 16 * pc)
                nk = TILE_PARTS[k]
                nc.vector.tensor_tensor(token[k][0:nk, :], ps_n[k][0:nk, D:2 * D], dense_b_row[0:nk, :],
                                        ALU.add).then_inc(token_ok, 1)

            moment(0, 0)
            dve.wait_ge(mix_step, MIX_EXP)
            nc.vector.tensor_reduce(mix_s[:, 1:2], mix[:, :], AX.X, ALU.add).then_inc(mix_step, 1)
            dve.wait_ge(mix_step, MIX_SUM)
            nc.vector.reciprocal(mix_s[:, 2:3], mix_s[:, 1:2]).then_inc(mix_step, 1)
            dve.wait_ge(mix_step, MIX_INV)
            nc.vector.tensor_scalar(mix[:, :], mix[:, :], mix_s[:, 2:3], None, ALU.mult).then_inc(mix_step, 1)
            dve.wait_ge(resp_rows, 2)
            dve.wait_ge(mix_step, MIX_OK)
            nc.vector.tensor_scalar(resp[:, 0:N], resp[:, 0:N], mix[:, 1:2], None,
                                    ALU.mult).then_inc(resp_ok, 1)

            second_half(1, 0)
            normalise(0, 0)
            gather_rest(2, 0)
            moment(0, 1)
            second_half(1, 1)
            normalise(0, 1)
            gather_rest(2, 1)
            moment(1, 0)
            dve.wait_ge(small_in, 64)
            with dve.Fori(2, G - 1) as pc:
                second_half(pc, 0)
                normalise(pc - 1, 0)
                add_bias(pc - 2, 0)
                gather_rest(pc + 1, 0)
                moment(pc - 1, 1)
                second_half(pc, 1)
                normalise(pc - 1, 1)
                add_bias(pc - 2, 1)
                gather_rest(pc + 1, 1)
                moment(pc, 0)
            second_half(G - 1, 0)
            normalise(G - 2, 0)
            add_bias(G - 3, 0)
            moment(G - 2, 1)
            second_half(G - 1, 1)
            normalise(G - 2, 1)
            add_bias(G - 3, 1)
            moment(G - 1, 0)
            normalise(G - 1, 0)
            add_bias(G - 2, 0)
            moment(G - 1, 1)
            normalise(G - 1, 1)
            add_bias(G - 2, 1)
            add_bias(G - 1, 0)
            add_bias(G - 1, 1)


HEADS, DK = 8, 16
HALF = HEADS // 2
CHUNK = 16
CHUNKS = D // CHUNK
QUARTERS = B // CHUNKS
FOURTH = CHUNK // QUARTERS
NDIM = 16
UNROLL = 8
MINE = 3 * B // 4
KPAD = 2 * N - 1

def attention(nc, h_dram, txt, wide, wout_sb, b_cols, bout_row, mix, response, r, fetch_experts):
    with ExitStack() as ctx:
        def sb(name, shape, dt=F32):
            return ctx.enter_context(nc.sbuf_tensor(name, shape, dt))

        def sem(name):
            return ctx.enter_context(nc.semaphore(name))

        xn = sb("xn", [N, B, D])
        ident = sb("ident_c", [PART, PART])
        bias = sb("bias", [N, D])
        mask = sb("mask", [N, N])
        head_of = sb("head_of", [D, HEADS])
        hankel = sb("hankel", [N, CHUNK, N])
        toeplitz = [sb(f"toeplitz{k}", [N, CHUNK, N]) for k in range(2)]
        st = sb("st", [N, B, 6])
        mean = sb("mean", [N, B])
        gap = sb("gap", [N, B])
        rstd = sb("rstd_c", [N, B])
        half = sb("half_c", [N, B])
        shift = sb("shift_c", [N, B])
        parts = ((0, B // 2), (B // 2, B))
        xr = [sb(f"xr{k}", [N, D]) for k in range(2)]
        xT = [sb(f"xT{k}", [D, N]) for k in range(2)]
        qT = sb("qT", [D, N])
        kx = sb("kx", [D, HEADS, N])
        vx = [sb(f"vx{k}", [N, HEADS, DK + 1]) for k in range(2)]
        prob = [sb(f"prob{k}", [N, HEADS, N]) for k in range(2)]
        top = [sb(f"top{k}", [N, HEADS]) for k in range(2)]
        probT = [sb(f"probT{k}", [N, HEADS, N]) for k in range(2)]
        inv = [sb(f"inv{k}", [N, HEADS]) for k in range(2)]
        on = [sb(f"on{k}", [N, D]) for k in range(2)]
        oT = [sb(f"oT{k}", [D, N]) for k in range(2)]

        def banks(name, n=1):
            return ctx.enter_context(nc.psum_tensor(name, [PART, n, 512], F32))
        ps_s = banks("ps_s", 2)
        ps_p = banks("ps_p", 2)
        ps_k, ps_x, ps_v, ps_o = banks("ps_k"), banks("ps_x"), banks("ps_v"), banks("ps_o")
        S = ps_s[0:N, :, 0:HALF * N].rearrange("p a (h j) -> p a h j", h=HALF)
        C = ps_k[0:N, 0, 128:128 + FOURTH * B].rearrange("p (e b) -> p e b", e=FOURTH)
        O = ps_o[0:N, 0, 0:HEADS * (DK + 1)].rearrange("p (h d) -> p h d", h=HEADS)
        OT = ps_o[:, 0, 160:160 + N]
        W = ps_o[0:N, 0, 256:256 + D]

        names = """setup_pool half_ok h_in h_rest bv_done bias_ok bias_w r_base st_ok
            m_gap m_ok var_ok rstd_ok shift_ok xn_ok xn_rest hankel_in toeplitz_ok cema_done cema_added
            xr_ok x_turned xT_ok k_done q_done v_done q_ok k_ok v_ok s_half s_done s_masked s_max s_sub p_ok p_turned pT_ok
            o_done o_inv o_ok o_turned oT_ok w_done r_ok vx_one""".split()
        q = {n: sem("c_" + n) for n in names}
        block = ctx.enter_context(nc.Block())

        SETUP_POOL = 7

        @block.sync
        def _(sp):
            for (lo, hi), name in zip(parts, ("h_in", "h_rest")):
                sp.dma_start(xn[0:PATCHES, lo:hi, :], h_dram[lo:hi].rearrange("b n d -> n b d")).then_inc(q[name], 16)
                sp.dma_start(xn[PATCHES:N, lo:hi, :], txt[lo:hi].rearrange("b n d -> n b d")).then_inc(q[name], 16)
            for c in range(CHUNKS):
                if c >= 1:
                    sp.wait_ge(q["toeplitz_ok"], c)
                start = response[c * CHUNK:c * CHUNK + 1, 0:1]
                sp.dma_start(hankel[:, :, :], bass.AP(start.tensor, start.offset, [[1, N], [KPAD, CHUNK], [1, N]])
                             ).then_inc(q["hankel_in"], 16)
                fetch_experts(sp, c)

        @block.scalar
        def _(act):
            def reverse(c, k, first=False):
                act.wait_ge(q["hankel_in"], 16 * c + 16)
                if not first:
                    act.wait_ge(q["cema_done"], QUARTERS * (c - 1))
                nc.scalar.copy(toeplitz[k][:, :, :], strided(hankel[:, 0, N - 1:N], [[N, CHUNK], [-1, N]])
                               ).then_inc(q["toeplitz_ok"], 1)

            def x_out(f, u, first):
                act.wait_ge(q["x_turned"], f + 1)
                if not first:
                    act.wait_ge(q["v_done"], f - 1)
                nc.scalar.copy(xT[u][:, :], ps_x[:, 0, 0:N]).then_inc(q["xT_ok"], 1)

            def q_out(f, fresh):
                act.wait_ge(q["q_done"], f + 1)
                if not fresh:
                    act.wait_ge(q["s_done"], f)
                nc.scalar.activation(qT[:, :], ps_x[:, 0, N:2 * N], ACT.Identity, bias=b_cols[:, 0:1]
                                     ).then_inc(q["q_ok"], 1)

            def v_out(f, u, first):
                act.wait_ge(q["v_done"], f + 1)
                if not first:
                    act.wait_ge(q["o_done"], f - 1)
                nc.scalar.copy(vx[u][:, :, 0:DK],
                               ps_v[0:N, 0, 0:D].rearrange("p (h d) -> p h d", h=HEADS)).then_inc(q["v_ok"], 1)

            def exponent(i, u):
                act.wait_ge(q["s_sub"], i + 1)
                nc.scalar.activation(prob[u][:, :, :], prob[u][:, :, :], ACT.Exp).then_inc(q["p_ok"], 1)

            def probs_out(i, u, first):
                for hf in range(2):
                    act.wait_ge(q["p_turned"], 2 * i + 1 + hf)
                    if not first:
                        act.wait_ge(q["o_done"], i - 1)
                    nc.scalar.copy(probT[u][:, HALF * hf:HALF * hf + HALF, :],
                                   ps_p[0:N, hf, 0:HALF * N].rearrange("p (h j) -> p h j", h=HALF)
                                   ).then_inc(q["pT_ok"], 1)

            def o_out(i, u, first):
                act.wait_ge(q["o_turned"], i + 1)
                if not first:
                    act.wait_ge(q["w_done"], i - 1)
                nc.scalar.copy(oT[u][:, :], OT).then_inc(q["oT_ok"], 1)

            def step(i, u, first=False, front=True, following=True):
                if front:
                    x_out(i + 2, u, False)
                probs_out(i, u, first)
                if front:
                    q_out(i + 2, False)
                if following:
                    exponent(i + 1, 1 - u)
                if front:
                    v_out(i + 2, u, False)
                o_out(i, u, first)

            def begin(f):
                x_out(f, f, True)
                q_out(f, f == 0)
                v_out(f, f, True)
            reverse(0, 0, first=True)
            begin(0)
            act.wait_ge(q["r_base"], 2)
            act.wait_ge(q["shift_ok"], 1)
            with act.Fori(MINE // UNROLL, B // UNROLL) as j:
                for u in range(UNROLL):
                    here = bass.ds(UNROLL * j + u, 1)
                    x = xn[:, here, :].rearrange("p o d -> p (o d)")
                    nc.scalar.activation(x, x, ACT.Identity, bias=shift[:, here], scale=rstd[:, here]
                                         ).then_inc(q["xn_rest"], 1)
            begin(1)
            exponent(0, 0)

            def chunk(c, k, last=False):
                for m in range(QUARTERS):
                    i, u = QUARTERS * c + m, m % 2
                    ends = last and m >= QUARTERS - 2
                    step(i, u, first=isinstance(c, int) and c == 0 and m < 2, front=not ends,
                         following=not (last and m == QUARTERS - 1))
                    if m == 1 and not last:
                        reverse(c + 1, 1 - k, first=isinstance(c, int) and c == 0)
            chunk(0, 0)
            chunk(1, 1)
            with act.Fori(1, CHUNKS // 2 - 1) as j:
                for k in range(2):
                    chunk(2 * j + k, k)
            chunk(CHUNKS - 2, 0)
            chunk(CHUNKS - 1, 1, last=True)

        @block.gpsimd
        def _(pool):
            nc.gpsimd.memset(ident[:, :], 0.0).then_inc(q["setup_pool"], 1)
            nc.gpsimd.memset(mask[:, :], DK ** -0.5).then_inc(q["setup_pool"], 1)
            nc.gpsimd.memset(head_of[:, :], 1.0).then_inc(q["setup_pool"], 1)
            nc.gpsimd.memset(half[:, :], -0.5).then_inc(q["half_ok"], 1)
            pool.wait_ge(q["setup_pool"], 3)
            nc.gpsimd.affine_select(out=head_of[:, :], in_=head_of[:, :], compare_op=ALU.is_ge, fill=0.0,
                                    base=0, pattern=[[-DK, HEADS]], channel_multiplier=1).then_inc(q["setup_pool"], 1)
            nc.gpsimd.affine_select(out=ident[:, :], in_=ident[:, :], compare_op=ALU.not_equal, fill=1.0,
                                    base=0, pattern=[[-1, PART]], channel_multiplier=1).then_inc(q["setup_pool"], 1)
            nc.gpsimd.affine_select(out=mask[:, :], in_=mask[:, :], compare_op=ALU.is_ge, fill=0.0,
                                    base=0, pattern=[[-1, N]], channel_multiplier=1).then_inc(q["setup_pool"], 1)
            pool.wait_ge(q["setup_pool"], 6)
            nc.gpsimd.affine_select(out=head_of[:, :], in_=head_of[:, :], compare_op=ALU.is_ge, fill=0.0,
                                    base=DK - 1, pattern=[[DK, HEADS]], channel_multiplier=-1
                                    ).then_inc(q["setup_pool"], 1)
            pool.wait_ge(q["bias_w"], 1)
            for (lo, hi), name in zip(parts, ("h_in", "h_rest")):
                pool.wait_ge(q[name], 32)
                nc.gpsimd.tensor_tensor(r[:, lo:hi, :], xn[:, lo:hi, :],
                                        bias[:, :].unsqueeze(1).to_broadcast([N, hi - lo, D]),
                                        ALU.add).then_inc(q["r_base"], 1)
            rstds(pool, nc, rstd, half, q, parts)

            def fetch(f, u, first):
                if not first:
                    pool.wait_ge(q["x_turned"], f - 1)
                nc.gpsimd.tensor_copy(xr[u][:, :], xn[:, bass.ds(f, 1), :].rearrange("p o d -> p (o d)")
                                      ).then_inc(q["xr_ok"], 1)

            def subtract(f, u):
                pool.wait_ge(q["s_max"], f + 1)
                nc.gpsimd.tensor_tensor(prob[u][:, :, :], prob[u][:, :, :],
                                        top[u][:, :].unsqueeze(2).to_broadcast([N, HEADS, N]),
                                        ALU.subtract).then_inc(q["s_sub"], 1)
            pool.wait_ge(q["xn_ok"], 2)
            fetch(0, 0, True)
            fetch(1, 1, True)
            pool.wait_ge(q["xn_ok"], MINE)
            pool.wait_ge(q["xn_rest"], B - MINE)
            subtract(0, 0)
            fetch(2, 0, False)
            subtract(1, 1)
            fetch(3, 1, False)
            with pool.Fori(1, B // 2 - 1) as j:
                for u in range(2):
                    subtract(2 * j + u, u)
                    fetch(2 * j + 2 + u, u, False)
            subtract(B - 2, 0)
            subtract(B - 1, 1)

        @block.tensor
        def _(pe):
            pe.matmul(ps_x[0:N, 0, 0:D], b_cols[:, 2:3].to_broadcast([D, N]), wout_sb[:, :],
                      start=True, stop=True).then_inc(q["bv_done"], 1)
            pe.wait_ge(q["bias_ok"], 1)
            pe.wait_ge(q["setup_pool"], SETUP_POOL)

            def turn_x(f, u):
                pe.wait_ge(q["xr_ok"], f + 1)
                pe.transpose(ps_x[:, 0, 0:N], xr[u][:, :], ident[0:N, 0:N]).then_inc(q["x_turned"], 1)

            def cema(i, c, m, k, first):
                if m == 0:
                    pe.wait_ge(q["toeplitz_ok"], c + 1)
                if not first:
                    pe.wait_ge(q["cema_added"], i)
                for e in range(FOURTH):
                    at = FOURTH * m + e
                    mm = pe.matmul(C[:, e, :], toeplitz[k][:, at, :],
                                   xn[:, :, bass.ds(c * CHUNK + at, 1)].rearrange("p b o -> p (b o)"),
                                   start=(e == 0), stop=(e == FOURTH - 1), skip_group_check=True)
                mm.then_inc(q["cema_done"], 1)

            def project(f, u, first):
                pe.wait_ge(q["xT_ok"], f + 1)
                pe.matmul(ps_k[:, 0, 0:N], wide[:, D:2 * D], xT[u][:, :], start=True, stop=True
                          ).then_inc(q["k_done"], 1)
                pe.matmul(ps_x[:, 0, N:2 * N], wide[:, 0:D], xT[u][:, :], start=True, stop=True
                          ).then_inc(q["q_done"], 1)
                if not first:
                    pe.wait_ge(q["v_ok"], f)
                pe.matmul(ps_v[0:N, 0, 0:D], xT[u][:, :], wide[:, 2 * D:3 * D], start=True,
                          stop=True).then_inc(q["v_done"], 1)

            def scores(f, a, first):
                if a == 0:
                    pe.wait_ge(q["q_ok"], f + 1)
                    pe.wait_ge(q["k_ok"], f + 1)
                    if not first:
                        pe.wait_ge(q["s_masked"], f)
                pe.matmul(ps_s[0:N, a, 0:HALF * N], qT[:, :], kx[:, HALF * a:HALF * a + HALF, :].rearrange(
                    "p h j -> p (h j)"), start=True, stop=True).then_inc(q["s_done" if a else "s_half"], 1)

            def turn_probs(i, u):
                pe.wait_ge(q["p_ok"], i + 1)
                for hf in range(2):
                    for hh in range(HALF):
                        mm = pe.transpose(ps_p[0:N, hf, N * hh:N * hh + N], prob[u][:, HALF * hf + hh, :],
                                          ident[0:N, 0:N])
                    mm.then_inc(q["p_turned"], 1)

            def weigh(i, u, first):
                pe.wait_ge(q["v_ok"], i + 1)
                pe.wait_ge(q["pT_ok"], 2 * i + 2)
                if not first:
                    pe.wait_ge(q["r_ok"], i)
                for hd in range(HEADS):
                    mm = pe.matmul(O[:, hd, :], probT[u][:, hd, :], vx[u][:, hd, :], start=(hd == 0),
                                   stop=(hd == HEADS - 1), skip_group_check=True)
                mm.then_inc(q["o_done"], 1)

            def turn_o(i, u):
                pe.wait_ge(q["o_ok"], i + 1)
                pe.transpose(OT, on[u][:, :], ident[0:N, 0:N]).then_inc(q["o_turned"], 1)

            def project_out(i, u):
                pe.wait_ge(q["oT_ok"], i + 1)
                pe.matmul(W, oT[u][:, :], wout_sb[:, :], start=True, stop=True).then_inc(q["w_done"], 1)

            def step(i, u, c, m, k, front=True):
                if front:
                    turn_x(i + 2, u)
                turn_probs(i, u)
                cema(i, c, m, k, isinstance(i, int) and i == 0)
                if front:
                    project(i + 2, u, False)
                weigh(i, u, isinstance(i, int) and i == 0)
                if front:
                    scores(i + 2, 0, False)
                turn_o(i, u)
                if front:
                    scores(i + 2, 1, False)
                project_out(i, u)

            def chunk(c, k, last=False):
                for m in range(QUARTERS):
                    step(QUARTERS * c + m, m % 2, c, m, k, front=not (last and m >= QUARTERS - 2))
            for u in range(2):
                turn_x(u, u)
                project(u, u, u == 0)
                for a in range(2):
                    scores(u, a, u == 0)
            pe.wait_ge(q["xn_ok"], MINE)
            pe.wait_ge(q["xn_rest"], B - MINE)
            chunk(0, 0)
            chunk(1, 1)
            with pe.Fori(1, CHUNKS // 2 - 1) as j:
                for k in range(2):
                    chunk(2 * j + k, k)
            chunk(CHUNKS - 2, 0)
            chunk(CHUNKS - 1, 1, last=True)

        @block.vector
        def _(dve):
            for u in range(2):
                nc.vector.memset(vx[u][:, :, DK:DK + 1], 1.0).then_inc(q["vx_one"], 1)
            dve.wait_ge(q["bv_done"], 1)
            nc.vector.tensor_tensor(bias[:, :], ps_x[0:N, 0, 0:D], bout_row[:, :], ALU.add).then_inc(q["bias_ok"], 1)
            dve.wait_ge(q["bias_ok"], 1)
            nc.vector.tensor_scalar(bias[:, :], bias[:, :], mix[0:N, 0:1], None, ALU.mult).then_inc(q["bias_w"], 1)
            def add_cema(i, c, m, first):
                dve.wait_ge(q["cema_done"], i + 1)
                if not first:
                    dve.wait_ge(q["r_ok"], i)
                at = r[:, :, bass.ds(c * CHUNK + FOURTH * m, FOURTH)]
                nc.vector.tensor_tensor(at, C.rearrange("p e b -> p b e"), at, ALU.add).then_inc(q["cema_added"], 1)

            def spread_keys(f, fresh):
                dve.wait_ge(q["k_done"], f + 1)
                if not fresh:
                    dve.wait_ge(q["s_done"], f)
                nc.vector.scalar_tensor_tensor(
                    out=kx[:, :, :], in0=ps_k[:, 0:1, 0:N].to_broadcast([D, HEADS, N]), scalar=b_cols[:, 1:2],
                    in1=head_of[:, :].unsqueeze(2).to_broadcast([D, HEADS, N]), op0=ALU.add, op1=ALU.mult
                ).then_inc(q["k_ok"], 1)

            def mask_scores(f, u, first):
                dve.wait_ge(q["s_done"], f + 1)
                if not first:
                    dve.wait_ge(q["p_turned"], 2 * f - 2)
                nc.vector.tensor_tensor(prob[u][:, :, :].rearrange("p (a h) j -> p a h j", a=2), S,
                                        strided(mask[:, :], [[0, 2], [0, HALF], [1, N]]), ALU.mult
                                        ).then_inc(q["s_masked"], 1)

            def maxima(f, u, first):
                dve.wait_ge(q["s_masked"], f + 1)
                if not first:
                    dve.wait_ge(q["s_sub"], f - 1)
                nc.vector.tensor_reduce(top[u][:, :], prob[u][:, :, :], AX.X, ALU.max).then_inc(q["s_max"], 1)

            def normalise(i, u, first):
                dve.wait_ge(q["o_done"], i + 1)
                nc.vector.reciprocal(inv[u][:, :], O[:, :, DK]).then_inc(q["o_inv"], 1)
                dve.wait_ge(q["o_inv"], i + 1)
                if not first:
                    dve.wait_ge(q["o_turned"], i - 1)
                nc.vector.tensor_tensor(on[u][:, :].rearrange("p (h d) -> p h d", h=HEADS), O[:, :, 0:DK],
                                        inv[u][:, :].unsqueeze(2).to_broadcast([N, HEADS, DK]), ALU.mult
                                        ).then_inc(q["o_ok"], 1)

            def accumulate(i):
                at = r[:, bass.ds(i, 1), :].rearrange("p o d -> p (o d)")
                dve.wait_ge(q["w_done"], i + 1)
                dve.wait_ge(q["cema_added"], i + 1)
                nc.vector.scalar_tensor_tensor(out=at, in0=W, scalar=mix[0:N, 0:1], in1=at, op0=ALU.mult,
                                               op1=ALU.add).then_inc(q["r_ok"], 1)

            def step(i, u, c, m, first=False, front=True):
                if front:
                    spread_keys(i + 2, False)
                add_cema(i, c, m, isinstance(i, int) and i == 0)
                normalise(i, u, first)
                if front:
                    mask_scores(i + 2, u, False)
                accumulate(i)
                if front:
                    maxima(i + 2, u, False)

            def chunk(c, last=False):
                for m in range(QUARTERS):
                    step(QUARTERS * c + m, m % 2, c, m, first=isinstance(c, int) and c == 0 and m < 2,
                         front=not (last and m >= QUARTERS - 2))
            variances(dve, nc, xn, st, mean, gap, rstd, q, parts, ("h_in", "h_rest"))
            dve.wait_ge(q["r_base"], 2)
            dve.wait_ge(q["rstd_ok"], 1)

            def centre(j):
                for u in range(UNROLL):
                    here = bass.ds(UNROLL * j + u, 1)
                    x = xn[:, here, :].rearrange("p o d -> p (o d)")
                    nc.vector.tensor_scalar(x, x, mean[:, here], rstd[:, here],
                                            ALU.subtract, ALU.mult).then_inc(q["xn_ok"], 1)
            centre(0)
            shifts(dve, nc, shift, mean, rstd, q, 1, MINE, B)
            for j in range(1, MINE // UNROLL - 1):
                centre(j)
            dve.wait_ge(q["setup_pool"], SETUP_POOL)
            spread_keys(0, True)
            centre(MINE // UNROLL - 1)
            mask_scores(0, 0, True)
            maxima(0, 0, True)
            spread_keys(1, False)
            mask_scores(1, 1, True)
            maxima(1, 1, True)

            chunk(0)
            with dve.Fori(1, CHUNKS - 1) as c:
                chunk(c)
            chunk(CHUNKS - 1, last=True)


def variances(dve, nc, x, st, mean, gap, rstd, q, parts, loaded=(), done=0):
    for n, (lo, hi) in enumerate(parts, done):
        if loaded:
            dve.wait_ge(q[loaded[n - done]], 32)
        with dve.Fori(lo // UNROLL, hi // UNROLL) as j:
            for u in range(UNROLL):
                here = bass.ds(UNROLL * j + u, 1)
                nc.vector.bn_stats(st[:, here, :].rearrange("p o s -> p (o s)"),
                                   x[:, here, :].rearrange("p o d -> p (o d)")).then_inc(q["st_ok"], 1)
        c = slice(lo, hi)
        dve.wait_ge(q["st_ok"], hi)
        nc.vector.tensor_tensor(mean[:, c], st[:, c, 1], st[:, c, 4], ALU.add).then_inc(q["m_gap"], 1)
        nc.vector.tensor_tensor(gap[:, c], st[:, c, 1], st[:, c, 4], ALU.subtract).then_inc(q["m_gap"], 1)
        nc.vector.tensor_tensor(rstd[:, c], st[:, c, 2], st[:, c, 5], ALU.add).then_inc(q["m_gap"], 1)
        dve.wait_ge(q["m_gap"], 3 * n + 3)
        nc.vector.tensor_scalar(mean[:, c], mean[:, c], 0.5, None, ALU.mult).then_inc(q["m_ok"], 1)
        nc.vector.scalar_tensor_tensor(out=gap[:, c], in0=gap[:, c], scalar=0.25, in1=gap[:, c], op0=ALU.mult,
                                       op1=ALU.mult).then_inc(q["m_ok"], 1)
        nc.vector.tensor_scalar(rstd[:, c], rstd[:, c], 1.0 / D, LN_EPS, ALU.mult, ALU.add).then_inc(q["m_ok"], 1)
        dve.wait_ge(q["m_ok"], 3 * n + 3)
        nc.vector.tensor_tensor(rstd[:, c], rstd[:, c], gap[:, c], ALU.add).then_inc(q["var_ok"], 1)


def rstds(pool, nc, rstd, half, q, parts):
    pool.wait_ge(q["half_ok"], 1)
    for n, (lo, hi) in enumerate(parts):
        pool.wait_ge(q["var_ok"], n + 1)
        nc.gpsimd.tensor_tensor(rstd[:, lo:hi], rstd[:, lo:hi], half[:, lo:hi], ALU.pow).then_inc(q["rstd_ok"], 1)


def shifts(dve, nc, shift, mean, rstd, q, n, lo, hi):
    dve.wait_ge(q["rstd_ok"], n + 1)
    nc.vector.scalar_tensor_tensor(out=shift[:, lo:hi], in0=mean[:, lo:hi], scalar=-1.0, in1=rstd[:, lo:hi],
                                   op0=ALU.mult, op1=ALU.mult).then_inc(q["shift_ok"], 1)


GROUPS, EXPERTS = 8, 8
GE = GROUPS * EXPERTS
GATES_OUT = GROUPS + GE
HID = 2 * D
TOKENS = B * N
PICKS = 4
QUAD = 4
QUADS = B // QUAD
QUAD_STORES = 16 * QUAD * PICKS
REGION = TOKENS
SLOT = D + 2
TILE = 128
TILES = (PICKS * TOKENS + GE * (TILE - 1)) // TILE
PACK = 4
SKIP = float(1 << 20)
BF16 = mybir.dt.bfloat16
BIG = 3.0e38

(TOP1, BELOW1, RANK1, FIRST1, HOT1, LEFT, TOP2, BELOW2, RANK2, FIRST2, HOT2, MARGIN, ODDS, PART1, PART2,
 EITHER, CHOSEN, SPLIT0, SPLIT1, SPLIT, GATES, SHARE0, SHARE1, SHARES, SLOTS, SORT0, SORT1,
 BY_GROUP, PICKED0, PICKED1, SLOT_OF, PLACE, WEIGHT, SLOT_INT, ADDED, RUNNING, RESULT) = range(1, 38)
ROUTE_STEPS = RESULT


def route(nc, r, g1, g2, b2, slots_dram, tab_base, tab_expert, tab_skip):
    with ExitStack() as ctx:
        def sb(name, shape, dt=F32):
            return ctx.enter_context(nc.sbuf_tensor(name, shape, dt))

        def sem(name):
            return ctx.enter_context(nc.semaphore(name))

        def bank(name, dt=F32):
            return ctx.enter_context(nc.psum_tensor(name, [PART, 2048 // (4 if dt == F32 else 2)], dt))

        ident = sb("ident_d", [PART, PART])
        gate_w = sb("gate_w", [D, GROUPS + GE])
        b2_sb = sb("b2_sb", [GE, D])
        st = sb("st_d", [N, B, 6])
        mean = sb("mean_d", [N, B])
        gap = sb("gap_d", [N, B])
        rstd = sb("rstd_d", [N, B])
        half = sb("half_d", [N, B])
        shift = sb("shift", [N, B])
        parts = ((0, 2 * QUAD), (2 * QUAD, B // 2), (B // 2, B))
        xn = sb("xn_d", [N, QUAD, D])
        rows = [sb(f"rows{k}", [N, QUAD, PICKS, SLOT]) for k in range(2)]
        xT = [sb(f"xT_d{k}", [D, QUAD * N]) for k in range(2)]
        place = sb("place", [N, B, PICKS])
        order = sb("order", [N, EXPERTS])
        region = sb("region", [N, GE])
        before = sb("before", [N, N], BF16)
        ones_b = sb("ones_b", [N, N], BF16)
        ones_f = sb("ones_f", [N, 1])
        top = sb("top_d", [N, 2, QUAD, 9])
        below = sb("below", [N, QUAD, 9, EXPERTS])
        ranked = sb("ranked", [N, QUAD, 9, EXPERTS])
        left = sb("left", [N, QUAD, 9, EXPERTS])
        winner = sb("winner", [N, 2, QUAD, 9])
        hot = sb("hot", [N, 2, QUAD, 9, EXPERTS])
        margin = sb("margin", [N, QUAD, 9])
        odds = sb("odds", [N, QUAD, 9])
        part = sb("part", [N, 2, QUAD, 9])
        either = sb("either", [N, QUAD, 9, EXPERTS])
        chosen = sb("chosen", [N, QUAD, GE], BF16)
        split = sb("split", [N, 2, QUAD, 9, EXPERTS])
        share = sb("share", [N, 2, 2, QUAD, GROUPS])
        gates = [sb(f"gates{k}", [N, QUAD, GE]) for k in range(2)]
        gates_T = [sb(f"gates_T{k}", [GE, QUAD * N]) for k in range(2)]
        slot_row = sb("slot_row", [N, QUAD, GE])
        by_expert = sb("by_expert", [N, 2, QUAD, GE])
        by_group = sb("by_group", [N, 2, QUAD, GROUPS])
        picked = sb("picked", [N, 2, 2, QUAD, GROUPS])
        slot_f = sb("slot_f", [N, PICKS, QUAD])
        shares = sb("shares", [N, PICKS, QUAD])
        slot = [sb(f"slot{k}", [N, PICKS, QUAD], I32) for k in range(2)]
        added_f = sb("added_f", [N, GE])
        running = sb("running", [N, GE], BF16)
        blank = sb("blank", [PART, SLOT])
        count = sb("count", [GE, 1])
        count_i = sb("count_i", [GE, 1], I32)
        tiles = sb("tiles", [GE, 1])
        upto = sb("upto", [GE, GE])
        bounds = sb("bounds", [GE, 2])
        tile_no = sb("tile_no", [GE, TILES])
        began = sb("began", [GE, TILES])
        mine = sb("mine", [GE, TILES])
        facts = sb("facts", [GE, 5])
        tile_of = sb("tile_of", [PART, TILES])
        at = sb("at", [PART, TILES])
        rel = sb("rel", [PART, TILES])
        unused = sb("unused", [PART, TILES])
        lane = sb("lane", [PART, 1])
        digit = sb("digit", [1, PACK])
        numbers = sb("numbers", [1, TILES // PACK, PACK])
        words = sb("words", [1, TILES // PACK])

        ps_x, ps_r, ps_g, ps_b = bank("ps_dx"), bank("ps_dr"), bank("ps_dg"), bank("ps_db")
        ps_l = [bank(f"ps_dl{k}") for k in range(2)]
        ps_f = [bank(f"ps_df{k}") for k in range(2)] + [ps_x]

        names = """pool_base pool_ok half_ok blank_ok blank_base blank_out gates_in b2_in st_ok m_gap m_ok var_ok rstd_ok
            shift_ok running_zero x_part x_ok row_part rows_ok x_turned xT_ok logits odds_exp ranks gates_turned gates_T_ok result
            route_step counted count_ok tiles_ok ends mine_ok spread table_step scattered0 scattered1""".split()
        q = {n: sem("d_" + n) for n in names}
        scattered = [q["scattered0"], q["scattered1"]]
        block = ctx.enter_context(nc.Block())
        POOL_SETUP = 12 + PACK

        @block.sync
        def _(sp):
            sp.dma_start(gate_w[:, 0:GROUPS], g1).then_inc(q["gates_in"], 16)
            sp.dma_start(gate_w[:, GROUPS:].rearrange("d (g e) -> d g e", g=GROUPS),
                         g2.rearrange("g d e -> d g e")).then_inc(q["gates_in"], 16)
            sp.dma_start(b2_sb[:, :], b2.rearrange("g e d -> (g e) d")).then_inc(q["b2_in"], 16)
            sp.wait_ge(q["blank_ok"], 1)
            sp.dma_start(slots_dram.rearrange("(e p) f -> p e f", p=REGION)[0:PART],
                         blank[:, :].unsqueeze(1).to_broadcast([PART, GE + 1, SLOT])).then_inc(q["blank_out"], 16)
            sp.wait_ge(q["blank_out"], 16)

        @block.gpsimd
        def _(pool):
            def setup(inst):
                inst.then_inc(q["pool_ok"], 1)
            nc.gpsimd.memset(blank[:, :], 0.0).then_inc(q["blank_base"], 1)
            nc.gpsimd.memset(ident[:, :], 0.0).then_inc(q["pool_base"], 1)
            nc.gpsimd.memset(before[:, :], 1.0).then_inc(q["pool_base"], 1)
            nc.gpsimd.memset(upto[:, :], 1.0).then_inc(q["pool_base"], 1)
            nc.gpsimd.memset(half[:, :], -0.5).then_inc(q["half_ok"], 1)
            pool.wait_ge(q["blank_base"], 1)
            nc.gpsimd.memset(blank[:, D:D + 1], SKIP).then_inc(q["blank_ok"], 1)
            pool.wait_ge(q["pool_base"], 3)
            setup(nc.gpsimd.affine_select(out=ident[:, :], in_=ident[:, :], compare_op=ALU.not_equal, fill=1.0,
                                             base=0, pattern=[[-1, PART]], channel_multiplier=1))
            setup(nc.gpsimd.affine_select(out=before[:, :], in_=before[:, :], compare_op=ALU.is_gt, fill=0.0,
                                             base=0, pattern=[[1, N]], channel_multiplier=-1))
            setup(nc.gpsimd.affine_select(out=upto[:, :], in_=upto[:, :], compare_op=ALU.is_ge, fill=0.0,
                                             base=0, pattern=[[1, GE]], channel_multiplier=-1))
            setup(nc.gpsimd.memset(ones_b[:, :], 1.0))
            setup(nc.gpsimd.memset(ones_f[:, :], 1.0))
            setup(nc.gpsimd.iota(place[:, :, :], pattern=[[N, B], [TOKENS, PICKS]], base=0, channel_multiplier=1,
                                    allow_small_or_imprecise_dtypes=True))
            setup(nc.gpsimd.iota(order[:, :], pattern=[[-1, EXPERTS]], base=EXPERTS, channel_multiplier=0,
                                    allow_small_or_imprecise_dtypes=True))
            setup(nc.gpsimd.iota(region[:, :], pattern=[[REGION, GE]], base=0, channel_multiplier=0,
                                    allow_small_or_imprecise_dtypes=True))
            setup(nc.gpsimd.iota(tile_no[:, :], pattern=[[1, TILES]], base=0, channel_multiplier=0,
                                    allow_small_or_imprecise_dtypes=True))
            setup(nc.gpsimd.iota(tile_of[:, :], pattern=[[TILE, TILES]], base=0, channel_multiplier=0,
                                    allow_small_or_imprecise_dtypes=True))
            setup(nc.gpsimd.iota(lane[:, :], pattern=[[0, 1]], base=0, channel_multiplier=1,
                                     allow_small_or_imprecise_dtypes=True))
            setup(nc.gpsimd.memset(facts[:, 0:1], 1.0))
            for k in range(PACK):
                setup(nc.gpsimd.memset(digit[:, k:k + 1], float(GE ** k)))
            rstds(pool, nc, rstd, half, q, parts)

            def scatter(t, u):
                pool.wait_ge(q["rows_ok"], t + 1)
                pool.wait_ge(q["route_step"], slots_known)
                pool.reg_add(slots_known, slots_known, ROUTE_STEPS)
                for b in range(QUAD):
                    for k in range(PICKS):
                        nc.gpsimd.indirect_dma_start(
                            out=slots_dram, out_offset=bass.IndirectOffsetOnAxis(ap=slot[u][:, k, b:b + 1], axis=0),
                            in_=rows[u][:, b, k, :], in_offset=None).then_inc(scattered[u], 16)
            slots_known = pool.alloc_register("slots_known")
            pool.reg_mov(slots_known, SLOT_INT)
            pool.wait_ge(q["blank_out"], 16)
            with pool.Fori(0, QUADS // 2) as j:
                for u in range(2):
                    scatter(2 * j + u, u)
            for u in range(2):
                pool.wait_ge(scattered[u], QUAD_STORES * QUADS // 2)

        @block.scalar
        def _(act):
            def normalise(t, u, first):
                if first:
                    act.wait_ge(q["shift_ok"], 1)
                elif isinstance(t, int):
                    if QUAD * t == parts[1][0]:
                        act.wait_ge(q["shift_ok"], 2)
                    act.wait_ge(q["x_turned"], t)
                else:
                    act.wait_ge(q["x_turned"], turned)
                    act.reg_add(turned, turned, 1)
                for b in range(QUAD):
                    i = bass.ds(QUAD * t + b, 1)
                    nc.scalar.activation(xn[:, b, :], r[:, i, :].rearrange("p o d -> p (o d)"), ACT.Identity,
                                         bias=shift[:, i], scale=rstd[:, i]
                                         ).then_inc(q["x_ok" if b == QUAD - 1 else "x_part"], 1)
                act.wait_ge(q["x_turned"], t + 1)
                if not (isinstance(t, int) and t < 2):
                    act.wait_ge(q["logits"], t - 1)
                nc.scalar.copy(xT[u][:, :], ps_x[:, 0:QUAD * N]).then_inc(q["xT_ok"], 1)

            def step(t, u, first, following=True):
                if following:
                    normalise(t + 1, 1 - u, False)
                act.wait_ge(q["route_step"], ROUTE_STEPS * t + MARGIN)
                nc.scalar.activation(odds[:, :, :], margin[:, :, :], ACT.Exp).then_inc(q["odds_exp"], 1)
                if isinstance(t, int) and not first:
                    act.wait_ge(scattered[u], QUAD_STORES // 2 * (t - u))
                elif not first:
                    act.wait_ge(scattered[u], written[u])
                    act.reg_add(written[u], written[u], QUAD_STORES)
                for b in range(QUAD):
                    i = bass.ds(QUAD * t + b, 1)
                    nc.scalar.activation(rows[u][:, b, :, 0:D], r[:, i, :].to_broadcast([N, PICKS, D]), ACT.Identity,
                                         bias=shift[:, i], scale=rstd[:, i]
                                         ).then_inc(q["rows_ok" if b == QUAD - 1 else "row_part"], 1)
                act.wait_ge(q["gates_turned"], t + 1)
                if not first:
                    act.wait_ge(q["result"], t - 1)
                nc.scalar.copy(gates_T[u][:, :], ps_g[0:GE, 0:QUAD * N]).then_inc(q["gates_T_ok"], 1)
            turned = act.alloc_register("turned")
            act.reg_mov(turned, 3)
            written = [act.alloc_register(f"written{k}") for k in range(2)]
            for u in range(2):
                act.reg_mov(written[u], QUAD_STORES)
            normalise(0, 0, True)
            for u in range(2):
                step(u, u, True)
            with act.Fori(1, QUADS // 2 - 1) as j:
                for u in range(2):
                    step(2 * j + u, u, False)
            step(QUADS - 2, 0, False)
            step(QUADS - 1, 1, False, following=False)

        @block.tensor
        def _(pe):
            pe.wait_ge(q["pool_ok"], POOL_SETUP)
            pe.wait_ge(q["gates_in"], 32)
            pe.wait_ge(q["b2_in"], 16)
            gates_known = pe.alloc_register("gates_known")
            pe.reg_mov(gates_known, GATES)

            def logits(t, u):
                pe.wait_ge(q["x_ok"], t + 1)
                for b in range(QUAD):
                    mm = pe.transpose(ps_x[:, N * b:N * b + N], xn[:, b, :], ident[0:N, 0:N])
                mm.then_inc(q["x_turned"], 1)
                pe.wait_ge(q["xT_ok"], t + 1)
                for b in range(QUAD):
                    mm = pe.matmul(ps_l[u][0:N, GATES_OUT * b:GATES_OUT * (b + 1)],
                                   xT[u][:, N * b:N * b + N], gate_w[:, :],
                                   start=(b == 0), stop=(b == QUAD - 1), skip_group_check=True)
                mm.then_inc(q["logits"], 1)

            def step(t, u, following=True):
                if following:
                    logits(t + 1, 1 - u)
                pe.wait_ge(q["route_step"], ROUTE_STEPS * t + CHOSEN)
                for b in range(QUAD):
                    out = ps_r[0:N, GE * b:GE * b + GE]
                    pe.matmul(out, before[:, :], chosen[:, b, :], start=(b == 0), stop=False, skip_group_check=True)
                    for c in range(b):
                        pe.matmul(out, ones_b[:, :], chosen[:, c, :], start=False, stop=False, skip_group_check=True)
                    mm = pe.matmul(out, ones_b[:, :], running[:, :], start=False, stop=(b == QUAD - 1),
                                   skip_group_check=True)
                mm.then_inc(q["ranks"], 1)
                if isinstance(t, int):
                    pe.wait_ge(q["route_step"], ROUTE_STEPS * t + GATES)
                else:
                    pe.wait_ge(q["route_step"], gates_known)
                    pe.reg_add(gates_known, gates_known, ROUTE_STEPS)
                for b in range(QUAD):
                    mm = pe.transpose(ps_g[0:GE, N * b:N * b + N], gates[u][:, b, :], ident[0:N, 0:N])
                mm.then_inc(q["gates_turned"], 1)
                pe.wait_ge(q["gates_T_ok"], t + 1)
                for b in range(QUAD):
                    mm = pe.matmul(ps_b[0:N, D * b:D * b + D], gates_T[u][:, N * b:N * b + N], b2_sb[:, :],
                                   start=(b == 0), stop=(b == QUAD - 1), skip_group_check=True)
                mm.then_inc(q["result"], 1)
            logits(0, 0)
            with pe.Fori(0, QUADS // 2 - 1) as j:
                for u in range(2):
                    step(2 * j + u, u)
            step(QUADS - 2, 0)
            step(QUADS - 1, 1, following=False)
            pe.wait_ge(q["route_step"], ROUTE_STEPS * QUADS)
            pe.wait_ge(q["count_ok"], 1)
            pe.matmul(ps_l[0][0:GE, 0:1], added_f[:, :], ones_f[:, :], start=True, stop=True).then_inc(q["counted"], 1)
            pe.wait_ge(q["tiles_ok"], 1)
            pe.matmul(ps_r[0:GE, 0:1], upto[:, :], tiles[:, :], start=True, stop=True).then_inc(q["ends"], 1)
            pe.wait_ge(q["mine_ok"], 1)
            for n in range(5):
                pe.matmul(ps_f[n // 2][:, TILES * (n % 2):TILES * (n % 2) + TILES],
                          facts[:, n:n + 1].to_broadcast([GE, PART]), mine[:, :], start=(n % 2 == 0),
                          stop=(n % 2 == 1 or n == 4), skip_group_check=True).then_inc(q["spread"], 1)

        @block.vector
        def _(dve):
            nc.vector.memset(running[:, :], 0.0).then_inc(q["running_zero"], 1)
            variances(dve, nc, r, st, mean, gap, rstd, q, parts[:2])
            shifts(dve, nc, shift, mean, rstd, q, 0, *parts[0])
            variances(dve, nc, r, st, mean, gap, rstd, q, parts[2:], done=2)
            dve.wait_ge(q["pool_ok"], POOL_SETUP)
            dve.wait_ge(q["running_zero"], 1)

            def flat(ap):
                return ap.rearrange("p b g e -> p (b g) e")

            def over(ap):
                return ap.rearrange("p b g -> p (b g)").unsqueeze(2).to_broadcast([N, QUAD * 9, EXPERTS])

            def step(t, u, first=False, fresh=False):
                def after(n):
                    dve.wait_ge(q["route_step"], ROUTE_STEPS * t + n)

                def done(inst, n):
                    inst.then_inc(q["route_step"], 1)
                L = ps_l[u][0:N, 0:QUAD * GATES_OUT].rearrange("p (b g e) -> p b g e", b=QUAD, g=9)
                dve.wait_ge(q["logits"], t + 1)
                if not first:
                    after(0)
                done(nc.vector.tensor_reduce(top[:, 0, :, :].rearrange("p b g -> p (b g)"), flat(L), AX.X, ALU.max), TOP1)
                after(TOP1)
                done(nc.vector.tensor_tensor(flat(below), flat(L), over(top[:, 0]), ALU.subtract), BELOW1)
                after(BELOW1)
                order_b = order[:, :].unsqueeze(1).to_broadcast([N, QUAD * 9, EXPERTS])
                done(nc.vector.scalar_tensor_tensor(out=flat(ranked), in0=flat(below), scalar=0.0, in1=order_b,
                                                    op0=ALU.is_ge, op1=ALU.mult), RANK1)
                after(RANK1)
                done(nc.vector.tensor_reduce(winner_[0], flat(ranked), AX.X, ALU.max), FIRST1)
                after(FIRST1)
                done(nc.vector.tensor_tensor(flat(hot[:, 0]), flat(ranked), over(winner[:, 0]), ALU.is_equal), HOT1)
                after(HOT1)
                done(nc.vector.scalar_tensor_tensor(out=flat(left), in0=flat(hot[:, 0]), scalar=-BIG, in1=flat(L),
                                                    op0=ALU.mult, op1=ALU.add), LEFT)
                after(LEFT)
                done(nc.vector.tensor_reduce(top[:, 1, :, :].rearrange("p b g -> p (b g)"), flat(left), AX.X, ALU.max), TOP2)
                after(TOP2)
                done(nc.vector.tensor_tensor(flat(below), flat(left), over(top[:, 1]), ALU.subtract), BELOW2)
                after(BELOW2)
                done(nc.vector.scalar_tensor_tensor(out=flat(ranked), in0=flat(below), scalar=0.0, in1=order_b,
                                                    op0=ALU.is_ge, op1=ALU.mult), RANK2)
                after(RANK2)
                done(nc.vector.tensor_reduce(winner_[1], flat(ranked), AX.X, ALU.max), FIRST2)
                after(FIRST2)
                done(nc.vector.tensor_tensor(flat(hot[:, 1]), flat(ranked), over(winner[:, 1]), ALU.is_equal), HOT2)
                done(nc.vector.tensor_tensor(margin[:, :, :], top[:, 1], top[:, 0], ALU.subtract), MARGIN)
                dve.wait_ge(q["odds_exp"], t + 1)
                done(nc.vector.tensor_scalar(margin[:, :, :], odds[:, :, :], 1.0, None, ALU.add), ODDS)
                after(ODDS)
                done(nc.vector.reciprocal(part[:, 0], margin[:, :, :]), PART1)
                after(PART1)
                done(nc.vector.tensor_tensor(part[:, 1], odds[:, :, :], part[:, 0], ALU.mult), PART2)
                done(nc.vector.tensor_tensor(flat(either), flat(hot[:, 0]), flat(hot[:, 1]), ALU.add), EITHER)
                after(EITHER)
                if not first:
                    dve.wait_ge(q["ranks"], t)
                done(nc.vector.tensor_tensor(
                    chosen[:, :, :].rearrange("p b (g e) -> p b g e", g=GROUPS),
                    either[:, :, 0, :].unsqueeze(3).to_broadcast([N, QUAD, GROUPS, EXPERTS]),
                    either[:, :, 1:9, :], ALU.mult), CHOSEN)
                after(PART2)
                for a in range(2):
                    done(nc.vector.tensor_tensor(flat(split[:, a]), flat(hot[:, a]), over(part[:, a]), ALU.mult),
                         SPLIT0 + a)
                after(SPLIT1)
                done(nc.vector.tensor_tensor(flat(split[:, 0]), flat(split[:, 0]), flat(split[:, 1]), ALU.add), SPLIT)
                after(SPLIT)
                if not fresh:
                    dve.wait_ge(q["gates_turned"], t - 1)
                done(nc.vector.tensor_tensor(
                    gates[u][:, :, :].rearrange("p b (g e) -> p b g e", g=GROUPS),
                    split[:, 0, :, 0, :].unsqueeze(3).to_broadcast([N, QUAD, GROUPS, EXPERTS]),
                    split[:, 0, :, 1:9, :], ALU.mult), GATES)
                for a in range(2):
                    done(nc.vector.tensor_tensor(
                        share[:, a], hot[:, a, :, 0, :].unsqueeze(1).to_broadcast([N, 2, QUAD, GROUPS]),
                        part[:, :, :, 1:9], ALU.mult), SHARE0 + a)
                after(SHARE1)
                done(nc.vector.tensor_reduce(shares[:, :, :].rearrange("p k b -> p (k b)"),
                                             share[:, :, :, :, :].rearrange("p a c b g -> p (a c b) g"),
                                             AX.X, ALU.add), SHARES)
                dve.wait_ge(q["ranks"], t + 1)
                done(nc.vector.tensor_tensor(
                    slot_row[:, :, :], ps_r[0:N, 0:QUAD * GE].rearrange("p (b e) -> p b e", b=QUAD),
                    region[:, :].unsqueeze(1).to_broadcast([N, QUAD, GE]), ALU.add), SLOTS)
                after(SLOTS)
                for c in range(2):
                    done(nc.vector.tensor_tensor(
                        by_expert[:, c].rearrange("p b (g e) -> p b g e", g=GROUPS), hot[:, c, :, 1:9, :],
                        slot_row[:, :, :].rearrange("p b (g e) -> p b g e", g=GROUPS), ALU.mult), SORT0 + c)
                after(SORT1)
                done(nc.vector.tensor_reduce(by_group[:, :, :, :].rearrange("p c b g -> p (c b g)"),
                                             by_expert[:, :, :, :].rearrange("p c b (g e) -> p (c b g) e", g=GROUPS),
                                             AX.X, ALU.add), BY_GROUP)
                after(BY_GROUP)
                for a in range(2):
                    done(nc.vector.tensor_tensor(
                        picked[:, a], hot[:, a, :, 0, :].unsqueeze(1).to_broadcast([N, 2, QUAD, GROUPS]),
                        by_group[:, :, :, :], ALU.mult), PICKED0 + a)
                after(PICKED1)
                done(nc.vector.tensor_reduce(slot_f[:, :, :].rearrange("p k b -> p (k b)"),
                                             picked[:, :, :, :, :].rearrange("p a c b g -> p (a c b) g"),
                                             AX.X, ALU.add), SLOT_OF)
                if not fresh:
                    dve.wait_ge(scattered[u], QUAD_STORES // 2 * (t - u))
                done(nc.vector.tensor_scalar(rows[u][:, :, :, D], place[:, bass.ds(QUAD * t, QUAD), :], 0.0, None,
                                             ALU.add), PLACE)
                done(nc.vector.tensor_tensor(
                    rows[u][:, :, :, D + 1].rearrange("p b (a c) -> p a c b", a=2),
                    shares[:, :, :].rearrange("p (a c) b -> p a c b", a=2),
                    part[:, :, :, 0].unsqueeze(2).to_broadcast([N, 2, 2, QUAD]), ALU.mult), WEIGHT)
                after(WEIGHT)
                done(nc.vector.tensor_copy(slot[u][:, :, :], slot_f[:, :, :]), SLOT_INT)
                done(nc.vector.tensor_reduce(added_f[:, :], chosen[:, :, :].rearrange("p b e -> p e b"),
                                             AX.X, ALU.add), ADDED)
                after(ADDED)
                done(nc.vector.tensor_tensor(running[:, :], running[:, :], added_f[:, :], ALU.add), RUNNING)
                dve.wait_ge(q["result"], t + 1)
                here = r[:, bass.ds(QUAD * t, QUAD), :]
                done(nc.vector.tensor_tensor(here, here, ps_b[0:N, :].rearrange("p (b d) -> p b d", b=QUAD),
                                             ALU.add), RESULT)
            winner_ = [winner[:, k].rearrange("p b g -> p (b g)") for k in range(2)]
            step(0, 0, first=True, fresh=True)
            shifts(dve, nc, shift, mean, rstd, q, 2, parts[1][0], B)
            step(1, 1, fresh=True)
            with dve.Fori(1, QUADS // 2) as j:
                for u in range(2):
                    step(2 * j + u, u)
            dve.wait_ge(q["route_step"], ROUTE_STEPS * QUADS)
            nc.vector.tensor_copy(added_f[:, :], running[:, :]).then_inc(q["count_ok"], 1)
            n = 0

            def then(inst):
                nonlocal n
                n += 1
                inst.then_inc(q["table_step"], 1)

            def last():
                dve.wait_ge(q["table_step"], n)
            dve.wait_ge(q["counted"], 1)
            then(nc.vector.tensor_copy(count[:, :], ps_l[0][0:GE, 0:1]))
            last()
            then(nc.vector.tensor_scalar(count_i[:, :], count[:, :], float(TILE - 1), None, ALU.add))
            last()
            then(nc.vector.tensor_scalar(count_i[:, :], count_i[:, :], TILE.bit_length() - 1, None, ALU.arith_shift_right))
            last()
            nc.vector.tensor_copy(tiles[:, :], count_i[:, :]).then_inc(q["tiles_ok"], 1)
            dve.wait_ge(q["ends"], 1)
            then(nc.vector.tensor_copy(bounds[:, 1:2], ps_r[0:GE, 0:1]))
            last()
            then(nc.vector.tensor_tensor(bounds[:, 0:1], bounds[:, 1:2], tiles[:, :], ALU.subtract))
            last()
            then(nc.vector.tensor_scalar(began[:, :], tile_no[:, :], bounds[:, 0:1], None, ALU.is_ge))
            then(nc.vector.tensor_scalar(mine[:, :], tile_no[:, :], bounds[:, 1:2], None, ALU.is_ge))
            last()
            then(nc.vector.tensor_copy(facts[:, 2:3], bounds[:, 0:1]))
            then(nc.vector.tensor_scalar(facts[:, 3:4], count[:, :], float(-TILE), 0.0, ALU.add, ALU.max))
            then(nc.vector.tensor_scalar(facts[:, 1:2], lane[0:GE, :], float(REGION), None, ALU.mult))
            then(nc.vector.tensor_copy(facts[:, 4:5], lane[0:GE, :]))
            last()
            nc.vector.tensor_tensor(mine[:, :], began[:, :], mine[:, :], ALU.subtract).then_inc(q["mine_ok"], 1)
            dve.wait_ge(q["spread"], 5)
            used, base = ps_f[0][:, 0:TILES], ps_f[0][:, TILES:2 * TILES]
            start, room = ps_f[1][:, 0:TILES], ps_f[1][:, TILES:2 * TILES]
            then(nc.vector.scalar_tensor_tensor(out=at[:, :], in0=start, scalar=float(-TILE), in1=tile_of[:, :],
                                                op0=ALU.mult, op1=ALU.add))
            then(nc.vector.tensor_scalar(unused[:, :], used, -float(GE * REGION), float(GE * REGION), ALU.mult, ALU.add))
            last()
            then(nc.vector.tensor_tensor(rel[:, :], at[:, :], room, ALU.min))
            last()
            then(nc.vector.tensor_tensor(unused[:, :], unused[:, :], rel[:, :], ALU.add))
            then(nc.vector.tensor_tensor(at[:, :], at[:, :], rel[:, :], ALU.subtract))
            last()
            then(nc.vector.tensor_tensor(tab_base[:, :], unused[0:1, :], base[0:1, :], ALU.add))
            then(nc.vector.tensor_tensor(
                numbers[:, :, :], ps_f[2][0:1, 0:TILES].rearrange("o (w k) -> o w k", k=PACK),
                digit[:, :].unsqueeze(1).to_broadcast([1, TILES // PACK, PACK]), ALU.mult))
            last()
            then(nc.vector.tensor_reduce(words[:, :], numbers[:, :, :], AX.X, ALU.add))
            last()
            then(nc.vector.tensor_copy(tab_expert[:, :], words[:, :]))
            then(nc.vector.tensor_scalar(tab_skip[:, :], at[:, :], lane[:, 0:1], SKIP, ALU.is_gt, ALU.mult))
            last()


def experts(nc, w1_sb, w2_sb, b1, experts_in, expert_loads, slots_dram, results_dram, tab_base, tab_expert, tab_skip):
    with ExitStack() as ctx:
        def sb(name, shape, dt=F32):
            return ctx.enter_context(nc.sbuf_tensor(name, shape, dt))

        def sem(name):
            return ctx.enter_context(nc.semaphore(name))

        RING = 8
        BITS = (GE - 1).bit_length()
        YRING = 4
        x = [sb(f"x_e{k}", [TILE, SLOT]) for k in range(RING)]
        y = [sb(f"y_e{k}", [TILE, D]) for k in range(YRING)]
        place = [sb(f"place_e{k}", [TILE, 1], I32) for k in range(YRING)]
        xT = [sb(f"xT_e{k}", [D, TILE]) for k in range(2)]
        hid = [sb(f"hid_e{k}", [TILE, HID]) for k in range(2)]
        hidT = [sb(f"hidT_e{k}", [D, 2, TILE]) for k in range(2)]
        b1_sb = sb("b1_sb", [GE, HID])
        b1_T = sb("b1_T", [D, 2, GE])
        b1_now = [sb(f"b1_now{k}", [D, 2]) for k in range(2)]
        ident = sb("ident_e", [PART, PART])
        ps_x = [ctx.enter_context(nc.psum_tensor(f"ps_ex{k}", [PART, 512], F32)) for k in range(2)]
        ps_h = [ctx.enter_context(nc.psum_tensor(f"ps_eh{k}", [PART, 512], F32)) for k in range(2)]
        ps_t = [ctx.enter_context(nc.psum_tensor(f"ps_et{k}", [PART, 512], F32)) for k in range(2)]
        ps_y = [ctx.enter_context(nc.psum_tensor(f"ps_ey{k}", [PART, 512], F32)) for k in range(2)]

        names = """b1_in base_ok ident_ok b1_turned b1_ok x_turned xT_ok hid_done hid_ok hid_turned hidT_ok
            y_done y_ok place_ok bias_ok""".split()
        q = {n: sem("e_" + n) for n in names}
        x_in = [sem(f"e_x_in{k}") for k in range(RING)]
        stored = [sem(f"e_stored{k}") for k in range(YRING)]
        block = ctx.enter_context(nc.Block())

        @block.sync
        def _(sp):
            sp.dma_start(b1_sb[:, :], b1.rearrange("g e h -> (g e) h")).then_inc(q["b1_in"], 16)

            base = sp.alloc_register("base")

            def load(t, u, fresh):
                sp.reg_load(base, tab_base[0:1, bass.ds(t, 1)])
                if not fresh:
                    sp.wait_ge(q["y_ok"], t - RING + 1)
                rows = slots_dram[bass.ds(sp.snap(base, min_val=0, max_val=GE * REGION), TILE), :]
                sp.dma_start(x[u][:, :], rows).then_inc(x_in[u], 16)
            for u in range(RING):
                load(u, u, True)
            with sp.Fori(1, TILES // RING) as j:
                for u in range(RING):
                    load(RING * j + u, u, False)

        def pipeline(eng, body, lead, lag):
            for t in range(-lead, RING):
                body(t, t % RING)
            with eng.Fori(1, TILES // RING - 1) as j:
                for u in range(RING):
                    body(RING * j + u, u)
            for t in range(TILES - RING, TILES + lag):
                body(t, t % RING)

        def next_word(eng, word, t, u):
            if has(t + 1) and (u + 1) % PACK == 0:
                eng.reg_load(word[(u + 1) % RING // PACK], tab_expert[0:1, bass.ds((t + 1) // PACK, 1)])

        def number(eng, word, u, times):
            u = u % RING
            packed = eng.snap(word[u // PACK])
            shift = BITS * (u % PACK) - (times.bit_length() - 1)
            if shift > 0:
                value = (packed >> shift) & (times * (GE - 1))
            else:
                value = (packed & ((times * (GE - 1)) >> -shift)) * (1 << -shift)
            return value

        def has(t):
            return not isinstance(t, int) or 0 <= t < TILES

        def later(t, n):
            return not isinstance(t, int) or t >= n

        @block.gpsimd
        def _(pool):
            nc.gpsimd.memset(ident[:, :], 0.0).then_inc(q["base_ok"], 1)
            pool.wait_ge(q["base_ok"], 1)
            nc.gpsimd.affine_select(out=ident[:, :], in_=ident[:, :], compare_op=ALU.not_equal, fill=1.0,
                                    base=0, pattern=[[-1, PART]], channel_multiplier=1).then_inc(q["ident_ok"], 1)

            def store(t, u):
                pool.wait_ge(q["place_ok"], t + 1)
                pool.wait_ge(q["y_ok"], stores)
                pool.reg_add(stores, stores, 1)
                nc.gpsimd.indirect_dma_start(
                    out=results_dram, out_offset=bass.IndirectOffsetOnAxis(ap=place[u][:, 0:1], axis=0),
                    in_=y[u][:, :], in_offset=None, bounds_check=PICKS * TOKENS - 1,
                    oob_is_err=False).then_inc(stored[u], 16)
            stores = pool.alloc_register("stores")
            pool.reg_mov(stores, 1)
            with pool.Fori(0, TILES // YRING) as j:
                for u in range(YRING):
                    store(YRING * j + u, u)
            for u in range(YRING):
                pool.wait_ge(stored[u], 16 * TILES // YRING)

        @block.tensor
        def _(pe):
            pe.wait_ge(q["ident_ok"], 1)
            pe.wait_ge(q["b1_in"], 16)
            for half in range(2):
                pe.transpose(ps_t[0][:, GE * half:GE * half + GE], b1_sb[:, D * half:D * half + D],
                             ident[0:GE, 0:GE]).then_inc(q["b1_turned"], 1)
            for k in range(len(experts_in)):
                pe.wait_ge(experts_in[k], 16 * expert_loads)
            pe.wait_ge(q["b1_ok"], 1)
            word = [pe.alloc_register(f"word{k}") for k in range(2)]

            def body(t, u):
                v = u % 2
                next_word(pe, word, t, u)
                if has(t + 2):
                    a = t + 2
                    pe.wait_ge(x_in[(u + 2) % RING],
                               16 * (a // RING + 1) if isinstance(a, int) else 16 // RING * (t - u) + (16 if u < RING - 2 else 32))
                    pe.transpose(ps_x[v][:, 0:TILE], x[(u + 2) % RING][:, 0:D], ident[:, :]).then_inc(q["x_turned"], 1)
                if has(t + 1):
                    a, w = t + 1, 1 - v
                    first = number(pe, word, u + 1, HID)
                    pe.wait_ge(q["xT_ok"], a + 1)
                    pe.matmul(ps_h[w][:, 0:HID], xT[w][:, :], w1_sb[:, bass.ds(first, HID)], start=True,
                              stop=True).then_inc(q["hid_done"], 1)
                if has(t):
                    pe.wait_ge(q["hid_ok"], t + 1)
                    for half in range(2):
                        pe.transpose(ps_t[v][:, TILE * half:TILE * half + TILE], hid[v][:, D * half:D * half + D],
                                     ident[:, :]).then_inc(q["hid_turned"], 1)
                if has(t - 1):
                    a, w = t - 1, 1 - v
                    w2 = w2_sb[:, bass.ds(number(pe, word, u - 1, HID), HID)]
                    pe.wait_ge(q["hidT_ok"], a + 1)
                    if later(a, 2):
                        pe.wait_ge(q["y_ok"], a - 1)
                    for half in range(2):
                        mm = pe.matmul(ps_y[w][:, 0:D], hidT[w][:, half, :], w2[:, D * half:D * half + D],
                                       start=(half == 0), stop=(half == 1))
                    mm.then_inc(q["y_done"], 1)
            pipeline(pe, body, 2, 1)

        @block.scalar
        def _(act):
            act.wait_ge(q["b1_turned"], 2)
            nc.scalar.copy(b1_T[:, :, :], ps_t[0][:, 0:2 * GE].rearrange("p (k e) -> p k e", k=2)).then_inc(q["b1_ok"], 1)

            def body(t, u):
                v = u % 2
                if has(t + 2):
                    a = t + 2
                    act.wait_ge(q["x_turned"], a + 1)
                    if later(a, 2):
                        act.wait_ge(q["hid_done"], a - 1)
                    nc.scalar.copy(xT[v][:, :], ps_x[v][:, 0:TILE]).then_inc(q["xT_ok"], 1)
                if has(t):
                    act.wait_ge(q["bias_ok"], t + 1)
                    if later(t, 2):
                        act.wait_ge(q["y_done"], t - 1)
                    act.wait_ge(q["hid_turned"], 2 * t + 2)
                    for half in range(2):
                        done = nc.scalar.activation(hidT[v][:, half, :], ps_t[v][:, TILE * half:TILE * half + TILE],
                                                    ACT.Relu, bias=b1_now[v][:, half:half + 1])
                    done.then_inc(q["hidT_ok"], 1)
            pipeline(act, body, 2, 0)

        @block.vector
        def _(dve):
            def body(t, u):
                v = u % 2
                if has(t + 1):
                    a, w = t + 1, 1 - v
                    next_word(dve, word, t, u)
                    expert = number(dve, word, u + 1, 1)
                    dve.wait_ge(q["hid_done"], a + 1)
                    if later(a, 2):
                        dve.wait_ge(q["hid_turned"], 2 * a - 2)
                    nc.vector.tensor_copy(hid[w][:, :], ps_h[w][:, 0:HID]).then_inc(q["hid_ok"], 1)
                    if later(a, 2):
                        dve.wait_ge(q["hidT_ok"], a - 1)
                    nc.vector.tensor_scalar(b1_now[w][:, :].unsqueeze(2), b1_T[:, :, bass.ds(expert, 1)], 0.0, None,
                                            ALU.add).then_inc(q["bias_ok"], 1)
                if has(t):
                    if later(t, YRING):
                        dve.wait_ge(stored[u % YRING], 16 * (t // YRING) if isinstance(t, int) else
                                    16 // YRING * (t - u % YRING))
                    nc.vector.tensor_tensor(place[u % YRING][:, :], x[u][:, D:D + 1], tab_skip[:, bass.ds(t, 1)],
                                            ALU.add).then_inc(q["place_ok"], 1)
                if has(t - 1):
                    a, w, z = t - 1, 1 - v, (u - 1) % YRING
                    dve.wait_ge(q["y_done"], a + 1)
                    if later(a, YRING):
                        dve.wait_ge(stored[z], 16 * (a // YRING) if isinstance(a, int) else
                                    16 // YRING * (a - z))
                    nc.vector.tensor_scalar(y[z][:, :], ps_y[w][:, 0:D], x[(u - 1) % RING][:, D + 1:SLOT], None,
                                            ALU.mult).then_inc(q["y_ok"], 1)

            dve.wait_ge(q["b1_ok"], 1)
            word = [dve.alloc_register(f"word{k}") for k in range(2)]
            pipeline(dve, body, 1, 1)


def combine(nc, r, results_dram, out):
    with ExitStack() as ctx:
        def sem(name):
            return ctx.enter_context(nc.semaphore(name))
        RING = 4
        parts = [ctx.enter_context(nc.sbuf_tensor(f"parts{k}", [N, PICKS, QUAD, D], F32)) for k in range(RING)]
        parts_in = [sem(f"f_parts_in{k}") for k in range(RING)]
        summed = sem("f_summed")
        summed_pool = sem("f_summed_pool")
        SHARE = QUAD - 1
        out_ok = sem("f_out_ok")
        block = ctx.enter_context(nc.Block())
        pick = results_dram.rearrange("(k b n) d -> k n b d", k=PICKS, b=B)

        def load(eng, t, u, fresh, picks):
            if not fresh:
                eng.wait_ge(summed, PICKS * (t - RING) + PICKS)
                eng.wait_ge(summed_pool, PICKS * (t - RING) + PICKS)
            for k in picks:
                eng.dma_start(parts[u][:, k, :, :], pick[k, :, bass.ds(QUAD * t, QUAD), :]).then_inc(parts_in[u], 16)

        def loads(eng, picks):
            for u in range(RING):
                load(eng, u, u, True, picks)
            with eng.Fori(1, QUADS // RING) as j:
                for u in range(RING):
                    load(eng, RING * j + u, u, False, picks)

        @block.sync
        def _(sp):
            loads(sp, range(0, PICKS // 2))
            with sp.Fori(0, QUADS) as t:
                sp.wait_ge(summed, PICKS * t + PICKS)
                sp.wait_ge(summed_pool, PICKS * t + PICKS)
                sp.dma_start(out[bass.ds(QUAD * t, QUAD)].rearrange("b n d -> n b d"),
                             r[:, bass.ds(QUAD * t, QUAD), :]).then_inc(out_ok, 16)
            sp.wait_ge(out_ok, 16 * QUADS)

        @block.scalar
        def _(act):
            loads(act, range(PICKS // 2, PICKS))

        def add(eng, engine, t, u, lo, hi, done):
            eng.wait_ge(parts_in[u], 16 * PICKS // RING * (t - u) + 16 * PICKS)
            at = r[:, bass.ds(QUAD * t + lo, hi - lo), :]
            for k in range(PICKS):
                if k > 0:
                    eng.wait_ge(done, PICKS * t + k)
                engine.tensor_tensor(at, at, parts[u][:, k, lo:hi, :], ALU.add).then_inc(done, 1)

        @block.vector
        def _(dve):
            with dve.Fori(0, QUADS // RING) as j:
                for u in range(RING):
                    add(dve, nc.vector, RING * j + u, u, 0, SHARE, summed)

        @block.gpsimd
        def _(pool):
            for t in range(QUADS):
                add(pool, nc.gpsimd, t, t % RING, SHARE, QUAD, summed_pool)


def early_fusion(nc, args, out):
    (x, txt, conv_w, conv_b, gamma, beta, dense_w, dense_b, w_qkv, b_qkv, w_out, b_out, p_coeff, q_coeff, cema_gamma,
     adaptive, g1, g2, w1, b1, w2, b2) = args
    h_dram = nc.dram_tensor("image_tokens", [B, PATCHES, D], F32, kind="Internal").ap()
    response = nc.dram_tensor("impulse_response", [D, KPAD], F32, kind="Internal").ap()
    slots_dram = nc.dram_tensor("expert_slots", [(GE + 1) * REGION, SLOT], F32, kind="Internal").ap()
    results_dram = nc.dram_tensor("expert_results", [PICKS * TOKENS, D], F32, kind="Internal").ap()
    with ExitStack() as ctx:
        mix = ctx.enter_context(nc.sbuf_tensor("mix", [PART, 2], F32))
        wide = ctx.enter_context(nc.sbuf_tensor("wide", [D, 3 * D], F32))
        wout_sb = ctx.enter_context(nc.sbuf_tensor("wout_sb", [D, D], F32))
        b_cols = ctx.enter_context(nc.sbuf_tensor("b_cols", [D, 3], F32))
        bout_row = ctx.enter_context(nc.sbuf_tensor("bout_row", [N, D], F32))
        attention_loads = [(wide[:, :], w_qkv), (wout_sb[:, :], w_out), (bout_row[:, :], b_out.partition_broadcast(N))]
        attention_loads += [(b_cols[:, a:a + 1], b_qkv[a * D:a * D + D].rearrange("(n o) -> n o", o=1)) for a in range(3)]
        patch_tokens(nc, x, conv_w, conv_b, gamma, beta, dense_w, dense_b, h_dram, (p_coeff, q_coeff, cema_gamma),
                     adaptive, mix, response, attention_loads)

        def sb(name, shape, dt=F32):
            return ctx.enter_context(nc.sbuf_tensor(name, shape, dt))
        r = sb("r", [N, B, D])
        w1_sb = sb("w1_sb", [D, GE * HID])
        w2_sb = sb("w2_sb", [D, GE * HID])
        experts_in = [ctx.enter_context(nc.semaphore(f"experts_in{k}")) for k in range(2)]

        def fetch_experts(sp, g):
            cols = slice(g * EXPERTS * HID, (g + 1) * EXPERTS * HID)
            sp.dma_start(w1_sb[:, cols].rearrange("d (e h) -> d e h", e=EXPERTS),
                         w1[g].rearrange("e d h -> d e h")).then_inc(experts_in[0], 16)
            sp.dma_start(w2_sb[:, cols].rearrange("p (k d) -> p k d", d=D),
                         w2[g].rearrange("e (k p) d -> p (e k) d", p=D)).then_inc(experts_in[1], 16)
        attention(nc, h_dram, txt, wide, wout_sb, b_cols, bout_row, mix, response, r, fetch_experts)
        tab_base = sb("tab_base", [1, TILES], I32)
        tab_expert = sb("tab_expert", [1, TILES // PACK], I32)
        tab_skip = sb("tab_skip", [PART, TILES])
        route(nc, r, g1, g2, b2, slots_dram, tab_base, tab_expert, tab_skip)
        experts(nc, w1_sb, w2_sb, b1, experts_in, GROUPS, slots_dram, results_dram, tab_base, tab_expert, tab_skip)
        combine(nc, r, results_dram, out)


_INS = ['x', 'txt', 'L0_tok_conv_w', 'L0_tok_conv_b', 'L0_tok_gamma', 'L0_tok_beta', 'L0_tok_dense_w',
        'L0_tok_dense_b', 'L0_attn_W_qkv', 'L0_attn_b_qkv', 'L0_attn_W_out', 'L0_attn_b_out', 'L0_attn_p_coeff',
        'L0_attn_q_coeff', 'L0_attn_gamma', 'L0_attn_adaptive_weights', 'L0_ffn_g1', 'L0_ffn_g2', 'L0_ffn_W1',
        'L0_ffn_b1', 'L0_ffn_W2', 'L0_ffn_b2']


def kernel(**inputs):
    import numpy as _np
    import concourse.bacc as _bacc
    from concourse import mybir as _mybir
    from concourse.bass_utils import run_bass_kernel_spmd as _run

    nc = _bacc.Bacc("TRN2", target_bir_lowering=False, num_devices=1)
    arrays, args = {}, []
    for name in _INS:
        a = _np.ascontiguousarray(inputs[name])
        arrays[f"in_{name}_dram"] = a
        args.append(nc.dram_tensor(f"in_{name}_dram", a.shape, _mybir.dt.from_np(a.dtype), kind="ExternalInput").ap())
    out = nc.dram_tensor("out_dram", (B, N, D), _mybir.dt.float32, kind="ExternalOutput").ap()
    early_fusion(nc, args, out)
    r = _run(nc, [arrays], core_ids=[0])
    return r.results[0]["out_dram"]
```
